# Optimizing a Trainium2 kernel written in Bass

```python
import numpy as np
import jax
import jax.numpy as jnp

def _softmax(x, axis=-1):
    return jax.nn.softmax(x, axis=axis)

def _gelu(x):
    return jax.nn.gelu(x, approximate=True)

def _silu(x):
    return jax.nn.silu(x)

def _sigmoid(x):
    return jax.nn.sigmoid(x)

def _layernorm(x, axis=-1, eps=1e-05):
    m = jnp.mean(x, axis=axis, keepdims=True)
    v = jnp.var(x, axis=axis, keepdims=True)
    return (x - m) / jnp.sqrt(v + eps)

def _scatter_add(tgt, idx, src, axis=0):
    return tgt.at[idx].add(src)

def _segment_sum(src, seg, n):
    return jax.ops.segment_sum(src, seg, n)
kernel_name = 'mk_adaln_d1_jaxref_r8_d22552'

def setup_inputs(seed: int=0):
    np.random.seed(seed)
    _w = jnp.asarray

    def _L0_attn_setup():
        import jax, jax.numpy as jnp
        import numpy as np
        H = 16
        KVH = 4
        D = 128
        HID = 256
        EPS = 1e-06
        GROUPS = H // KVH

        def elu_plus_one(x):
            return jax.nn.elu(x) + 1.0

        def _repeat_kv(x, b, s):
            x = x.reshape(b, s, KVH, 1, D)
            x = jnp.broadcast_to(x, (b, s, KVH, GROUPS, D))
            return x.reshape(b, s, H * D)

        def _split_heads(x, b, s, nh):
            return x.reshape(b, s, nh, D).transpose(0, 2, 1, 3)
        key = jax.random.key(seed)
        ks = jax.random.split(key, 8)
        s = 0.02
        return {'hidden_states': jax.random.normal(ks[0], (2, 512, HID), jnp.float32), 'Wq': jax.random.normal(ks[1], (H * D, HID), jnp.float32) * s, 'bq': jnp.zeros((H * D,), jnp.float32), 'Wk': jax.random.normal(ks[2], (KVH * D, HID), jnp.float32) * s, 'bk': jnp.zeros((KVH * D,), jnp.float32), 'Wv': jax.random.normal(ks[3], (KVH * D, HID), jnp.float32) * s, 'bv': jnp.zeros((KVH * D,), jnp.float32), 'Wo': jax.random.normal(ks[4], (HID, H * D), jnp.float32) * s}
    _L0_attn_in = _L0_attn_setup()

    def _L0_ffn_setup():
        import jax, jax.numpy as jnp
        import numpy as np
        TOP_K = 4
        NUM_EXPERTS = 16
        key = jax.random.key(seed)
        ks = jax.random.split(key, 6)
        B, S, H, I, E = (2, 128, 256, 224, NUM_EXPERTS)
        return {'x': jax.random.normal(ks[0], (B, S, H), dtype=jnp.float32), 'router_w': jax.random.normal(ks[1], (E, H), dtype=jnp.float32) * 0.02, 'expert_bias': jnp.zeros((E,), dtype=jnp.float32), 'gate_proj': jax.random.normal(ks[2], (E, H, I), dtype=jnp.float32) * 0.02, 'up_proj': jax.random.normal(ks[3], (E, H, I), dtype=jnp.float32) * 0.02, 'down_proj': jax.random.normal(ks[4], (E, I, H), dtype=jnp.float32) * 0.02}
    _L0_ffn_in = _L0_ffn_setup()
    _L0_c = _w((lambda *s: np.random.randn(*s).astype(np.float32) * 0.05)(8, 256))
    _L0_wmod = _w((lambda *s: np.random.randn(*s).astype(np.float32) * 0.05)(256, 6 * 256) * 256 ** (-0.5))
    _d = {'L0_attn_hidden_states': _L0_attn_in['hidden_states'], 'L0_attn_Wq': _L0_attn_in['Wq'], 'L0_attn_bq': _L0_attn_in['bq'], 'L0_attn_Wk': _L0_attn_in['Wk'], 'L0_attn_bk': _L0_attn_in['bk'], 'L0_attn_Wv': _L0_attn_in['Wv'], 'L0_attn_bv': _L0_attn_in['bv'], 'L0_attn_Wo': _L0_attn_in['Wo'], 'L0_ffn_router_w': _L0_ffn_in['router_w'], 'L0_ffn_expert_bias': _L0_ffn_in['expert_bias'], 'L0_ffn_gate_proj': _L0_ffn_in['gate_proj'], 'L0_ffn_up_proj': _L0_ffn_in['up_proj'], 'L0_ffn_down_proj': _L0_ffn_in['down_proj'], 'L0_c': _L0_c, 'L0_wmod': _L0_wmod}
    _x0 = _d['L0_attn_hidden_states']
    _d['L0_attn_hidden_states'] = jax.random.normal(jax.random.fold_in(jax.random.key(seed), 1), (8, 256, 256), dtype=_x0.dtype)
    del _x0
    return _d

def reference(L0_attn_hidden_states, L0_attn_Wq, L0_attn_bq, L0_attn_Wk, L0_attn_bk, L0_attn_Wv, L0_attn_bv, L0_attn_Wo, L0_ffn_router_w, L0_ffn_expert_bias, L0_ffn_gate_proj, L0_ffn_up_proj, L0_ffn_down_proj, L0_c, L0_wmod):

    def _L0_attn_ref(hidden_states, Wq, bq, Wk, bk, Wv, bv, Wo):
        import jax, jax.numpy as jnp
        import numpy as np
        H = 16
        KVH = 4
        D = 128
        HID = 256
        EPS = 1e-06
        GROUPS = H // KVH

        def elu_plus_one(x):
            return jax.nn.elu(x) + 1.0

        def _repeat_kv(x, b, s):
            x = x.reshape(b, s, KVH, 1, D)
            x = jnp.broadcast_to(x, (b, s, KVH, GROUPS, D))
            return x.reshape(b, s, H * D)

        def _split_heads(x, b, s, nh):
            return x.reshape(b, s, nh, D).transpose(0, 2, 1, 3)
        b, s, _ = hidden_states.shape
        q = hidden_states @ Wq.T + bq
        k = hidden_states @ Wk.T + bk
        v = hidden_states @ Wv.T + bv
        k = _repeat_kv(k, b, s)
        v = _repeat_kv(v, b, s)
        q = _split_heads(q, b, s, H)
        k = _split_heads(k, b, s, H)
        v = _split_heads(v, b, s, H)
        sq = elu_plus_one(q)
        sk = elu_plus_one(k)
        kv = jnp.einsum('bhsd,bhse->bhde', sk, v)
        qkv = jnp.einsum('bhsd,bhde->bhse', sq, kv)
        k_sum = sk.sum(axis=2)
        norm = jnp.einsum('bhsd,bhd->bhs', sq, k_sum)
        attn = qkv / (norm[..., None] + EPS)
        attn = attn.transpose(0, 2, 1, 3).reshape(b, s, H * D)
        return attn @ Wo.T

    def _L0_ffn_ref(x, router_w, expert_bias, gate_proj, up_proj, down_proj):
        import jax, jax.numpy as jnp
        import numpy as np
        TOP_K = 4
        NUM_EXPERTS = 16
        logits = jnp.einsum('bsh,eh->bse', x, router_w) + expert_bias
        scores = jax.nn.softmax(logits, axis=-1)
        top_w, top_idx = jax.lax.top_k(scores, TOP_K)
        top_w = top_w / jnp.sum(top_w, axis=-1, keepdims=True)
        g = jnp.einsum('bsh,khe->bske', x, gate_proj)
        u = jnp.einsum('bsh,khe->bske', x, up_proj)
        act = jax.nn.silu(g) * u
        out = jnp.einsum('bske,keh->bskh', act, down_proj)
        sel = jnp.take_along_axis(out, top_idx[..., None], axis=2)
        return jnp.sum(sel * top_w[..., None], axis=2)
    x = L0_attn_hidden_states
    mod = (_silu(L0_c) @ L0_wmod).reshape(L0_c.shape[0], 6, 1, -1)
    sa, ca, ga, sb, cb, gb = (mod[:, 0], mod[:, 1], mod[:, 2], mod[:, 3], mod[:, 4], mod[:, 5])
    ga = (2 * (ga >= 0) - 1) * jnp.maximum(jnp.abs(ga), 0.25)
    gb = (2 * (gb >= 0) - 1) * jnp.maximum(jnp.abs(gb), 0.25)
    h = _layernorm(x, axis=-1) * (1 + ca) + sa
    x = x + ga * _L0_attn_ref(h, L0_attn_Wq, L0_attn_bq, L0_attn_Wk, L0_attn_bk, L0_attn_Wv, L0_attn_bv, L0_attn_Wo)
    h = _layernorm(x, axis=-1) * (1 + cb) + sb
    x = x + gb * _L0_ffn_ref(h, L0_ffn_router_w, L0_ffn_expert_bias, L0_ffn_gate_proj, L0_ffn_up_proj, L0_ffn_down_proj)
    return x

_drawn_inputs = setup_inputs


def setup_inputs(seed=0):
    import zlib

    import numpy as np

    out = dict(_drawn_inputs(seed))
    spreads = {'L0_attn_bq': (0.0, 2.0),
     'L0_attn_bk': (0.0, 2.0),
     'L0_attn_bv': (0.0, 0.392),
     'L0_ffn_expert_bias': (0.0, 0.8)}
    factors = {'L0_attn_Wq': 86.956,
     'L0_attn_Wk': 22.541,
     'L0_attn_Wv': 8.0,
     'L0_ffn_router_w': 8.0,
     'L0_ffn_gate_proj': 8.0,
     'L0_ffn_up_proj': 8.0,
     'L0_ffn_down_proj': 8.0,
     'L0_c': 2.676,
     'L0_wmod': 2.673}
    for name, (base, spread) in spreads.items():
        noise = np.random.default_rng([zlib.crc32(name.encode()), seed]).standard_normal(out[name].shape)
        drawn = base * np.exp(spread * noise) if base else spread * noise
        out[name] = jnp.asarray(drawn.astype(out[name].dtype))
    for name, factor in factors.items():
        out[name] = (out[name] * factor).astype(out[name].dtype)
    return out
```

```python
from contextlib import ExitStack

import concourse.bass as bass
from concourse import mybir

P = 128
F32 = mybir.dt.float32
F32R = mybir.dt.float32r
BF16 = mybir.dt.bfloat16
I32 = mybir.dt.int32
U32 = mybir.dt.uint32
ALU = mybir.AluOpType
ACT = mybir.ActivationFunctionType
AX_X = mybir.AxisListType.X

B, S, HID = 8, 256, 256
H, KVH, D = 16, 4, 128
GROUPS = H // KVH
KT = HID // P
TOK = B * S
CH = TOK // P
PAIRS = B // 2
PC = CH // PAIRS
PT = PC * P
E, TOPK, FF = 16, 4, 224
FH = FF // 2
LN_EPS, NORM_EPS = 1e-5, 1e-6
TILES = (TOK * TOPK + E * (P - 1)) // P
TILES += -TILES % 4
SLOTS = TILES * P
W2 = HID + 2
XR = 4
RING = 4
ROUTING_AT = 153 * 1024
STAGE = 512


def constants():
    import numpy as np
    eye = np.eye(P)
    iota = np.tile(np.arange(E), (P, 1))
    low = np.tile((np.arange(E)[None, :] < np.arange(E)[:, None]).reshape(1, E * E), (P, 1))
    before = np.arange(P)[:, None] < np.arange(P)[None, :]
    tiles = np.tile(np.arange(TILES), (P, 1))
    return np.concatenate([eye, iota, low, before, np.ones((P, P)), tiles], axis=1).astype(np.float32)


C_EYE, C_IOTA, C_LOW, C_TRI, C_TILE, C_END = 0, P, P + E, P + E + E * E, 3 * P + E + E * E, 3 * P + E + E * E + TILES


def adaln_block(nc, x_in, wqT, wkvT, woT, bqT, bkv, routerT, ebias, w_gu, w_down, cT, wmod, consts, out):
    mod_rows = nc.dram_tensor("mod_rows", (B, 4 * HID), F32).ap()
    x1_dram = nc.dram_tensor("x1_dram", (TOK, HID), F32).ap()
    xs_dram = nc.dram_tensor("xs_dram", (SLOTS, HID), F32).ap()
    ys_dram = nc.dram_tensor("ys_dram", (SLOTS, HID), F32).ap()

    with ExitStack() as ctx:
        keep = lambda name, shape, dt=F32: ctx.enter_context(nc.sbuf_tensor(name, shape, dt))
        ps_q = ctx.enter_context(nc.psum_tensor("ps_q", [P, 2, 512], F32))
        ps_d = ctx.enter_context(nc.psum_tensor("ps_d", [P, PC, 512], F32))
        ps_m = ctx.enter_context(nc.psum_tensor("ps_m", [P, 2, 512], F32))

        ident = keep("ident", [P, P])
        wgt = keep("wgt", [P, CH, TOPK])
        slot_i = keep("slot_i", [P, CH, TOPK], I32)
        tile_e = keep("tile_e", [1, TILES], I32)
        ebias_sb = keep("ebias_sb", [P, E])
        router_sb = keep("router_sb", [P, KT, E])
        carry_v, carry_g = keep("carry_v", [P, 8]), keep("carry_g", [P, 8])
        zero = keep("zero", [P, HID])
        half = keep("half", [P, PC])
        stats = keep("stats", [P, PC, 6])
        mv = keep("mv", [P, PC, 2])
        ve = keep("ve", [P, PC])
        rstd = keep("rstd", [P, PC])
        rr = keep("rr", [P, 2, 2])
        rn = keep("rn", [P, 2, 2])

        with ExitStack() as attn:
            sb = lambda name, shape, dt=F32: attn.enter_context(nc.sbuf_tensor(name, shape, dt))
            wq_hi, wq_lo = (sb(n, [P, KT, H * D], F32R) for n in ("wq_hi", "wq_lo"))
            wkv_hi, wkv_lo = (sb(n, [P, KT, 2, KVH * D], F32R) for n in ("wkv_hi", "wkv_lo"))
            wo_hi, wo_lo = (sb(n, [P, H, HID], F32R) for n in ("wo_hi", "wo_lo"))
            hT_hi, hT_lo = (sb(n, [P, KT, PT], F32R) for n in ("hT_hi", "hT_lo"))
            sk_hi, sk_lo = (sb(n, [P, PC, KVH * D], F32R) for n in ("sk_hi", "sk_lo"))
            v_hi, v_lo = (sb(n, [P, PC, KVH * D], F32R) for n in ("v_hi", "v_lo"))
            kvT_hi, kvT_lo = (sb(n, [P, 2, KVH * D], F32R) for n in ("kvT_hi", "kvT_lo"))
            kvwo_hi, kvwo_lo = (sb(n, [P, 2, 2, 2, W2], F32R) for n in ("kvwo_hi", "kvwo_lo"))
            ks_hi, ks_lo = (sb(n, [P, 2, KVH, 2], F32R) for n in ("ks_hi", "ks_lo"))
            sq_hi, sq_lo = (sb(n, [P, 2, PT], F32R) for n in ("sq_hi", "sq_lo"))
            ones2 = sb("ones2", [P, 2], F32R)
            kt = sb("kt", [P, 2, 512])
            vf = sb("vf", [P, 2, 512])
            ke = sb("ke", [P, 512])
            acc = sb("acc", [P, PC, HID])
            bkv_sb = sb("bkv_sb", [P, 2, 512])
            wst = sb("wst", [P, 2, STAGE])
            rows = sb("rows", [P, 3, HID])
            ones_f = sb("ones_f", [P, 2])
            bq_sb, nbq_sb = (sb(n, [P, H]) for n in ("bq_sb", "nbq_sb"))
            cs = sb("cs", [P, KT, 4, B])
            sa_col, ca_col = (sb(n, [P, KT, B]) for n in ("sa_col", "ca_col"))
            qr = sb("qr", [P, 2, PT])
            qe = sb("qe", [P, 2, PT])
            x_sb = sb("x_sb", [P, CH, HID])
        xn = kt[:].rearrange("p a (c n) -> p (a c) n", n=HID)
        wmod_sb = [t[:].rearrange("p a n -> p (a n)")[:, 0:3 * HID] for t in (kt, vf, qe, qr)]
        wmod_of = lambda k, m: wmod_sb[2 * k + m // 3][:, (m % 3) * HID:(m % 3 + 1) * HID]
        gate_rows = qr[0:B].rearrange("p a n -> p (a n)")
        wkv_raw = [acc[:, 0:2, :].rearrange("p c n -> p (c n)"), acc[:, 2:4, :].rearrange("p c n -> p (c n)"),
                   wst[:, 0, :], wst[:, 1, :]]


        with ExitStack() as ffn:
            sb = lambda name, shape, dt=F32: ffn.enter_context(nc.sbuf_tensor(name, shape, dt))
            gu_hi, gu_lo = (sb(n, [P, KT, E, 2 * FF], F32R) for n in ("gu_hi", "gu_lo"))
            dn_hi, dn_lo = (sb(n, [FH, 2, E, HID], F32R) for n in ("dn_hi", "dn_lo"))
            gu_raw = sb("gu_raw", [P, KT, 2 * FF])
            dn_raw = sb("dn_raw", [FH, 2, HID])
            xt = sb("xt", [P, XR, HID])
            xT_hi, xT_lo = (sb(n, [P, 2, KT, P], F32R) for n in ("xT_hi", "xT_lo"))
            silu = sb("silu", [P, 2, FF])
            mid = sb("mid", [P, 2, FF])
            mT_hi, mT_lo = (sb(n, [FH, 2, 2, P], F32R) for n in ("mT_hi", "mT_lo"))
            y_sb = sb("y_sb", [P, 2, HID])
        with ExitStack() as route:
            sb = lambda name, shape, dt=F32: route.enter_context(nc.sbuf_tensor(name, shape, dt))
            sb("below_routing", [P, ROUTING_AT // 4])
            cst = sb("cst", [P, C_END])
            hot = sb("hot", [P, CH, TOPK, E])
            pos = sb("pos", [P, CH, E])
            cum = sb("cum", [P, CH + 1, E])
            lg = sb("lg", [P, CH, E])
            mask = sb("mask", [P, CH, E], BF16)
            h2T = sb("h2T", [P, 2, KT, P])
            tri = sb("tri", [P, 2 * P], BF16)
            top8 = sb("top8", [P, CH, 8])
            arg8 = sb("arg8", [P, CH, 8], U32)
            arg_f, gap, weight = (sb(n, [P, CH, TOPK]) for n in ("arg_f", "gap", "weight"))
            wsum, wrec = (sb(n, [P, CH]) for n in ("wsum", "wrec"))
            cmp = sb("cmp", [P, E, E])
            steps = sb("steps", [P, E])
            ntile, start, start_slot = (sb(n, [P, E]) for n in ("ntile", "start", "start_slot"))
            tcmp = sb("tcmp", [1, TILES, E])
            tsum = sb("tsum", [1, TILES])
        with ExitStack() as combine:
            sb = lambda name, shape, dt=F32: combine.enter_context(nc.sbuf_tensor(name, shape, dt))
            yg = sb("yg", [P, RING, TOPK, HID])
            x1_sb = sb("x1_sb", [P, RING, HID])
            gb_sb = sb("gb_sb", [P, B, HID])
            o_sb = sb("o_sb", [P, RING, HID])

        s = {n: ctx.enter_context(nc.semaphore(n)) for n in (
            "x_in0", "x_in", "ident_in", "bias_in", "router_in", "mod_in", "wkv_in", "wst_in0", "wst_in1", "rows_in", "zero_made", "zeroed", "x1_out",
            "silu_exp", "silu_step", "gates", "gate_step", "modrow_out", "ones_made", "half_made",
            "wkv_hi", "wkv_lo", "wst_hi", "wst_lo", "misc_ready", "misc_done", "misc_hi",
            "ln1_step", "ln1_rstd", "ln2_step", "ln2_rstd", "xn_ready", "hT_hi", "hT_lo",
            "k_neg", "k_act", "q_neg", "q_exp", "nbq", "sk_f", "sk_hi", "sk_lo", "v_hi", "v_lo",
            "q_ready", "q_act", "sq_f", "sq_hi", "sq_lo", "d_ready", "rn_step", "acc_done",
            "x1_step", "x1_made", "h2_n", "h2_step",
            "cst_in", "h2_turned", "h2T_made", "logits", "route_step", "exp_done", "mask_made", "counted",
            "slots_made", "tiles_made", "scattered",
            "gu_in", "dn_in", "gw_hi", "gw_lo", *(f"xt_in{r}" for r in range(XR)), "x_turned", "xT_hi", "xT_lo", "gu_done", "silu_done", "mid_done",
            "m_turned", "mT_hi", "mT_lo", "down_done", "y_made", "y_out0", "y_out1",
            "lg_made", "gap_made", *(f"{n}{r}" for n in ("gathered", "x1_back", "o_out") for r in range(RING)), "gb_in", "sum_step", "o_made")}

        JOBS = 30
        job_T = lambda j, k: j * JOBS + (4 + k)
        job_KV = lambda j, c, v: j * JOBS + (6 + 2 * c + v)
        job_kvT = lambda j, b: j * JOBS + (14 + b)
        job_ks = lambda j, b: j * JOBS + (16 + b)
        job_fold = lambda j, hp, b: j * JOBS + (18 + 2 * hp + b)
        bank = lambda n: ps_m[:, n % 2, :]
        HIS = 20
        hi_kvT = lambda j, b: j * HIS + b
        hi_ks = lambda j, b: j * HIS + (2 + b)
        hi_fold = lambda j, hp, b: j * HIS + (4 + 2 * hp + b)

        carried = [0]

        def wait_from(eng, semaphore, value):
            if not (isinstance(value, int) and value == 0):
                eng.wait_ge(semaphore, value)

        def wait_apart(eng, semaphore, value):
            eng.wait_ge(semaphore, value)
            col = slice(carried[0] % 8, carried[0] % 8 + 1)
            carried[0] += 1
            if eng.engine == nc.vector.engine:
                eng.memset(carry_v[:, col], 0.0)
            else:
                eng.tensor_tensor(carry_g[:, col], half[:, 0:1], half[:, 0:1], ALU.add)

        def over_pairs(eng, body):
            body(0, True)
            with eng.Fori(1, PAIRS - 1) as j:
                body(j, True)
            body(PAIRS - 1, False)

        ALL_HEADS = 2 * H * PAIRS

        def over_tiles(eng, step):
            for t in range(4):
                step(t, t % XR, "LGX" + "A" * (t >= 1) + "D" * (t >= 2))
            with eng.Fori(1, TILES // XR - 1) as m:
                for n in range(XR):
                    step(m * XR + n, n, "LGXAD")
            for t in range(TILES - XR, TILES + 2):
                step(t, t % XR, "L" * (t + XR - 1 < TILES) + "X" * (t + 1 < TILES) + "G" * (t < TILES) + "A" * (t <= TILES) + "D")

        block = ctx.enter_context(nc.Block())

        @block.sync
        def _(sp):
            def load_x(j, arrived):
                sp.dma_start(x_sb[:, PC * j:PC * (j + 1), :],
                             x_in[PT * j:PT * (j + 1), :].rearrange("(c p) n -> p c n", p=P)).then_inc(arrived, 16)

            load_x(0, s["x_in0"])
            sp.dma_start(ident[:], consts[:, C_EYE:C_EYE + P]).then_inc(s["ident_in"], 16)
            for k in range(KT):
                sp.dma_start(cs[:, k, 0, :], cT[k * P:(k + 1) * P, :]).then_inc(s["mod_in"], 16)
                for n in range(2):
                    sp.dma_start(wmod_sb[2 * k + n], wmod[k * P:(k + 1) * P, 3 * HID * n:3 * HID * (n + 1)]).then_inc(s["mod_in"], 16)
            sp.dma_start(bkv_sb[:].rearrange("p a n -> p (a n)"), bkv.partition_broadcast(P)).then_inc(s["bias_in"], 16)
            sp.dma_start(bq_sb[:], bqT).then_inc(s["bias_in"], 16)
            for n in range(4):
                sp.dma_start(wkv_raw[n], wkvT[(n % 2) * P:(n % 2 + 1) * P, (n // 2) * 512:(n // 2 + 1) * 512]).then_inc(s["wkv_in"], 16)
            for j in range(1, PAIRS):
                load_x(j, s["x_in"])
            sp.dma_start(ebias_sb[:], ebias.partition_broadcast(P)).then_inc(s["router_in"], 16)
            sp.dma_start(router_sb[:], routerT.rearrange("(k p) e -> p k e", p=P)).then_inc(s["router_in"], 16)
            sp.wait_ge(s["gates"], 1)
            sp.dma_start(mod_rows, gate_rows).then_inc(s["modrow_out"], 16)
            sp.wait_ge(s["wkv_lo"], 4)
            for n in range(16):
                if n >= 2:
                    sp.wait_ge(s["wst_lo"], n - 1)
                quad, m = n // 4, n % 4
                if m < 2:
                    src = wqT[m * P:(m + 1) * P, quad * STAGE:(quad + 1) * STAGE]
                else:
                    src = woT[:, (2 * quad + m - 2) * STAGE:(2 * quad + m - 1) * STAGE]
                sp.dma_start(wst[:, n % 2, :], src).then_inc(s[f"wst_in{n % 2}"], 16)
            sp.wait_ge(s["modrow_out"], 16)
            sp.wait_ge(s["zero_made"], 1)
            sp.dma_start(xs_dram.rearrange("(p t) n -> p t n", p=P), zero[:].unsqueeze(1).broadcast_to([P, TILES, HID])).then_inc(s["zeroed"], 16)

            def x1_rows(j):
                for b in range(2):
                    wait_from(sp, s["h2_step"], j * (2 * PC) + 4 * b)
                    row = mod_rows[bass.ds(j * 2 + b, 1), 0:3 * HID].rearrange("a n -> (a n)")
                    sp.dma_start(rows[:].rearrange("p a n -> p (a n)"), row.partition_broadcast(P)).then_inc(s["rows_in"], 16)
                    for c in (2 * b, 2 * b + 1):
                        sp.wait_ge(s["x1_made"], j * PC + (c + 1))
                        sp.dma_start(x1_dram[bass.ds(j * PT + c * P, P), :], acc[:, c, :]).then_inc(s["x1_out"], 16)

            x1_rows(0)
            with sp.Fori(1, PAIRS) as j:
                x1_rows(j)
            sp.wait_ge(s["h2_step"], 2 * CH)
            sp.wait_ge(s["x1_out"], 16 * CH)
            sp.dma_start(cst[:], consts).then_inc(s["cst_in"], 16)

            def load_expert(e):
                sp.dma_start(gu_raw[:], w_gu[bass.ds(e, 1), :, :].rearrange("a (k p) n -> p (a k) n", p=P)).then_inc(s["gu_in"], 16)
                sp.dma_start(dn_raw[:], w_down[bass.ds(e, 1), :, :].rearrange("a (k p) n -> p (a k) n", p=FH)).then_inc(s["dn_in"], 16)

            load_expert(0)
            with sp.Fori(1, E) as e:
                sp.wait_ge(s["gw_lo"], e * 2)
                load_expert(e)
            sp.wait_ge(s["scattered"], 16 * CH * TOPK)

            def load_tile(n, place):
                sp.dma_start(xt[:, place, :], xs_dram[bass.ds(n * P, P), :]).then_inc(s[f"xt_in{place}"], 16)

            def step(t, par, what):
                if "L" in what:
                    wait_from(sp, s["x_turned"], t)
                    load_tile(t + XR - 1, (par + XR - 1) % XR)
                if "D" in what:
                    sp.wait_ge(s["y_made"], t - 1)
                    sp.dma_start(ys_dram[bass.ds((t - 2) * P, P), :], y_sb[:, par % 2, :]).then_inc(s[f"y_out{par % 2}"], 16)

            for n in range(XR - 1):
                load_tile(n, n)
            over_tiles(sp, step)
            for par in range(2):
                sp.wait_ge(s[f"y_out{par}"], 8 * TILES)
            sp.dma_start(gb_sb[:], mod_rows[:, 3 * HID:4 * HID].partition_broadcast(P)).then_inc(s["gb_in"], 16)
            def store_chunk(c):
                sp.wait_ge(s["o_made"], c + 1)
                sp.dma_start(out[c * P:(c + 1) * P, :], o_sb[:, c % RING, :]).then_inc(s[f"o_out{c % RING}"], 16)

            for c in range(CH):
                if c >= RING:
                    sp.wait_ge(s["o_made"], c - RING + 1)
                sp.dma_start(x1_sb[:, c % RING, :], x1_dram[c * P:(c + 1) * P, :]).then_inc(s[f"x1_back{c % RING}"], 16)
                if c >= RING - 1:
                    store_chunk(c - RING + 1)
            for c in range(CH - RING + 1, CH):
                store_chunk(c)
            sp.wait_ge(s["zeroed"], 16)
            for r in range(RING):
                sp.wait_ge(s[f"o_out{r}"], 16 * CH // RING)

        @block.tensor
        def _(pe):
            def product(dst, l_hi, l_lo, r_hi, r_lo, first, last):
                pe.matmul(dst, l_hi, r_hi, start=first, stop=False)
                pe.matmul(dst, l_hi, r_lo, start=False, stop=False)
                return pe.matmul(dst, l_lo, r_hi, start=False, stop=last)

            def modulation():
                pe.wait_ge(s["silu_step"], 3)
                for m in range(2):
                    for kk in range(KT):
                        for k in range(KT):
                            last = pe.matmul(bank(m)[:, kk * B:(kk + 1) * B], wmod_of(k, m)[:, kk * P:(kk + 1) * P], cs[:, k, 0, :],
                                             start=(k == 0), stop=(k == KT - 1))
                    last.then_inc(s["misc_ready"], 1)
                for n in range(2):
                    pe.wait_ge(s["misc_done"], n + 1)
                    for m in range(2):
                        for k in range(KT):
                            last = pe.matmul(bank(n)[0:B, m * HID:(m + 1) * HID], cs[:, k, 0, :], wmod_of(k, 2 + 2 * n + m),
                                             start=(k == 0), stop=(k == KT - 1))
                    last.then_inc(s["misc_ready"], 1)

            def T(j):
                pe.wait_ge(s["xn_ready"], j * PC + PC)
                for k in range(KT):
                    pe.wait_ge(s["misc_done"], job_T(j, k) - 1)
                    for c in range(PC):
                        last = pe.transpose(bank(k)[:, c * P:(c + 1) * P], xn[:, c, k * P:(k + 1) * P], ident[:])
                    last.then_inc(s["misc_ready"], 1)

            def KV(j, c):
                pe.wait_ge(s["hT_lo"], j * KT + KT)
                for v in range(2):
                    pe.wait_ge(s["misc_done"], job_KV(j, c, v) - 1)
                    tok = slice(c * P, (c + 1) * P)
                    for k in range(KT):
                        last = product(bank(v), hT_hi[:, k, tok], hT_lo[:, k, tok], wkv_hi[:, k, v, :], wkv_lo[:, k, v, :],
                                       k == 0, k == KT - 1)
                    last.then_inc(s["misc_ready"], 1)

            def state(j):
                pe.wait_ge(s["sk_lo"], j * PC + PC)
                pe.wait_ge(s["v_lo"], j * PC + PC)
                for b in range(2):
                    pe.wait_ge(s["misc_done"], job_kvT(j, b) - 1)
                    for g in range(KVH):
                        gd = slice(g * D, (g + 1) * D)
                        for n in range(2):
                            c = 2 * b + n
                            last = product(bank(b)[:, gd], v_hi[:, c, gd], v_lo[:, c, gd], sk_hi[:, c, gd], sk_lo[:, c, gd],
                                           n == 0, n == 1)
                    last.then_inc(s["misc_ready"], 1)
                for b in range(2):
                    pe.wait_ge(s["misc_done"], job_ks(j, b) - 1)
                    for g in range(KVH):
                        for n in range(2):
                            c, gd = 2 * b + n, slice(g * D, (g + 1) * D)
                            pe.matmul(bank(b)[:, 2 * g:2 * g + 2], sk_hi[:, c, gd], ones2[:], start=(n == 0), stop=False)
                            last = pe.matmul(bank(b)[:, 2 * g:2 * g + 2], sk_lo[:, c, gd], ones2[:], start=False, stop=(n == 1))
                    last.then_inc(s["misc_ready"], 1)

            def fold(j, hp, b):
                pe.wait_ge(s["misc_done"], job_fold(j, hp, b) - 1)
                gd = slice((hp // 2) * D, (hp // 2 + 1) * D)
                w_hi, w_lo = (w[:, 2 * hp:2 * hp + 2, :].rearrange("p h n -> p (h n)") for w in (wo_hi, wo_lo))
                product(bank(b), kvT_hi[:, b, gd], kvT_lo[:, b, gd], w_hi, w_lo, True, True).then_inc(s["misc_ready"], 1)

            def Q(j, h):
                wait_from(pe, s["q_act"], j * H + (h - 1 if h >= 2 else 0))
                hd = slice(h * D, (h + 1) * D)
                for k in range(KT):
                    last = product(ps_q[:, h % 2, :], wq_hi[:, k, hd], wq_lo[:, k, hd], hT_hi[:, k, :], hT_lo[:, k, :],
                                   k == 0, k == KT - 1)
                last.then_inc(s["q_ready"], 1)

            def heads_out(j, h):
                pe.wait_ge(s["sq_lo"], j * H + (h + 1))
                for b in range(2):
                    pe.wait_ge(s["misc_done"], job_fold(j, h // 2, b) + 1)
                    wait_from(pe, s["acc_done"], j * (PC * H) + (PC * (h - 1) + 2 * b + 2 if h else 0))
                    r_hi, r_lo = (r[:, (h // 2) % 2, b, h % 2, :] for r in (kvwo_hi, kvwo_lo))
                    for c in (2 * b, 2 * b + 1):
                        tok = slice(c * P, (c + 1) * P)
                        last = product(ps_d[:, c, 0:W2], sq_hi[:, h % 2, tok], sq_lo[:, h % 2, tok], r_hi, r_lo, True, True)
                    last.then_inc(s["d_ready"], 1)

            def pair(j, more):
                state(j)
                pe.wait_ge(s["wst_lo"], 2)
                Q(j, 0)
                pe.wait_ge(s["wst_lo"], 4)
                for b in range(2):
                    fold(j, 0, b)
                Q(j, 1)
                for h in range(H):
                    if h + 2 < H:
                        pe.wait_ge(s["wst_lo"], 4 * ((h + 2) // 4) + 4)
                        Q(j, h + 2)
                    if h // 2 + 1 < H // 2:
                        fold(j, h // 2 + 1, h % 2)
                    heads_out(j, h)
                    if more and h == H - 2:
                        T(j + 1)
                        KV(j + 1, 0)
                if more:
                    for c in range(1, PC):
                        KV(j + 1, c)

            pe.wait_ge(s["ident_in"], 16)
            pe.wait_ge(s["mod_in"], 96)
            modulation()
            T(0)
            pe.wait_ge(s["wkv_lo"], 4)
            for c in range(PC):
                KV(0, c)
            pe.wait_ge(s["ones_made"], 2)
            over_pairs(pe, pair)
            pe.wait_ge(s["h2_step"], 2 * CH)
            pe.wait_ge(s["x1_out"], 16 * CH)

            def turn(c):
                if c >= PC:
                    pe.wait_ge(s["h2T_made"], c - PC + 1)
                for k in range(KT):
                    last = pe.transpose(ps_d[:, c % PC, k * P:(k + 1) * P], x_sb[:, c, k * P:(k + 1) * P], ident[:])
                last.then_inc(s["h2_turned"], 1)

            def logits(c):
                pe.wait_ge(s["h2T_made"], c + 1)
                if c >= 2:
                    pe.wait_ge(s["lg_made"], c - 1)
                for k in range(KT):
                    last = pe.matmul(ps_q[:, c % 2, 0:E], h2T[:, c % 2, k, :], router_sb[:, k, :], start=(k == 0), stop=(k == KT - 1))
                last.then_inc(s["logits"], 1)

            pe.wait_ge(s["router_in"], 32)
            turn(0)
            for c in range(1, CH):
                turn(c)
                logits(c - 1)
            logits(CH - 1)
            pe.wait_ge(s["mask_made"], 1)
            for n in range(2):
                last = pe.matmul(ps_d[:, n, 0:CH * E], tri[:, n * P:(n + 1) * P], mask[:].rearrange("p c e -> p (c e)"), start=True, stop=True)
            last.then_inc(s["counted"], 1)

            pe.wait_ge(s["tiles_made"], 1)

            def step(t, par, what):
                if "X" in what:
                    n, q, place = t + 1, 1 - par % 2, (par + 1) % XR
                    pe.wait_ge(s[f"xt_in{place}"], n * (16 // XR) + (16 - 16 // XR * place))
                    if not (isinstance(n, int) and n < 2):
                        pe.wait_ge(s["xT_lo"], n - 1)
                    for k in range(KT):
                        last = pe.transpose(ps_d[:, q, k * P:(k + 1) * P], xt[:, place, k * P:(k + 1) * P], ident[:])
                    last.then_inc(s["x_turned"], 1)
                par %= 2
                if "G" in what:
                    e = pe.value_load(tile_e[0:1, bass.ds(t, 1)], min_val=0, max_val=E - 1)
                    pe.wait_ge(s["xT_lo"], t + 1)
                    if not (isinstance(t, int) and t < 2):
                        pe.wait_ge(s["mid_done"], t - 1)
                    for k in range(KT):
                        r_hi, r_lo = (w[:, k, bass.ds(e, 1), :] for w in (gu_hi, gu_lo))
                        last = product(ps_q[:, par, 0:2 * FF], xT_hi[:, par, k, :], xT_lo[:, par, k, :], r_hi, r_lo, k == 0, k == KT - 1)
                    last.then_inc(s["gu_done"], 1)
                if "A" in what:
                    n, q = t - 1, 1 - par
                    pe.wait_ge(s["mid_done"], n + 1)
                    if not (isinstance(n, int) and n < 2):
                        pe.wait_ge(s["mT_lo"], n - 1)
                    for i in range(2):
                        last = pe.transpose(ps_d[0:FH, 2 + q, i * P:(i + 1) * P], mid[:, q, i * FH:(i + 1) * FH], ident[:])
                    last.then_inc(s["m_turned"], 1)
                if "D" in what:
                    n = t - 2
                    e = pe.value_load(tile_e[0:1, bass.ds(n, 1)], min_val=0, max_val=E - 1)
                    pe.wait_ge(s["mT_lo"], n + 1)
                    if not (isinstance(n, int) and n < 2):
                        pe.wait_ge(s["y_made"], n - 1)
                    for i in range(2):
                        r_hi, r_lo = (w[:, i, bass.ds(e, 1), :] for w in (dn_hi, dn_lo))
                        last = product(ps_m[:, par, 0:HID], mT_hi[:, par, i, :], mT_lo[:, par, i, :], r_hi, r_lo, i == 0, i == 1)
                    last.then_inc(s["down_done"], 1)

            pe.wait_ge(s["xt_in0"], 16)
            for k in range(KT):
                last = pe.transpose(ps_d[:, 0, k * P:(k + 1) * P], xt[:, 0, k * P:(k + 1) * P], ident[:])
            last.then_inc(s["x_turned"], 1)
            pe.wait_ge(s["gw_lo"], 2 * E)
            over_tiles(pe, step)

        @block.scalar
        def _(act):
            def copy_hi(dst, src):
                return act.activation(dst, src, ACT.Copy)

            def T(j, first=False):
                for k in range(KT):
                    act.wait_ge(s["misc_done"], job_T(j, k) + 1)
                    if not first:
                        act.wait_ge(s["q_ready"], j * H)
                    copy_hi(hT_hi[:, k, :], vf[:, k, :]).then_inc(s["hT_hi"], 1)

            def KV(j, c, first=False):
                act.wait_ge(s["misc_done"], job_KV(j, c, 0) + 1)
                wait_from(act, s["sk_f"], j * PC + c)
                act.activation(ke[:], kt[:, c % 2, :], ACT.Relu, scale=-1.0).then_inc(s["k_neg"], 1)
                act.activation(kt[:, c % 2, :], kt[:, c % 2, :], ACT.Relu)
                act.wait_ge(s["k_neg"], j * PC + (c + 1))
                act.activation(ke[:], ke[:], ACT.Exp, scale=-1.0).then_inc(s["k_act"], 1)
                act.wait_ge(s["misc_done"], job_KV(j, c, 1) + 1)
                if not first:
                    act.wait_ge(s["misc_ready"], j * JOBS + (18 - JOBS))
                copy_hi(v_hi[:, c, :], vf[:, c % 2, :]).then_inc(s["v_hi"], 1)
                act.wait_ge(s["sk_f"], j * PC + (c + 1))
                copy_hi(sk_hi[:, c, :], kt[:, c % 2, :]).then_inc(s["sk_hi"], 1)

            def state(j):
                for b in range(2):
                    act.wait_ge(s["misc_ready"], job_kvT(j, b) + 1)
                    copy_hi(kvT_hi[:, b, :], bank(b)).then_inc(s["misc_hi"], 1)
                for b in range(2):
                    act.wait_ge(s["misc_ready"], job_ks(j, b) + 1)
                    copy_hi(ks_hi[:, b, :, :].rearrange("p g n -> p (g n)"), bank(b)[:, 0:2 * KVH]).then_inc(s["misc_hi"], 1)

            def fold(j, hp, b):
                act.wait_ge(s["misc_ready"], job_fold(j, hp, b) + 1)
                wait_from(act, s["d_ready"], j * (2 * H) + (4 * hp - 4 if hp >= 2 else 0))
                copy_hi(kvwo_hi[:, hp % 2, b, :, 0:HID], bank(b).rearrange("p (h n) -> p h n", h=2)).then_inc(s["misc_hi"], 1)

            def elu(j, h):
                act.wait_ge(s["q_ready"], j * H + (h + 1))
                wait_from(act, s["sq_lo"], j * H + (h - 1 if h >= 2 else 0))
                act.activation(qe[:, h % 2, :], ps_q[:, h % 2, :], ACT.Relu, bias=nbq_sb[:, h:h + 1], scale=-1.0).then_inc(s["q_neg"], 1)
                act.activation(qr[:, h % 2, :], ps_q[:, h % 2, :], ACT.Relu, bias=bq_sb[:, h:h + 1]).then_inc(s["q_act"], 1)
                act.wait_ge(s["q_neg"], j * H + (h + 1))
                act.activation(qe[:, h % 2, :], qe[:, h % 2, :], ACT.Exp, scale=-1.0).then_inc(s["q_exp"], 1)

            def hi(j, h):
                act.wait_ge(s["sq_f"], j * H + (h + 1))
                wait_from(act, s["d_ready"], j * (2 * H) + (2 * h - 2 if h >= 2 else 0))
                copy_hi(sq_hi[:, h % 2, :], qe[:, h % 2, :]).then_inc(s["sq_hi"], 1)

            def pair(j, more):
                state(j)
                elu(j, 0)
                for b in range(2):
                    fold(j, 0, b)
                hi(j, 0)
                elu(j, 1)
                for h in range(H):
                    if h + 1 < H:
                        hi(j, h + 1)
                    if h + 2 < H:
                        elu(j, h + 2)
                    if h // 2 + 1 < H // 2:
                        fold(j, h // 2 + 1, h % 2)
                    if more and h == H - 2:
                        T(j + 1)
                        KV(j + 1, 0)
                if more:
                    for c in range(1, PC):
                        KV(j + 1, c)

            act.wait_ge(s["mod_in"], 96)
            act.wait_ge(s["bias_in"], 32)
            act.activation(nbq_sb[:], bq_sb[:], ACT.Copy, scale=-1.0).then_inc(s["nbq"], 1)
            act.wait_ge(s["nbq"], 1)
            act.activation(cs[:, :, 1, :], cs[:, :, 0, :], ACT.Exp, scale=-1.0).then_inc(s["silu_exp"], 1)
            for n in range(4):
                act.wait_ge(s["wkv_in"], 64)
                copy_hi(wkv_hi[:, n % 2, n // 2, :], wkv_raw[n]).then_inc(s["wkv_hi"], 1)
            T(0, first=True)
            for c in range(PC):
                KV(0, c, first=True)
            over_pairs(act, pair)
            for c in range(CH):
                act.wait_ge(s["h2_turned"], c + 1)
                if c >= 2:
                    act.wait_ge(s["logits"], c - 1)
                act.activation(h2T[:, c % 2, :, :].rearrange("p k n -> p (k n)"), ps_d[:, c % PC, 0:HID], ACT.Copy).then_inc(s["h2T_made"], 1)
            act.wait_ge(s["gap_made"], 1)
            act.activation(weight[:], gap[:], ACT.Exp).then_inc(s["exp_done"], 1)

            def split_expert(e):
                act.wait_ge(s["gu_in"], e * 16 + 16)
                copy_hi(gu_hi[:, :, bass.ds(e, 1), :].rearrange("p k a n -> p k (a n)"), gu_raw[:]).then_inc(s["gw_hi"], 1)
                act.wait_ge(s["dn_in"], e * 16 + 16)
                copy_hi(dn_hi[:, :, bass.ds(e, 1), :].rearrange("p k a n -> p k (a n)"), dn_raw[:]).then_inc(s["gw_hi"], 1)

            with act.Fori(0, E) as e:
                split_expert(e)

            def x_hi(n, q):
                act.wait_ge(s["x_turned"], n + 1)
                if not (isinstance(n, int) and n < 2):
                    act.wait_ge(s["gu_done"], n - 1)
                copy_hi(xT_hi[:, q, :, :].rearrange("p k n -> p (k n)"), ps_d[:, q, 0:HID]).then_inc(s["xT_hi"], 1)

            def step(t, par, what):
                par %= 2
                if "X" in what:
                    x_hi(t + 1, 1 - par)
                if "G" in what:
                    act.wait_ge(s["gu_done"], t + 1)
                    act.activation(silu[:, par, :], ps_q[:, par, 0:FF], ACT.Silu).then_inc(s["silu_done"], 1)
                if "A" in what:
                    n, q = t - 1, 1 - par
                    act.wait_ge(s["m_turned"], n + 1)
                    if not (isinstance(n, int) and n < 2):
                        act.wait_ge(s["down_done"], n - 1)
                    copy_hi(mT_hi[:, q, :, :].rearrange("p i n -> p (i n)"), ps_d[0:FH, 2 + q, 0:2 * P]).then_inc(s["mT_hi"], 1)
                if "D" in what:
                    n = t - 2
                    act.wait_ge(s["down_done"], n + 1)
                    if not (isinstance(n, int) and n < 2):
                        act.wait_ge(s[f"y_out{par}"], n * 8 - 8 * par)
                    act.activation(y_sb[:, par, :], ps_m[:, par, 0:HID], ACT.Copy).then_inc(s["y_made"], 1)

            x_hi(0, 0)
            over_tiles(act, step)

        @block.vector
        def _(dve):
            def split(dst, src, hi):
                return dve.tensor_tensor(dst, src, hi.bitcast(F32), ALU.subtract)

            def silu_c():
                dve.wait_ge(s["silu_exp"], 1)
                dve.tensor_scalar(cs[:, :, 2, :], cs[:, :, 1, :], 1.0, None, ALU.add).then_inc(s["silu_step"], 1)
                dve.wait_ge(s["silu_step"], 1)
                dve.reciprocal(cs[:, :, 3, :], cs[:, :, 2, :]).then_inc(s["silu_step"], 1)
                dve.wait_ge(s["silu_step"], 2)
                dve.tensor_tensor(cs[:, :, 0, :], cs[:, :, 0, :], cs[:, :, 3, :], ALU.mult).then_inc(s["silu_step"], 1)

            def modulation():
                for m, dst in enumerate((sa_col, ca_col)):
                    dve.wait_ge(s["misc_ready"], m + 1)
                    dve.tensor_scalar(dst[:].rearrange("p k b -> p (k b)"), bank(m)[:, 0:KT * B], float(m), None,
                                      ALU.add).then_inc(s["misc_done"], 1)
                dve.wait_ge(s["misc_ready"], 4)
                for n in range(2):
                    dve.tensor_copy(gate_rows[:, 2 * n * HID:(2 * n + 2) * HID], bank(n)[0:B, :]).then_inc(s["misc_done"], 1)
                dve.wait_ge(s["misc_done"], 4)
                step = 0
                tmp = qe[0:B].rearrange("p a n -> p (a n)")
                for m in (0, 3):
                    g, sign, size = gate_rows[:, m * HID:(m + 1) * HID], tmp[:, 0:HID], tmp[:, HID:2 * HID]
                    dve.tensor_scalar(sign, g, 0.0, 2.0, ALU.is_ge, ALU.mult).then_inc(s["gate_step"], 1)
                    dve.scalar_tensor_tensor(size, g, -1.0, g, ALU.mult, ALU.max).then_inc(s["gate_step"], 1)
                    dve.wait_ge(s["gate_step"], step + 2)
                    dve.tensor_scalar(sign, sign, -1.0, None, ALU.add).then_inc(s["gate_step"], 1)
                    dve.wait_ge(s["gate_step"], step + 3)
                    dve.scalar_tensor_tensor(g, size, 0.25, sign, ALU.max, ALU.mult).then_inc(s["gate_step"], 1)
                    step += 4
                    dve.wait_ge(s["gate_step"], step)
                cb = gate_rows[:, 2 * HID:3 * HID]
                dve.tensor_scalar(cb, cb, 1.0, None, ALU.add).then_inc(s["gates"], 1)

            def moments(src, n, step, base):
                for c in range(n):
                    dve.bn_stats(stats[:, c, :], src(c)).then_inc(step, 1)
                wait_apart(dve, step, base + n)
                for c in range(n):
                    dve.bn_aggr(mv[:, c, :], stats[:, c, :]).then_inc(step, 1)
                dve.wait_ge(step, base + 2 * n)
                dve.tensor_scalar(ve[:, 0:n], mv[:, 0:n, 1], LN_EPS, None, ALU.add).then_inc(step, 1)

            def ln1_moments(j):
                dve.wait_ge(s["x_in0"], 16)
                if not (isinstance(j, int) and j == 0):
                    dve.wait_ge(s["x_in"], 16 * (PAIRS - 1))
                moments(lambda c: x_sb[:, bass.ds(j * PC + c, 1), :], PC, s["ln1_step"], j * (2 * PC + 1))

            def ln1_rows(j):
                dve.wait_ge(s["ln1_rstd"], j + 1)
                for c in range(PC):
                    dve.tensor_scalar(xn[:, c:c + 1, :], x_sb[:, bass.ds(j * PC + c, 1), :], mv[:, c, 0:1], rstd[:, c:c + 1],
                                      ALU.subtract, ALU.mult).then_inc(s["xn_ready"], 1)

            def T(j):
                for k in range(KT):
                    dve.wait_ge(s["misc_ready"], job_T(j, k) + 1)
                    for b in range(2):
                        col = bass.ds(j * 2 + b, 1)
                        tok = slice(b * S, (b + 1) * S)
                        last = dve.tensor_scalar(vf[:, k, tok], bank(k)[:, tok], ca_col[:, k, col], sa_col[:, k, col], ALU.mult, ALU.add)
                    last.then_inc(s["misc_done"], 1)
                for k in range(KT):
                    dve.wait_ge(s["hT_hi"], j * KT + (k + 1))
                    split(hT_lo[:, k, :], vf[:, k, :], hT_hi[:, k, :]).then_inc(s["hT_lo"], 1)

            def KV(j, c):
                for v, dst in enumerate((kt, vf)):
                    dve.wait_ge(s["misc_ready"], job_KV(j, c, v) + 1)
                    dve.tensor_tensor(dst[:, c % 2, :], bank(v), bkv_sb[:, v, :], ALU.add).then_inc(s["misc_done"], 1)
                dve.wait_ge(s["k_act"], j * PC + (c + 1))
                dve.tensor_tensor(kt[:, c % 2, :], ke[:], kt[:, c % 2, :], ALU.add).then_inc(s["sk_f"], 1)
                dve.wait_ge(s["v_hi"], j * PC + (c + 1))
                split(v_lo[:, c, :], vf[:, c % 2, :], v_hi[:, c, :]).then_inc(s["v_lo"], 1)
                dve.wait_ge(s["sk_hi"], j * PC + (c + 1))
                split(sk_lo[:, c, :], kt[:, c % 2, :], sk_hi[:, c, :]).then_inc(s["sk_lo"], 1)

            def state(j):
                for b in range(2):
                    dve.wait_ge(s["misc_hi"], hi_kvT(j, b) + 1)
                    split(kvT_lo[:, b, :], bank(b), kvT_hi[:, b, :]).then_inc(s["misc_done"], 1)
                for b in range(2):
                    dve.wait_ge(s["misc_hi"], hi_ks(j, b) + 1)
                    split(ks_lo[:, b, :, :].rearrange("p g n -> p (g n)"), bank(b)[:, 0:2 * KVH],
                          ks_hi[:, b, :, :].rearrange("p g n -> p (g n)")).then_inc(s["misc_done"], 1)
                dve.wait_ge(s["misc_done"], job_ks(j, 1) + 1)

            def fold(j, hp, b):
                dve.wait_ge(s["misc_hi"], hi_fold(j, hp, b) + 1)
                for src, dst in ((ks_hi, kvwo_hi), (ks_lo, kvwo_lo)):
                    dve.tensor_copy(dst[:, hp % 2, b, :, HID:W2], src[:, b, hp // 2:hp // 2 + 1, :].broadcast_to([P, 2, 2]))
                split(kvwo_lo[:, hp % 2, b, :, 0:HID], bank(b).rearrange("p (h n) -> p h n", h=2),
                      kvwo_hi[:, hp % 2, b, :, 0:HID]).then_inc(s["misc_done"], 1)

            def elu(j, h):
                dve.wait_ge(s["q_exp"], j * H + (h + 1))
                dve.tensor_tensor(qe[:, h % 2, :], qe[:, h % 2, :], qr[:, h % 2, :], ALU.add).then_inc(s["sq_f"], 1)

            def lo(j, h):
                dve.wait_ge(s["sq_hi"], j * H + (h + 1))
                split(sq_lo[:, h % 2, :], qe[:, h % 2, :], sq_hi[:, h % 2, :]).then_inc(s["sq_lo"], 1)

            def heads_out(j, h):
                for b in range(2):
                    dve.wait_ge(s["d_ready"], j * (2 * H) + (2 * h + b + 1))
                    n = 4 * h + 2 * b
                    dve.tensor_scalar(rr[:, b, :], ps_d[:, 2 * b:2 * b + 2, HID], NORM_EPS, None, ALU.add).then_inc(s["rn_step"], 1)
                    dve.wait_ge(s["rn_step"], j * (4 * H) + (n + 1))
                    dve.reciprocal(rn[:, b, :], rr[:, b, :]).then_inc(s["rn_step"], 1)
                    dve.wait_ge(s["rn_step"], j * (4 * H) + (n + 2))
                    for i in range(2):
                        c = 2 * b + i
                        if h == 0:
                            wait_from(dve, s["x1_out"], j * (16 * PC))
                            dve.tensor_scalar(acc[:, c, :], ps_d[:, c, 0:HID], rn[:, b, i:i + 1], None, ALU.mult).then_inc(s["acc_done"], 1)
                        else:
                            dve.wait_ge(s["acc_done"], j * (PC * H) + (PC * (h - 1) + c + 1))
                            dve.scalar_tensor_tensor(acc[:, c, :], ps_d[:, c, 0:HID], rn[:, b, i:i + 1], acc[:, c, :],
                                                     ALU.mult, ALU.add).then_inc(s["acc_done"], 1)

            def ln2(j):
                for b in range(2):
                    dve.wait_ge(s["x1_made"], j * PC + (2 * b + 2))
                    moments(lambda c: acc[:, 2 * b + c, :], 2, s["ln2_step"], j * 10 + 5 * b)
                    dve.wait_ge(s["ln2_rstd"], j * 2 + (b + 1))
                    for i in range(2):
                        c = 2 * b + i
                        dve.tensor_scalar(x_sb[:, bass.ds(j * PC + c, 1), :], acc[:, c:c + 1, :], mv[:, i, 0:1], rstd[:, i:i + 1],
                                          ALU.subtract, ALU.mult).then_inc(s["h2_n"], 1)

            def pair(j, more):
                state(j)
                elu(j, 0)
                for b in range(2):
                    fold(j, 0, b)
                lo(j, 0)
                elu(j, 1)
                for h in range(H):
                    if h + 1 < H:
                        lo(j, h + 1)
                    if h + 2 < H:
                        elu(j, h + 2)
                    if h // 2 + 1 < H // 2:
                        fold(j, h // 2 + 1, h % 2)
                    heads_out(j, h)
                    if more and h == H - 6:
                        ln1_moments(j + 1)
                    if more and h == H - 4:
                        ln1_rows(j + 1)
                    if more and h == H - 2:
                        T(j + 1)
                        KV(j + 1, 0)
                if more:
                    for c in range(1, PC):
                        KV(j + 1, c)
                ln2(j)

            dve.memset(ones_f[:], 1.0).then_inc(s["ones_made"], 1)
            dve.wait_ge(s["ones_made"], 1)
            dve.tensor_copy(ones2[:], ones_f[:]).then_inc(s["ones_made"], 1)
            silu_c()
            ln1_moments(0)
            modulation()
            dve.wait_ge(s["misc_ready"], 4)
            ln1_rows(0)
            for n in range(4):
                dve.wait_ge(s["wkv_hi"], n + 1)
                split(wkv_lo[:, n % 2, n // 2, :], wkv_raw[n], wkv_hi[:, n % 2, n // 2, :]).then_inc(s["wkv_lo"], 1)
            T(0)
            dve.wait_ge(s["bias_in"], 32)
            for c in range(PC):
                KV(0, c)
            dve.wait_ge(s["modrow_out"], 16)
            over_pairs(dve, pair)
            steps_done = [0]

            def then(ins):
                ins.then_inc(s["route_step"], 1)
                steps_done[0] += 1
                dve.wait_ge(s["route_step"], steps_done[0])

            iota_row, tile_row = cst[:, C_IOTA:C_IOTA + E], cst[0:1, C_TILE:C_TILE + TILES]
            flat = lambda t: t.rearrange("p c k -> p (c k)")
            dve.wait_ge(s["cst_in"], 16)
            dve.wait_ge(s["router_in"], 32)
            dve.wait_ge(s["h2_step"], 2 * CH)
            dve.wait_ge(s["x1_out"], 16 * CH)
            dve.tensor_copy(tri[:], cst[:, C_TRI:C_TRI + 2 * P])
            dve.memset(cum[:, 0, :], 0.0)
            for c in range(CH):
                dve.wait_ge(s["logits"], c + 1)
                dve.tensor_tensor(lg[:, c, :], ps_q[:, c % 2, 0:E], ebias_sb[:], ALU.add).then_inc(s["lg_made"], 1)
            dve.wait_ge(s["lg_made"], CH)
            for c in range(CH):
                last = dve.max(top8[:, c, :], lg[:, c, :])
            then(last)
            for c in range(CH):
                last = dve.max_index(arg8[:, c, :], top8[:, c, :], lg[:, c, :])
            dve.tensor_tensor(gap[:], top8[:, :, 0:TOPK], top8[:, :, 0:1].broadcast_to([P, CH, TOPK]), ALU.subtract).then_inc(s["gap_made"], 1)
            then(last)
            then(dve.tensor_copy(arg_f[:], arg8[:, :, 0:TOPK]))
            hot_n = hot[:].rearrange("p c k e -> p (c k) e")
            then(dve.tensor_tensor(hot_n, flat(arg_f[:]).unsqueeze(2).broadcast_to([P, CH * TOPK, E]),
                                   iota_row.unsqueeze(1).broadcast_to([P, CH * TOPK, E]), ALU.is_equal))
            then(dve.tensor_reduce(pos[:], hot[:].rearrange("p c k e -> p c e k"), AX_X, ALU.add))
            dve.tensor_copy(mask[:], pos[:]).then_inc(s["mask_made"], 1)
            dve.wait_ge(s["exp_done"], 1)
            then(dve.tensor_reduce(wsum[:], weight[:], AX_X, ALU.add))
            then(dve.reciprocal(wrec[:], wsum[:]))
            then(dve.tensor_tensor(wgt[:], weight[:], wrec[:].unsqueeze(2).broadcast_to([P, CH, TOPK]), ALU.mult))
            dve.wait_ge(s["counted"], 1)
            for c in range(CH):
                then(dve.tensor_tensor(cum[:, c + 1, :], cum[:, c, :], ps_d[:, 1, c * E:(c + 1) * E], ALU.add))
            then(dve.tensor_scalar(steps[:], iota_row, float(P), None, ALU.mult))
            then(dve.tensor_tensor(cmp[:], cum[:, CH, :].unsqueeze(2).broadcast_to([P, E, E]), steps[:].unsqueeze(1).broadcast_to([P, E, E]), ALU.is_gt))
            then(dve.tensor_reduce(ntile[:], cmp[:], AX_X, ALU.add))
            low = cst[:, C_LOW:C_LOW + E * E].rearrange("p (a b) -> p a b", b=E)
            then(dve.tensor_tensor(cmp[:], low, ntile[:].unsqueeze(1).broadcast_to([P, E, E]), ALU.mult))
            then(dve.tensor_reduce(start[:], cmp[:], AX_X, ALU.add))
            then(dve.tensor_scalar(start_slot[:], start[:], float(P), None, ALU.mult))
            then(dve.tensor_tensor(pos[:], ps_d[:, 0, 0:CH * E].rearrange("p (c e) -> p c e", e=E), cum[:, 0:CH, :], ALU.add))
            then(dve.tensor_tensor(pos[:], pos[:], start_slot[:].unsqueeze(1).broadcast_to([P, CH, E]), ALU.add))
            then(dve.tensor_tensor(hot[:], hot[:], pos[:].unsqueeze(2).broadcast_to([P, CH, TOPK, E]), ALU.mult))
            then(dve.tensor_reduce(flat(arg_f[:]), hot_n, AX_X, ALU.add))
            dve.tensor_copy(slot_i[:], arg_f[:]).then_inc(s["slots_made"], 1)
            then(dve.tensor_tensor(tcmp[:], start[0:1, :].unsqueeze(1).broadcast_to([1, TILES, E]), tile_row.unsqueeze(2).broadcast_to([1, TILES, E]), ALU.is_le))
            then(dve.tensor_reduce(tsum[:], tcmp[:], AX_X, ALU.add))
            dve.tensor_scalar(tile_e[:], tsum[:], -1.0, None, ALU.add).then_inc(s["tiles_made"], 1)
            dve.wait_ge(s["tiles_made"], 1)

            def split_expert(e):
                dve.wait_ge(s["gw_hi"], e * 2 + 1)
                split(gu_lo[:, :, bass.ds(e, 1), :].rearrange("p k a n -> p k (a n)"), gu_raw[:],
                      gu_hi[:, :, bass.ds(e, 1), :].rearrange("p k a n -> p k (a n)")).then_inc(s["gw_lo"], 1)
                dve.wait_ge(s["gw_hi"], e * 2 + 2)
                split(dn_lo[:, :, bass.ds(e, 1), :].rearrange("p k a n -> p k (a n)"), dn_raw[:],
                      dn_hi[:, :, bass.ds(e, 1), :].rearrange("p k a n -> p k (a n)")).then_inc(s["gw_lo"], 1)

            with dve.Fori(0, E) as e:
                split_expert(e)

            def x_lo(n, q):
                dve.wait_ge(s["xT_hi"], n + 1)
                split(xT_lo[:, q, :, :].rearrange("p k n -> p (k n)"), ps_d[:, q, 0:HID],
                      xT_hi[:, q, :, :].rearrange("p k n -> p (k n)")).then_inc(s["xT_lo"], 1)

            def step(t, par, what):
                par %= 2
                if "X" in what:
                    x_lo(t + 1, 1 - par)
                if "G" in what:
                    dve.wait_ge(s["silu_done"], t + 1)
                    if not (isinstance(t, int) and t < 2):
                        dve.wait_ge(s["m_turned"], t - 1)
                    dve.tensor_tensor(mid[:, par, :], silu[:, par, :], ps_q[:, par, FF:2 * FF], ALU.mult).then_inc(s["mid_done"], 1)
                if "A" in what:
                    n, q = t - 1, 1 - par
                    dve.wait_ge(s["mT_hi"], n + 1)
                    split(mT_lo[:, q, :, :].rearrange("p i n -> p (i n)"), ps_d[0:FH, 2 + q, 0:2 * P],
                          mT_hi[:, q, :, :].rearrange("p i n -> p (i n)")).then_inc(s["mT_lo"], 1)

            x_lo(0, 0)
            over_tiles(dve, step)

            dve.wait_ge(s["gb_in"], 16)
            for c in range(CH):
                r, o = c % RING, o_sb[:, c % RING, :]
                dve.wait_ge(s[f"gathered{r}"], 16 * TOPK * (c // RING + 1))
                if c >= RING:
                    dve.wait_ge(s[f"o_out{r}"], 16 * (c // RING))
                then(dve.tensor_scalar(o, yg[:, r, 0, :], wgt[:, c, 0:1], None, ALU.mult))
                for k in range(1, TOPK):
                    then(dve.scalar_tensor_tensor(o, yg[:, r, k, :], wgt[:, c, k:k + 1], o, ALU.mult, ALU.add))
                then(dve.tensor_tensor(o, o, gb_sb[:, c * P // S, :], ALU.mult))
                dve.wait_ge(s[f"x1_back{r}"], 16 * (c // RING + 1))
                dve.tensor_tensor(o, o, x1_sb[:, r, :], ALU.add).then_inc(s["o_made"], 1)

        @block.gpsimd
        def _(pool):
            def inverse_root(n, counter):
                pool.tensor_tensor(rstd[:, 0:n], ve[:, 0:n], half[:, 0:n], ALU.pow).then_inc(counter, 1)

            pool.memset(half[:], -0.5).then_inc(s["half_made"], 1)
            pool.memset(zero[:], 0.0).then_inc(s["zero_made"], 1)
            pool.wait_ge(s["half_made"], 1)
            pool.wait_ge(s["ln1_step"], 2 * PC + 1)
            inverse_root(PC, s["ln1_rstd"])
            for n in range(16):
                pool.wait_ge(s[f"wst_in{n % 2}"], 16 * (n // 2 + 1))
                quad, m = n // 4, n % 4
                if m < 2:
                    hi, lo = (w[:, m, quad * STAGE:(quad + 1) * STAGE] for w in (wq_hi, wq_lo))
                else:
                    hi, lo = (w[:, 4 * quad + 2 * m - 4:4 * quad + 2 * m - 2, :].rearrange("p h n -> p (h n)") for w in (wo_hi, wo_lo))
                pool.tensor_copy(hi, wst[:, n % 2, :]).then_inc(s["wst_hi"], 1)
                pool.wait_ge(s["wst_hi"], n + 1)
                pool.tensor_tensor(lo, wst[:, n % 2, :], hi.bitcast(F32), ALU.subtract).then_inc(s["wst_lo"], 1)

            def pair(j, more):
                if more:
                    pool.wait_ge(s["ln1_step"], j * (2 * PC + 1) + 2 * (2 * PC + 1))
                    inverse_root(PC, s["ln1_rstd"])
                for b in range(2):
                    pool.wait_ge(s["rows_in"], j * 32 + 16 * (b + 1))
                    pool.wait_ge(s["acc_done"], j * (PC * H) + PC * H)
                    for i in range(2):
                        c = 2 * b + i
                        x = x_sb[:, bass.ds(j * PC + c, 1), :]
                        pool.tensor_tensor(acc[:, c, :], acc[:, c, :], rows[:, 0, :], ALU.mult).then_inc(s["x1_step"], 1)
                        wait_apart(pool, s["x1_step"], j * PC + (c + 1))
                        pool.tensor_tensor(acc[:, c:c + 1, :], acc[:, c:c + 1, :], x, ALU.add).then_inc(s["x1_made"], 1)
                    pool.wait_ge(s["ln2_step"], j * 10 + 5 * (b + 1))
                    inverse_root(2, s["ln2_rstd"])
                    for i in range(2):
                        c = 2 * b + i
                        x = x_sb[:, bass.ds(j * PC + c, 1), :]
                        wait_apart(pool, s["h2_n"], j * PC + (c + 1))
                        pool.tensor_tensor(x, x, rows[:, 2:3, :], ALU.mult).then_inc(s["h2_step"], 1)
                        wait_apart(pool, s["h2_step"], j * (2 * PC) + (2 * c + 1))
                        pool.tensor_tensor(x, x, rows[:, 1:2, :], ALU.add).then_inc(s["h2_step"], 1)

            over_pairs(pool, pair)
            pool.wait_ge(s["zeroed"], 16)
            pool.wait_ge(s["slots_made"], 1)
            for c in range(CH):
                for k in range(TOPK):
                    pool.indirect_dma_start(xs_dram, bass.IndirectOffsetOnAxis(slot_i[:, c, k:k + 1], 0), x_sb[:, c, :], None
                                            ).then_inc(s["scattered"], 16)
            for par in range(2):
                pool.wait_ge(s[f"y_out{par}"], 8 * TILES)
            for c in range(CH):
                if c >= RING:
                    pool.wait_ge(s["o_made"], c - RING + 1)
                for k in range(TOPK):
                    pool.indirect_dma_start(yg[:, c % RING, k, :], None, ys_dram, bass.IndirectOffsetOnAxis(slot_i[:, c, k:k + 1], 0)
                                            ).then_inc(s[f"gathered{c % RING}"], 16)


def kernel(**inputs):
    import numpy as np
    import concourse.bacc as bacc
    from concourse.bass_utils import run_bass_kernel_spmd

    a = {n.removeprefix("L0_").removeprefix("attn_").removeprefix("ffn_"): np.asarray(v) for n, v in inputs.items()}
    laid = {
        "x_in": a["hidden_states"].reshape(TOK, HID),
        "wqT": a["Wq"].T,
        "wkvT": np.concatenate([a["Wk"].T, a["Wv"].T], axis=1),
        "woT": a["Wo"].T.reshape(H, D, HID).transpose(1, 0, 2).reshape(D, H * HID),
        "bqT": a["bq"].reshape(H, D).T,
        "bkv": np.concatenate([a["bk"], a["bv"]]),
        "routerT": a["router_w"].T,
        "ebias": a["expert_bias"],
        "w_gu": np.concatenate([a["gate_proj"], a["up_proj"]], axis=2),
        "w_down": a["down_proj"],
        "cT": a["c"].T,
        "wmod": a["wmod"],
        "consts": constants(),
    }
    nc = bacc.Bacc("TRN2", target_bir_lowering=False, num_devices=1)
    arrays, args = {}, []
    for name, v in laid.items():
        arrays[name] = np.ascontiguousarray(v)
        args.append(nc.dram_tensor(name, v.shape, mybir.dt.from_np(v.dtype), kind="ExternalInput").ap())
    args.append(nc.dram_tensor("out", (TOK, HID), F32, kind="ExternalOutput").ap())
    adaln_block(nc, *args)
    r = run_bass_kernel_spmd(nc, [arrays], core_ids=[0])
    return r.results[0]["out"].reshape(B, S, HID)
```

```python
from contextlib import ExitStack

import concourse.bass as bass
from concourse import mybir

P = 128
F32 = mybir.dt.float32
F32R = mybir.dt.float32r
BF16 = mybir.dt.bfloat16
I32 = mybir.dt.int32
U32 = mybir.dt.uint32
ALU = mybir.AluOpType
ACT = mybir.ActivationFunctionType
AX_X = mybir.AxisListType.X

B, S, HID = 8, 256, 256
H, KVH, D = 16, 4, 128
GROUPS = H // KVH
KT = HID // P
TOK = B * S
CH = TOK // P
PAIRS = B // 2
PC = CH // PAIRS
PT = PC * P
E, TOPK, FF = 16, 4, 224
FH = FF // 2
LN_EPS, NORM_EPS = 1e-5, 1e-6
TILES = (TOK * TOPK + E * (P - 1)) // P
UNROLL = 8
TILES += -TILES % UNROLL
SLOTS = TILES * P
W2 = HID + 2
XR = 4
RING = 4
ROUTING_AT = 153 * 1024
WR = 4
STAGE = 512


def constants():
    import numpy as np
    eye = np.eye(P)
    iota = np.tile(np.arange(E), (P, 1))
    low = np.tile((np.arange(E)[None, :] < np.arange(E)[:, None]).reshape(1, E * E), (P, 1))
    before = np.arange(P)[:, None] < np.arange(P)[None, :]
    tiles = np.tile(np.arange(TILES), (P, 1))
    return np.concatenate([eye, iota, low, before, np.ones((P, P)), tiles], axis=1).astype(np.float32)


C_EYE, C_IOTA, C_LOW, C_TRI, C_TILE, C_END = 0, P, P + E, P + E + E * E, 3 * P + E + E * E, 3 * P + E + E * E + TILES


def adaln_block(nc, x_in, wqT, wkvT, woT, bqT, bkv, routerT, ebias, w_gu, w_down, cT, wmod, consts, out):
    mod_rows = nc.dram_tensor("mod_rows", (B, 4 * HID), F32).ap()
    x1_dram = nc.dram_tensor("x1_dram", (TOK, HID), F32).ap()
    xs_dram = nc.dram_tensor("xs_dram", (SLOTS, HID), F32).ap()
    ys_dram = nc.dram_tensor("ys_dram", (SLOTS, HID), F32).ap()

    with ExitStack() as ctx:
        keep = lambda name, shape, dt=F32: ctx.enter_context(nc.sbuf_tensor(name, shape, dt))
        ps_q = ctx.enter_context(nc.psum_tensor("ps_q", [P, 2, 512], F32))
        ps_d = ctx.enter_context(nc.psum_tensor("ps_d", [P, PC, 512], F32))
        ps_m = ctx.enter_context(nc.psum_tensor("ps_m", [P, 2, 512], F32))

        ident = keep("ident", [P, P])
        wgt = keep("wgt", [P, CH, TOPK])
        slot_i = keep("slot_i", [P, CH, TOPK], I32)
        tile_e = keep("tile_e", [1, TILES], I32)
        ebias_sb = keep("ebias_sb", [P, E])
        router_sb = keep("router_sb", [P, KT, E])
        carry_v, carry_g = keep("carry_v", [P, 8]), keep("carry_g", [P, 8])
        half = keep("half", [P, PC])
        stats = keep("stats", [P, PC, 6])
        mv = keep("mv", [P, PC, 2])
        ve = keep("ve", [P, PC])
        rstd = keep("rstd", [P, PC])
        rr = keep("rr", [P, 2, 2])
        rn = keep("rn", [P, 2, 2])

        with ExitStack() as attn:
            sb = lambda name, shape, dt=F32: attn.enter_context(nc.sbuf_tensor(name, shape, dt))
            wq_hi, wq_lo = (sb(n, [P, KT, H * D], F32R) for n in ("wq_hi", "wq_lo"))
            wkv_hi, wkv_lo = (sb(n, [P, KT, 2, KVH * D], F32R) for n in ("wkv_hi", "wkv_lo"))
            wo_hi, wo_lo = (sb(n, [P, H, HID], F32R) for n in ("wo_hi", "wo_lo"))
            hT_hi, hT_lo = (sb(n, [P, KT, PT], F32R) for n in ("hT_hi", "hT_lo"))
            sk_hi, sk_lo = (sb(n, [P, PC, KVH * D], F32R) for n in ("sk_hi", "sk_lo"))
            v_hi, v_lo = (sb(n, [P, PC, KVH * D], F32R) for n in ("v_hi", "v_lo"))
            kvT_hi, kvT_lo = (sb(n, [P, 2, KVH * D], F32R) for n in ("kvT_hi", "kvT_lo"))
            kvwo_hi, kvwo_lo = (sb(n, [P, 2, 2, 2, W2], F32R) for n in ("kvwo_hi", "kvwo_lo"))
            ks_hi, ks_lo = (sb(n, [P, 2, KVH, 2], F32R) for n in ("ks_hi", "ks_lo"))
            sq_hi, sq_lo = (sb(n, [P, 2, PT], F32R) for n in ("sq_hi", "sq_lo"))
            kt = sb("kt", [P, 2, 512])
            vf = sb("vf", [P, 2, 512])
            ke = sb("ke", [P, 512])
            acc = sb("acc", [P, PC, HID])
            bkv_sb = sb("bkv_sb", [P, 2, 512])
            wst = sb("wst", [P, 2, STAGE])
            rows = sb("rows", [P, 2, 2, HID])
            ones_f = sb("ones_f", [P, 2])
            zero = sb("zero", [P, HID])
            bq_sb, nbq_sb, bq1_sb = (sb(n, [P, H]) for n in ("bq_sb", "nbq_sb", "bq1_sb"))
            cs = sb("cs", [P, KT, 4, B])
            sa_col, ca_col = (sb(n, [P, KT, B]) for n in ("sa_col", "ca_col"))
            key_sums = sb("key_sums", [P, 2, KVH * D])
            qe = sb("qe", [P, 2, PT])
            x_sb = sb("x_sb", [P, CH, HID])
        ga_rows = wst[:, 0, :].rearrange("p (b n) -> p b n", b=2)
        xn = kt[:].rearrange("p a (c n) -> p (a c) n", n=HID)
        wmod_sb = x_sb[:, PC:, :].rearrange("p (k m) n -> p k m n", k=KT)
        gate_rows = rows[0:B].rearrange("p a m n -> p (a m n)")
        d3 = key_sums[:].rearrange("p b (n m) -> p b n m", n=2)[:, :, 0, :]
        wkv_raw = [acc[:, 0:2, :].rearrange("p c n -> p (c n)"), acc[:, 2:4, :].rearrange("p c n -> p (c n)"),
                   wst[:, 0, :], wst[:, 1, :]]


        with ExitStack() as ffn:
            sb = lambda name, shape, dt=F32: ffn.enter_context(nc.sbuf_tensor(name, shape, dt))
            gu_hi, gu_lo = (sb(n, [P, E, KT, 2 * FF], F32R) for n in ("gu_hi", "gu_lo"))
            dn_hi, dn_lo = (sb(n, [FH, E, 2, HID], F32R) for n in ("dn_hi", "dn_lo"))
            xt = sb("xt", [P, XR, HID])
            xT_hi, xT_lo = (sb(n, [P, 2, KT, P], F32R) for n in ("xT_hi", "xT_lo"))
            silu = sb("silu", [P, 2, FF])
            mid = sb("mid", [P, 2, FF])
            mT_hi, mT_lo = (sb(n, [FH, 2, 2, P], F32R) for n in ("mT_hi", "mT_lo"))
            y_sb = sb("y_sb", [P, 2, HID])
        with ExitStack() as arrive:
            sb = lambda name, shape, dt=F32: arrive.enter_context(nc.sbuf_tensor(name, shape, dt))
            sb("over_gu_hi", [P, E, KT, 2 * FF])
            gu_raw = sb("gu_raw", [P, E, KT, 2 * FF])
            sb("over_dn_hi", [FH, E, 2, HID])
            dn_raw = sb("dn_raw", [FH, E, 2, HID])
        with ExitStack() as route:
            sb = lambda name, shape, dt=F32: route.enter_context(nc.sbuf_tensor(name, shape, dt))
            sb("below_routing", [P, ROUTING_AT // 4])
            cst = sb("cst", [P, C_END])
            hot = sb("hot", [P, CH, TOPK, E])
            pos = sb("pos", [P, CH, E])
            cum = sb("cum", [P, CH + 1, E])
            lg = sb("lg", [P, CH, E])
            mask = sb("mask", [P, CH, E], BF16)
            h2T = sb("h2T", [P, 2, KT, P])
            tri = sb("tri", [P, 2 * P], BF16)
            top8 = sb("top8", [P, CH, 8])
            arg8 = sb("arg8", [P, CH, 8], U32)
            arg_f, gap, weight = (sb(n, [P, CH, TOPK]) for n in ("arg_f", "gap", "weight"))
            wsum, wrec = (sb(n, [P, CH]) for n in ("wsum", "wrec"))
            cmp = sb("cmp", [P, E, E])
            steps = sb("steps", [P, E])
            ntile, start, start_slot = (sb(n, [P, E]) for n in ("ntile", "start", "start_slot"))
            tcmp = sb("tcmp", [1, TILES, E])
            tsum = sb("tsum", [1, TILES])
        with ExitStack() as combine:
            sb = lambda name, shape, dt=F32: combine.enter_context(nc.sbuf_tensor(name, shape, dt))
            yg = sb("yg", [P, RING, TOPK, HID])
            x1_sb = sb("x1_sb", [P, RING, HID])
            gb_sb = sb("gb_sb", [P, B, HID])
            o_sb = sb("o_sb", [P, RING, HID])

        s = {n: ctx.enter_context(nc.semaphore(n)) for n in (
            "x_in0", "x_in", "ident_in", "bias_in", "router_in", "c_in", "mod_in0", "mod_in1",  "wkv_in", "wst_in0", "wst_in1", "ga_in", "rows_in", "ksum_in", "zero_made", "zeroed", "x1_out",
            "silu_exp", "silu_step", "gates", "gate_step", "modrow_out", "ones_made", "half_made",
            "wkv_hi", "wkv_lo", "wst_hi", "wst_lo", "misc_ready", "misc_done", "misc_hi",
            "ln1_step", "ln1_rstd", "ln2_step", "ln2_rstd", "xn_ready", "hT_hi", "hT_lo",
            "k_neg", "k_act", "q_neg", "q_exp", "nbq", "bq1", "sk_f", "sk_hi", "sk_lo", "v_hi", "v_lo",
            "q_ready", "sq_f", "sq_hi", "sq_lo", "d_ready", "rn_step", "acc_done", "d3_scaled", "acc3_done",
            "x1_step", "x1_made", "h2_n", "h2_step",
            "cst_in", "h2_turned", "h2T_made", "logits", "route_step", "exp_done", "mask_made", "counted",
            "slots_made", "tiles_made", "scattered",
            *(f"w_in{r}" for r in range(WR)), "gw_hi", "gw_lo", *(f"xt_in{r}" for r in range(XR)), "x_turned", "xT_hi", "xT_lo", "gu_done", "silu_done", "mid_done",
            "m_turned", "mT_hi", "mT_lo", "down_done", "y_made", "y_out0", "y_out1",
            "lg_made", "gap_made", *(f"{n}{r}" for n in ("gathered", "x1_back", "o_out") for r in range(RING)), "gb_in", "sum_step", "o_made")}

        JOBS = 30
        job_T = lambda j, k: j * JOBS + ((2 if isinstance(j, int) and j == 0 else 4) + k)
        job_KV = lambda j, c, v: j * JOBS + (6 + 2 * c + 2 * (c // 3) + v)
        job_kvT = lambda j, b: j * JOBS + (12 + 6 * b)
        job_ks = lambda j, b: j * JOBS + (13 + 6 * b)
        fold_place = lambda hp, b: (4 + 2 * hp + b) if hp >= 2 else (2 + hp + 4 * b)
        job_fold = lambda j, hp, b: j * JOBS + (14 + fold_place(hp, b))
        bank = lambda n: ps_m[:, n % 2, :]
        def piece_of(n, wq, wo):
            quad, m = n // 4, n % 4
            if m < 2:
                return wq[:, m, quad * STAGE:(quad + 1) * STAGE]
            return wo[:, 4 * quad + 2 * m - 4:4 * quad + 2 * m - 2, :].rearrange("p h n -> p (h n)")

        FOLDS_AT = [[(h // 2 + 1, h % 2)] if 2 <= h < H - 4 else [] for h in range(H)]
        FOLDS_AT[H - 4] = [(H // 2 - 1, 0), (H // 2 - 1, 1)]
        HIS = 20
        hi_kvT = lambda j, b: j * HIS + 4 * b
        hi_ks = lambda j, b: j * HIS + (4 * b + 1)
        hi_fold = lambda j, hp, b: j * HIS + fold_place(hp, b)
        bank_fold = lambda hp, b: bank(job_fold(0, hp, b))

        carried = [0]

        def wait_from(eng, semaphore, value):
            if not (isinstance(value, int) and value == 0):
                eng.wait_ge(semaphore, value)

        def wait_apart(eng, semaphore, value):
            eng.wait_ge(semaphore, value)
            col = slice(carried[0] % 8, carried[0] % 8 + 1)
            carried[0] += 1
            if eng.engine == nc.vector.engine:
                eng.memset(carry_v[:, col], 0.0)
            else:
                eng.tensor_tensor(carry_g[:, col], half[:, 0:1], half[:, 0:1], ALU.add)

        def over_pairs(eng, body):
            body(0, False, True)
            with eng.Fori(1, PAIRS - 1) as j:
                body(j, True, True)
            body(PAIRS - 1, True, False)

        ALL_HEADS = 2 * H * PAIRS

        def over_tiles(eng, step):
            for t in range(UNROLL):
                step(t, t, "LGX" + "A" * (t >= 1) + "D" * (t >= 2))
            with eng.Fori(1, TILES // UNROLL - 1) as m:
                for n in range(UNROLL):
                    step(m * UNROLL + n, n, "LGXAD")
            for n in range(UNROLL + 2):
                t = TILES - UNROLL + n
                step(t, n, "L" * (t + XR - 1 < TILES) + "X" * (t + 1 < TILES) + "G" * (t < TILES) + "A" * (t <= TILES) + "D")

        block = ctx.enter_context(nc.Block())

        @block.sync
        def _(sp):
            def load_x(j, arrived):
                sp.dma_start(x_sb[:, PC * j:PC * (j + 1), :],
                             x_in[PT * j:PT * (j + 1), :].rearrange("(c p) n -> p c n", p=P)).then_inc(arrived, 16)

            for k in range(KT):
                sp.dma_start(cs[:, k, 0, :], cT[k * P:(k + 1) * P, :]).then_inc(s["c_in"], 16)
            load_x(0, s["x_in0"])
            load_wmod = lambda part, k, m: sp.dma_start(wmod_sb[:, k, m[0]:m[1], :], wmod[k * P:(k + 1) * P, HID * m[0]:HID * m[1]].rearrange(
                "p (m n) -> p m n", n=HID)).then_inc(s[f"mod_in{part}"], 16)
            for k in range(KT):
                load_wmod(0, k, (0, 2))
            sp.dma_start(ident[:], consts[:, C_EYE:C_EYE + P]).then_inc(s["ident_in"], 16)
            for n in range(4):
                sp.dma_start(wkv_raw[n], wkvT[(n % 2) * P:(n % 2 + 1) * P, (n // 2) * 512:(n // 2 + 1) * 512]).then_inc(s["wkv_in"], 16)
            for k in range(KT):
                load_wmod(1, k, (2, 6))
            sp.dma_start(bkv_sb[:].rearrange("p a n -> p (a n)"), bkv.partition_broadcast(P)).then_inc(s["bias_in"], 16)
            sp.dma_start(bq_sb[:], bqT).then_inc(s["bias_in"], 16)
            sp.dma_start(ebias_sb[:], ebias.partition_broadcast(P)).then_inc(s["router_in"], 16)
            sp.dma_start(router_sb[:], routerT.rearrange("(k p) e -> p k e", p=P)).then_inc(s["router_in"], 16)
            sp.wait_ge(s["misc_ready"], 6)
            for j in range(1, PAIRS):
                load_x(j, s["x_in"])
            sp.wait_ge(s["wkv_lo"], 4)
            for n in range(16):
                if n >= 2:
                    sp.wait_ge(s["wst_lo"], n - 1)
                quad, m = n // 4, n % 4
                if m < 2:
                    src = wqT[m * P:(m + 1) * P, quad * STAGE:(quad + 1) * STAGE]
                else:
                    src = woT[:, (2 * quad + m - 2) * STAGE:(2 * quad + m - 1) * STAGE]
                sp.dma_start(wst[:, n % 2, :], src).then_inc(s[f"wst_in{n % 2}"], 16)
            sp.wait_ge(s["gates"], 1)
            sp.dma_start(mod_rows, gate_rows).then_inc(s["modrow_out"], 16)
            sp.wait_ge(s["modrow_out"], 16)
            sp.wait_ge(s["zero_made"], 1)
            sp.dma_start(xs_dram.rearrange("(p t) n -> p t n", p=P), zero[:].unsqueeze(1).broadcast_to([P, TILES, HID])).then_inc(s["zeroed"], 16)

            def x1_rows(j):
                of_pair = lambda lo, hi: mod_rows[bass.ds(j * 2, 2), lo:hi].partition_broadcast(P)
                if isinstance(j, int):
                    sp.wait_ge(s["wst_lo"], 16)
                else:
                    sp.wait_ge(s["x1_made"], j * PC)
                sp.dma_start(ga_rows, of_pair(0, HID)).then_inc(s["ga_in"], 16)
                if isinstance(j, int):
                    sp.wait_ge(s["zeroed"], 16)
                else:
                    sp.wait_ge(s["h2_step"], j * (2 * PC))
                sp.dma_start(rows[:].rearrange("p b m n -> p b (m n)"), of_pair(HID, 3 * HID)).then_inc(s["rows_in"], 16)
                sp.wait_ge(s["x1_made"], j * PC + PC)
                sp.dma_start(x1_dram[bass.ds(j * PT, PT), :].rearrange("(c p) n -> p c n", p=P),
                             x_sb[:, bass.ds(j * PC, PC), :]).then_inc(s["x1_out"], 16)

            x1_rows(0)
            with sp.Fori(1, PAIRS) as j:
                x1_rows(j)
            sp.wait_ge(s["h2_step"], 2 * CH)
            sp.wait_ge(s["x1_out"], 16 * PAIRS)
            sp.dma_start(cst[:], consts).then_inc(s["cst_in"], 16)

            def load_weights(raw, src, rows, base):
                def load(e, r):
                    sp.dma_start(raw[:, bass.ds(e, 1), :, :], src[bass.ds(e, 1), :, :].rearrange("a (k p) n -> p a k n", p=rows)
                                 ).then_inc(s[f"w_in{r}"], 16)

                for r in range(WR):
                    if base:
                        sp.wait_ge(s["gw_hi"], base - WR + r + 1)
                    load(r, r)
                with sp.Fori(1, E // WR) as m:
                    for r in range(WR):
                        sp.wait_ge(s["gw_hi"], m * WR + (base - WR + r + 1))
                        load(m * WR + r, r)

            load_weights(gu_raw, w_gu, P, 0)
            sp.wait_ge(s["tiles_made"], 1)
            sp.wait_ge(s["slots_made"], 1)
            load_weights(dn_raw, w_down, FH, E)
            sp.wait_ge(s["scattered"], 16 * CH * TOPK)

            def load_tile(n, place):
                sp.dma_start(xt[:, place, :], xs_dram[bass.ds(n * P, P), :]).then_inc(s[f"xt_in{place}"], 16)

            def step(t, n, what):
                if "L" in what:
                    wait_from(sp, s["x_turned"], t)
                    load_tile(t + XR - 1, (n + XR - 1) % XR)
                if "D" in what:
                    sp.wait_ge(s["y_made"], t - 1)
                    sp.dma_start(ys_dram[bass.ds((t - 2) * P, P), :], y_sb[:, n % 2, :]).then_inc(s[f"y_out{n % 2}"], 16)

            for n in range(XR - 1):
                load_tile(n, n)
            over_tiles(sp, step)
            for par in range(2):
                sp.wait_ge(s[f"y_out{par}"], 8 * TILES)
            sp.dma_start(gb_sb[:], mod_rows[:, 3 * HID:4 * HID].partition_broadcast(P)).then_inc(s["gb_in"], 16)
            def store_chunk(c):
                sp.wait_ge(s["o_made"], c + 1)
                sp.dma_start(out[c * P:(c + 1) * P, :], o_sb[:, c % RING, :]).then_inc(s[f"o_out{c % RING}"], 16)

            for c in range(CH):
                if c >= RING:
                    sp.wait_ge(s["o_made"], c - RING + 1)
                sp.dma_start(x1_sb[:, c % RING, :], x1_dram[c * P:(c + 1) * P, :]).then_inc(s[f"x1_back{c % RING}"], 16)
                if c >= RING - 1:
                    store_chunk(c - RING + 1)
            for c in range(CH - RING + 1, CH):
                store_chunk(c)
            sp.wait_ge(s["zeroed"], 16)
            for r in range(RING):
                sp.wait_ge(s[f"o_out{r}"], 16 * CH // RING)

        @block.tensor
        def _(pe):
            def product(dst, l_hi, l_lo, r_hi, r_lo, first, last):
                pe.matmul(dst, l_hi, r_hi, start=first, stop=False)
                pe.matmul(dst, l_hi, r_lo, start=False, stop=False)
                return pe.matmul(dst, l_lo, r_hi, start=False, stop=last)

            def columns():
                pe.wait_ge(s["silu_step"], 3)
                pe.wait_ge(s["mod_in0"], 32)
                for m in range(2):
                    for kk in range(KT):
                        for k in range(KT):
                            last = pe.matmul(bank(m)[:, kk * B:(kk + 1) * B], wmod_sb[:, k, m, kk * P:(kk + 1) * P], cs[:, k, 0, :],
                                             start=(k == 0), stop=(k == KT - 1))
                    last.then_inc(s["misc_ready"], 1)

            def gates():
                pe.wait_ge(s["mod_in1"], 32)
                for n in range(2):
                    pe.wait_ge(s["misc_done"], n + 3)
                    for k in range(KT):
                        last = pe.matmul(bank(n)[0:B, :], cs[:, k, 0, :], wmod_sb[:, k, 2 + 2 * n:4 + 2 * n, :].rearrange("p m n -> p (m n)"),
                                         start=(k == 0), stop=(k == KT - 1))
                    last.then_inc(s["misc_ready"], 1)

            def T(j):
                pe.wait_ge(s["xn_ready"], j * PC + PC)
                for k in range(KT):
                    pe.wait_ge(s["misc_done"], job_T(j, k) - 1)
                    for c in range(PC):
                        last = pe.transpose(bank(k)[:, c * P:(c + 1) * P], xn[:, c, k * P:(k + 1) * P], ident[:])
                    last.then_inc(s["misc_ready"], 1)

            def KV(j, c):
                pe.wait_ge(s["hT_lo"], j * KT + KT)
                for v in range(2):
                    pe.wait_ge(s["misc_done"], job_KV(j, c, v) - 1)
                    tok = slice(c * P, (c + 1) * P)
                    for k in range(KT):
                        last = product(bank(v), hT_hi[:, k, tok], hT_lo[:, k, tok], wkv_hi[:, k, v, :], wkv_lo[:, k, v, :],
                                       k == 0, k == KT - 1)
                    last.then_inc(s["misc_ready"], 1)

            def state(j, b):
                pe.wait_ge(s["sk_lo"], j * PC + 2 * (b + 1))
                pe.wait_ge(s["v_lo"], j * PC + 2 * (b + 1))
                pe.wait_ge(s["misc_done"], job_kvT(j, b) - 1)
                for g in range(KVH):
                    gd = slice(g * D, (g + 1) * D)
                    for n in range(2):
                        c = 2 * b + n
                        last = product(bank(0)[:, gd], v_hi[:, c, gd], v_lo[:, c, gd], sk_hi[:, c, gd], sk_lo[:, c, gd],
                                       n == 0, n == 1)
                last.then_inc(s["misc_ready"], 1)
                pe.wait_ge(s["ksum_in"], j * 2 + (b + 1))
                pe.wait_ge(s["misc_done"], job_ks(j, b) - 1)
                for g in range(KVH):
                    last = pe.matmul(bank(1)[:, 2 * g:2 * g + 2], key_sums[:, b, g * D:(g + 1) * D], ones_f[:], start=True, stop=True)
                last.then_inc(s["misc_ready"], 1)

            def fold(j, hp, b):
                pe.wait_ge(s["misc_done"], job_fold(j, hp, b) - 1)
                gd = slice((hp // 2) * D, (hp // 2 + 1) * D)
                w_hi, w_lo = (w[:, 2 * hp:2 * hp + 2, :].rearrange("p h n -> p (h n)") for w in (wo_hi, wo_lo))
                product(bank_fold(hp, b), kvT_hi[:, b, gd], kvT_lo[:, b, gd], w_hi, w_lo, True, True).then_inc(s["misc_ready"], 1)

            def Q(j, h):
                wait_from(pe, s["sq_f"], j * H + (h - 1 if h >= 2 else 0))
                hd = slice(h * D, (h + 1) * D)
                for k in range(KT):
                    last = product(ps_q[:, h % 2, :], wq_hi[:, k, hd], wq_lo[:, k, hd], hT_hi[:, k, :], hT_lo[:, k, :],
                                   k == 0, k == KT - 1)
                last.then_inc(s["q_ready"], 1)

            def heads_out(j, h, b):
                pe.wait_ge(s["sq_lo"], j * H + (h + 1))
                pe.wait_ge(s["misc_done"], job_fold(j, h // 2, b) + 1)
                wait_from(pe, s["acc_done"], j * (3 * H) + (3 * (h - 1) + 2 + b if h else 0))
                if b == 1:
                    wait_from(pe, s["d3_scaled"], j * H + h)
                r_hi, r_lo = (r[:, (h // 2) % 2, b, h % 2, :] for r in (kvwo_hi, kvwo_lo))
                for c in (2 * b, 2 * b + 1):
                    tok = slice(c * P, (c + 1) * P)
                    last = product(ps_d[:, c, 0:W2], sq_hi[:, h % 2, tok], sq_lo[:, h % 2, tok], r_hi, r_lo, True, True)
                last.then_inc(s["d_ready"], 1)

            def pair(j, before, after):
                for h in range(H):
                    if after and h == H - 3:
                        T(j + 1)
                    heads_out(j, h, 0)
                    if h + 2 < H:
                        pe.wait_ge(s["wst_lo"], 4 * ((h + 2) // 4) + 4)
                        Q(j, h + 2)
                    heads_out(j, h, 1)
                    for hp, b in FOLDS_AT[h]:
                        fold(j, hp, b)
                    if after and h == H - 2:
                        KV(j + 1, 0)
                if after:
                    prepare(j + 1)

            def prepare(j):
                KV(j, 1)
                KV(j, 2)
                pe.wait_ge(s["wst_lo"], 2)
                Q(j, 0)
                state(j, 0)
                KV(j, 3)
                pe.wait_ge(s["wst_lo"], 4)
                fold(j, 0, 0)
                Q(j, 1)
                fold(j, 1, 0)
                state(j, 1)
                fold(j, 0, 1)
                fold(j, 1, 1)

            pe.wait_ge(s["ident_in"], 16)
            columns()
            T(0)
            gates()
            pe.wait_ge(s["wkv_lo"], 4)
            pe.wait_ge(s["ones_made"], 1)
            KV(0, 0)
            prepare(0)
            over_pairs(pe, pair)
            pe.wait_ge(s["h2_step"], 2 * CH)
            pe.wait_ge(s["x1_out"], 16 * PAIRS)

            def turn(c):
                if c >= PC:
                    pe.wait_ge(s["h2T_made"], c - PC + 1)
                for k in range(KT):
                    last = pe.transpose(ps_d[:, c % PC, k * P:(k + 1) * P], x_sb[:, c, k * P:(k + 1) * P], ident[:])
                last.then_inc(s["h2_turned"], 1)

            def logits(c):
                pe.wait_ge(s["h2T_made"], c + 1)
                if c >= 2:
                    pe.wait_ge(s["lg_made"], c - 1)
                for k in range(KT):
                    last = pe.matmul(ps_q[:, c % 2, 0:E], h2T[:, c % 2, k, :], router_sb[:, k, :], start=(k == 0), stop=(k == KT - 1))
                last.then_inc(s["logits"], 1)

            pe.wait_ge(s["router_in"], 32)
            turn(0)
            for c in range(1, CH):
                turn(c)
                logits(c - 1)
            logits(CH - 1)
            pe.wait_ge(s["mask_made"], 1)
            for n in range(2):
                last = pe.matmul(ps_d[:, n, 0:CH * E], tri[:, n * P:(n + 1) * P], mask[:].rearrange("p c e -> p (c e)"), start=True, stop=True)
            last.then_inc(s["counted"], 1)

            pe.wait_ge(s["tiles_made"], 1)

            expert_of = {}

            def step(t, place, what):
                par, other = place % 2, 1 - place % 2
                if "X" in what:
                    n, r = t + 1, (place + 1) % XR
                    pe.wait_ge(s[f"xt_in{r}"], n * (16 // XR) + (16 - 16 // XR * r))
                    for k in range(KT):
                        last = pe.transpose(ps_d[:, other, k * P:(k + 1) * P], xt[:, r, k * P:(k + 1) * P], ident[:])
                    last.then_inc(s["x_turned"], 1)
                if "G" in what:
                    e = expert_of[place] = pe.value_load(tile_e[0:1, bass.ds(t, 1)], min_val=0, max_val=E - 1)
                    pe.wait_ge(s["xT_lo"], t + 1)
                    for k in range(KT):
                        r_hi, r_lo = (w[:, bass.ds(e, 1), k, :] for w in (gu_hi, gu_lo))
                        last = product(ps_q[:, par, 0:2 * FF], xT_hi[:, par, k, :], xT_lo[:, par, k, :], r_hi, r_lo, k == 0, k == KT - 1)
                    last.then_inc(s["gu_done"], 1)
                if "A" in what:
                    pe.wait_ge(s["mid_done"], t)
                    for i in range(2):
                        last = pe.transpose(ps_d[0:FH, 2 + other, i * P:(i + 1) * P], mid[:, other, i * FH:(i + 1) * FH], ident[:])
                    last.then_inc(s["m_turned"], 1)
                if "D" in what:
                    e = expert_of[place - 2] if place >= 2 else pe.value_load(tile_e[0:1, bass.ds(t - 2, 1)], min_val=0, max_val=E - 1)
                    pe.wait_ge(s["mT_lo"], t - 1)
                    for i in range(2):
                        r_hi, r_lo = (w[:, bass.ds(e, 1), i, :] for w in (dn_hi, dn_lo))
                        last = product(ps_m[:, par, 0:HID], mT_hi[:, par, i, :], mT_lo[:, par, i, :], r_hi, r_lo, i == 0, i == 1)
                    last.then_inc(s["down_done"], 1)

            pe.wait_ge(s["xt_in0"], 16)
            for k in range(KT):
                last = pe.transpose(ps_d[:, 0, k * P:(k + 1) * P], xt[:, 0, k * P:(k + 1) * P], ident[:])
            last.then_inc(s["x_turned"], 1)
            pe.wait_ge(s["gw_lo"], 2 * E)
            over_tiles(pe, step)

        @block.scalar
        def _(act):
            def copy_hi(dst, src):
                return act.activation(dst, src, ACT.Copy)

            def T(j, first=False):
                for k in range(KT):
                    act.wait_ge(s["misc_done"], job_T(j, k) + 1)
                    if not first:
                        act.wait_ge(s["q_ready"], j * H)
                    copy_hi(hT_hi[:, k, :], vf[:, k, :]).then_inc(s["hT_hi"], 1)

            def KV(j, c, first=False):
                act.wait_ge(s["misc_done"], job_KV(j, c, 0) + 1)
                wait_from(act, s["sk_f"], j * PC + c)
                act.activation(ke[:], kt[:, c % 2, :], ACT.Relu, scale=-1.0).then_inc(s["k_neg"], 1)
                act.wait_ge(s["k_neg"], j * PC + (c + 1))
                act.activation(ke[:], ke[:], ACT.Exp, scale=-1.0).then_inc(s["k_act"], 1)
                act.wait_ge(s["misc_done"], job_KV(j, c, 1) + 1)
                if not first:
                    act.wait_ge(s["misc_ready"], j * JOBS + (18 - JOBS))
                copy_hi(v_hi[:, c, :], vf[:, c % 2, :]).then_inc(s["v_hi"], 1)
                act.wait_ge(s["sk_f"], j * PC + (c + 1))
                copy_hi(sk_hi[:, c, :], kt[:, c % 2, :]).then_inc(s["sk_hi"], 1)

            def state(j, b):
                act.wait_ge(s["misc_ready"], job_kvT(j, b) + 1)
                copy_hi(kvT_hi[:, b, :], bank(0)).then_inc(s["misc_hi"], 1)
                act.wait_ge(s["misc_ready"], job_ks(j, b) + 1)
                copy_hi(ks_hi[:, b, :, :].rearrange("p g n -> p (g n)"), bank(1)[:, 0:2 * KVH]).then_inc(s["misc_hi"], 1)

            def fold(j, hp, b):
                act.wait_ge(s["misc_ready"], job_fold(j, hp, b) + 1)
                wait_from(act, s["d_ready"], j * (2 * H) + (4 * hp - 4 if hp >= 2 else 0))
                copy_hi(kvwo_hi[:, hp % 2, b, :, 0:HID], bank_fold(hp, b).rearrange("p (h n) -> p h n", h=2)).then_inc(s["misc_hi"], 1)

            def elu(j, h):
                act.wait_ge(s["q_ready"], j * H + (h + 1))
                wait_from(act, s["sq_lo"], j * H + (h - 1 if h >= 2 else 0))
                act.activation(qe[:, h % 2, :], ps_q[:, h % 2, :], ACT.Relu, bias=nbq_sb[:, h:h + 1], scale=-1.0).then_inc(s["q_neg"], 1)
                act.wait_ge(s["q_neg"], j * H + (h + 1))
                act.activation(qe[:, h % 2, :], qe[:, h % 2, :], ACT.Exp, scale=-1.0).then_inc(s["q_exp"], 1)

            def hi(j, h):
                act.wait_ge(s["sq_f"], j * H + (h + 1))
                wait_from(act, s["d_ready"], j * (2 * H) + (2 * h - 2 if h >= 2 else 0))
                copy_hi(sq_hi[:, h % 2, :], qe[:, h % 2, :]).then_inc(s["sq_hi"], 1)

            def pair(j, before, after):
                for h in range(H):
                    if h == H - 2:
                        scale3(j, h - 1)
                    if h + 1 < H:
                        hi(j, h + 1)
                    if 1 <= h < H - 2:
                        scale3(j, h - 1)
                    if after and h == H - 3:
                        T(j + 1)
                    if h + 2 < H:
                        elu(j, h + 2)
                    for hp, b in FOLDS_AT[h]:
                        fold(j, hp, b)
                    if not before and h < 8:
                        piece_hi(8 + h)
                    if h == H - 2:
                        scale3(j, h)
                    if after and h == H - 2:
                        KV(j + 1, 0)
                scale3(j, H - 1)
                if after:
                    prepare(j + 1)

            def scale3(j, h):
                act.wait_ge(s["rn_step"], j * (4 * H) + (4 * h + 4))
                if h == 0:
                    wait_from(act, s["x1_made"], j * PC)
                elif h >= 3:
                    act.wait_ge(s["acc3_done"], j * (H - 1) + (h - 2))
                act.activation(acc[:, 3, :] if h == 0 else d3[:, h % 2, :], ps_d[:, 3, 0:HID], ACT.Copy,
                               scale=rn[:, 1, 1:2]).then_inc(s["d3_scaled"], 1)

            def piece_hi(n):
                act.wait_ge(s[f"wst_in{n % 2}"], 16 * (n // 2 + 1))
                copy_hi(piece_of(n, wq_hi, wo_hi), wst[:, n % 2, :]).then_inc(s["wst_hi"], 1)

            def prepare(j, first=False):
                for c in range(1, PC):
                    if first:
                        piece_hi(2 * c - 2)
                        piece_hi(2 * c - 1)
                    KV(j, c, first)
                    if c == 2:
                        elu(j, 0)
                        state(j, 0)
                        hi(j, 0)
                if first:
                    piece_hi(6)
                    piece_hi(7)
                fold(j, 0, 0)
                elu(j, 1)
                fold(j, 1, 0)
                state(j, 1)
                fold(j, 0, 1)
                fold(j, 1, 1)

            act.wait_ge(s["c_in"], 32)
            act.activation(cs[:, :, 1, :], cs[:, :, 0, :], ACT.Exp, scale=-1.0).then_inc(s["silu_exp"], 1)
            for n in range(4):
                act.wait_ge(s["wkv_in"], 64)
                copy_hi(wkv_hi[:, n % 2, n // 2, :], wkv_raw[n]).then_inc(s["wkv_hi"], 1)
            T(0, first=True)
            act.wait_ge(s["bias_in"], 32)
            act.activation(nbq_sb[:], bq_sb[:], ACT.Copy, scale=-1.0).then_inc(s["nbq"], 1)
            act.wait_ge(s["nbq"], 1)
            KV(0, 0, first=True)
            prepare(0, first=True)
            over_pairs(act, pair)
            for c in range(CH):
                act.wait_ge(s["h2_turned"], c + 1)
                if c >= 2:
                    act.wait_ge(s["logits"], c - 1)
                act.activation(h2T[:, c % 2, :, :].rearrange("p k n -> p (k n)"), ps_d[:, c % PC, 0:HID], ACT.Copy).then_inc(s["h2T_made"], 1)
            act.wait_ge(s["gap_made"], 1)
            act.activation(weight[:], gap[:], ACT.Exp).then_inc(s["exp_done"], 1)

            for i, (hi, raw) in enumerate(((gu_hi, gu_raw), (dn_hi, dn_raw))):
                with act.Fori(0, E // WR) as m:
                    for r in range(WR):
                        e = bass.ds(m * WR + r, 1)
                        act.wait_ge(s[f"w_in{r}"], m * 16 + (16 * (E // WR) * i + 16))
                        copy_hi(hi[:, e, :, :], raw[:, e, :, :]).then_inc(s["gw_hi"], 1)

            def x_hi(n, q):
                act.wait_ge(s["x_turned"], n + 1)
                if not (isinstance(n, int) and n < 2):
                    act.wait_ge(s["gu_done"], n - 1)
                copy_hi(xT_hi[:, q, :, :].rearrange("p k n -> p (k n)"), ps_d[:, q, 0:HID]).then_inc(s["xT_hi"], 1)

            def step(t, par, what):
                par %= 2
                if "X" in what:
                    x_hi(t + 1, 1 - par)
                if "G" in what:
                    act.wait_ge(s["gu_done"], t + 1)
                    act.activation(silu[:, par, :], ps_q[:, par, 0:FF], ACT.Silu).then_inc(s["silu_done"], 1)
                if "A" in what:
                    n, q = t - 1, 1 - par
                    act.wait_ge(s["m_turned"], n + 1)
                    if not (isinstance(n, int) and n < 2):
                        act.wait_ge(s["down_done"], n - 1)
                    copy_hi(mT_hi[:, q, :, :].rearrange("p i n -> p (i n)"), ps_d[0:FH, 2 + q, 0:2 * P]).then_inc(s["mT_hi"], 1)
                if "D" in what:
                    n = t - 2
                    act.wait_ge(s["down_done"], n + 1)
                    if not (isinstance(n, int) and n < 2):
                        act.wait_ge(s[f"y_out{par}"], n * 8 - 8 * par)
                    act.activation(y_sb[:, par, :], ps_m[:, par, 0:HID], ACT.Copy).then_inc(s["y_made"], 1)

            x_hi(0, 0)
            over_tiles(act, step)

        @block.vector
        def _(dve):
            def split(dst, src, hi):
                return dve.tensor_tensor(dst, src, hi.bitcast(F32), ALU.subtract)

            def silu_c():
                dve.wait_ge(s["silu_exp"], 1)
                dve.tensor_scalar(cs[:, :, 2, :], cs[:, :, 1, :], 1.0, None, ALU.add).then_inc(s["silu_step"], 1)
                dve.wait_ge(s["silu_step"], 1)
                dve.reciprocal(cs[:, :, 3, :], cs[:, :, 2, :]).then_inc(s["silu_step"], 1)
                dve.wait_ge(s["silu_step"], 2)
                dve.tensor_tensor(cs[:, :, 0, :], cs[:, :, 0, :], cs[:, :, 3, :], ALU.mult).then_inc(s["silu_step"], 1)

            def columns():
                for m, dst in enumerate((sa_col, ca_col)):
                    dve.wait_ge(s["misc_ready"], m + 1)
                    dve.tensor_scalar(dst[:].rearrange("p k b -> p (k b)"), bank(m)[:, 0:KT * B], float(m), None,
                                      ALU.add).then_inc(s["misc_done"], 1)
                dve.wait_ge(s["misc_done"], 2)

            def gates_read():
                for n in range(2):
                    dve.wait_ge(s["misc_ready"], n + 5)
                    dve.tensor_copy(gate_rows[:, 2 * n * HID:(2 * n + 2) * HID], bank(n)[0:B, :]).then_inc(s["misc_done"], 1)

            def gates_made():
                dve.wait_ge(s["misc_done"], 6)
                step = 0
                tmp = qe[0:B].rearrange("p a n -> p (a n)")
                for m in (0, 3):
                    g, sign, size = gate_rows[:, m * HID:(m + 1) * HID], tmp[:, 0:HID], tmp[:, HID:2 * HID]
                    dve.tensor_scalar(sign, g, 0.0, 2.0, ALU.is_ge, ALU.mult).then_inc(s["gate_step"], 1)
                    dve.scalar_tensor_tensor(size, g, -1.0, g, ALU.mult, ALU.max).then_inc(s["gate_step"], 1)
                    dve.wait_ge(s["gate_step"], step + 2)
                    dve.tensor_scalar(sign, sign, -1.0, None, ALU.add).then_inc(s["gate_step"], 1)
                    dve.wait_ge(s["gate_step"], step + 3)
                    dve.scalar_tensor_tensor(g, size, 0.25, sign, ALU.max, ALU.mult).then_inc(s["gate_step"], 1)
                    step += 4
                    dve.wait_ge(s["gate_step"], step)
                cb = gate_rows[:, 2 * HID:3 * HID]
                dve.tensor_scalar(cb, cb, 1.0, None, ALU.add).then_inc(s["gates"], 1)

            def moments(src, n, step, base):
                for c in range(n):
                    dve.bn_stats(stats[:, c, :], src(c)).then_inc(step, 1)
                wait_apart(dve, step, base + n)
                for c in range(n):
                    dve.bn_aggr(mv[:, c, :], stats[:, c, :]).then_inc(step, 1)
                dve.wait_ge(step, base + 2 * n)
                dve.tensor_scalar(ve[:, 0:n], mv[:, 0:n, 1], LN_EPS, None, ALU.add).then_inc(step, 1)

            def ln1_moments(j):
                dve.wait_ge(s["x_in0"], 16)
                if not (isinstance(j, int) and j == 0):
                    dve.wait_ge(s["x_in"], 16 * (PAIRS - 1))
                moments(lambda c: x_sb[:, bass.ds(j * PC + c, 1), :], PC, s["ln1_step"], j * (2 * PC + 1))

            def ln1_rows(j):
                dve.wait_ge(s["ln1_rstd"], j + 1)
                for c in range(PC):
                    dve.tensor_scalar(xn[:, c:c + 1, :], x_sb[:, bass.ds(j * PC + c, 1), :], mv[:, c, 0:1], rstd[:, c:c + 1],
                                      ALU.subtract, ALU.mult).then_inc(s["xn_ready"], 1)

            def T_turned(j):
                for k in range(KT):
                    dve.wait_ge(s["misc_ready"], job_T(j, k) + 1)
                    for b in range(2):
                        col = bass.ds(j * 2 + b, 1)
                        tok = slice(b * S, (b + 1) * S)
                        last = dve.tensor_scalar(vf[:, k, tok], bank(k)[:, tok], ca_col[:, k, col], sa_col[:, k, col], ALU.mult, ALU.add)
                    last.then_inc(s["misc_done"], 1)

            def T_lo(j):
                for k in range(KT):
                    dve.wait_ge(s["hT_hi"], j * KT + (k + 1))
                    split(hT_lo[:, k, :], vf[:, k, :], hT_hi[:, k, :]).then_inc(s["hT_lo"], 1)

            def KV_bias(j, c):
                for v, dst in enumerate((kt, vf)):
                    if c == 2 and v == 0:
                        dve.wait_ge(s["ksum_in"], j * 2 + 1)
                    dve.wait_ge(s["misc_ready"], job_KV(j, c, v) + 1)
                    if v == 1 and c >= 2 and not (isinstance(j, int) and j == 0):
                        dve.wait_ge(s["v_lo"], j * PC + (c - 1))
                    dve.tensor_tensor(dst[:, c % 2, :], bank(v), bkv_sb[:, v, :], ALU.add).then_inc(s["misc_done"], 1)

            def KV_elu(j, c):
                dve.wait_ge(s["k_act"], j * PC + (c + 1))
                dve.scalar_tensor_tensor(kt[:, c % 2, :], kt[:, c % 2, :], 1.0, ke[:], ALU.add, ALU.max).then_inc(s["sk_f"], 1)

            def KV_lo(j, c):
                if isinstance(j, int) and j == 0:
                    dve.wait_ge(s["v_hi"], j * PC + (c + 1))
                    split(v_lo[:, c, :], vf[:, c % 2, :], v_hi[:, c, :]).then_inc(s["v_lo"], 1)
                dve.wait_ge(s["sk_hi"], j * PC + (c + 1))
                split(sk_lo[:, c, :], kt[:, c % 2, :], sk_hi[:, c, :]).then_inc(s["sk_lo"], 1)

            def state(j, b):
                dve.wait_ge(s["misc_hi"], hi_kvT(j, b) + 1)
                split(kvT_lo[:, b, :], bank(0), kvT_hi[:, b, :]).then_inc(s["misc_done"], 1)
                dve.wait_ge(s["misc_hi"], hi_ks(j, b) + 1)
                split(ks_lo[:, b, :, :].rearrange("p g n -> p (g n)"), bank(1)[:, 0:2 * KVH],
                      ks_hi[:, b, :, :].rearrange("p g n -> p (g n)")).then_inc(s["misc_done"], 1)
                dve.wait_ge(s["misc_done"], job_ks(j, b) + 1)

            def fold(j, hp, b):
                dve.wait_ge(s["misc_hi"], hi_fold(j, hp, b) + 1)
                for src, dst in ((ks_hi, kvwo_hi), (ks_lo, kvwo_lo)):
                    dve.tensor_copy(dst[:, hp % 2, b, :, HID:W2], src[:, b, hp // 2:hp // 2 + 1, :].broadcast_to([P, 2, 2]))
                split(kvwo_lo[:, hp % 2, b, :, 0:HID], bank_fold(hp, b).rearrange("p (h n) -> p h n", h=2),
                      kvwo_hi[:, hp % 2, b, :, 0:HID]).then_inc(s["misc_done"], 1)

            def elu(j, h):
                dve.wait_ge(s["q_exp"], j * H + (h + 1))
                dve.scalar_tensor_tensor(qe[:, h % 2, :], ps_q[:, h % 2, :], bq1_sb[:, h:h + 1], qe[:, h % 2, :], ALU.add, ALU.max
                                         ).then_inc(s["sq_f"], 1)

            def heads_out(j, h, b):
                dve.wait_ge(s["d_ready"], j * (2 * H) + (2 * h + b + 1))
                n = 4 * h + 2 * b
                dve.tensor_scalar(rr[:, b, :], ps_d[:, 2 * b:2 * b + 2, HID], NORM_EPS, None, ALU.add).then_inc(s["rn_step"], 1)
                dve.wait_ge(s["rn_step"], j * (4 * H) + (n + 1))
                dve.reciprocal(rn[:, b, :], rr[:, b, :]).then_inc(s["rn_step"], 1)
                dve.wait_ge(s["rn_step"], j * (4 * H) + (n + 2))
                for i in range(2 - b):
                    c = 2 * b + i
                    if h == 0:
                        wait_from(dve, s["x1_made"], j * PC)
                        dve.tensor_scalar(acc[:, c, :], ps_d[:, c, 0:HID], rn[:, b, i:i + 1], None, ALU.mult).then_inc(s["acc_done"], 1)
                    else:
                        dve.wait_ge(s["acc_done"], j * (3 * H) + (3 * (h - 1) + c + 1))
                        dve.scalar_tensor_tensor(acc[:, c, :], ps_d[:, c, 0:HID], rn[:, b, i:i + 1], acc[:, c, :],
                                                 ALU.mult, ALU.add).then_inc(s["acc_done"], 1)

            def ln2_moments(j):
                dve.wait_ge(s["x1_made"], j * PC + PC)
                moments(lambda c: x_sb[:, bass.ds(j * PC + c, 1), :], PC, s["ln2_step"], j * (2 * PC + 1))

            def ln2_rows(j):
                dve.wait_ge(s["ln2_rstd"], j + 1)
                dve.wait_ge(s["x1_out"], j * 16 + 16)
                for c in range(PC):
                    x = x_sb[:, bass.ds(j * PC + c, 1), :]
                    dve.tensor_scalar(x, x, mv[:, c, 0:1], rstd[:, c:c + 1], ALU.subtract, ALU.mult).then_inc(s["h2_n"], 1)

            def pair(j, before, after):
                for h in range(H):
                    if after and h == H - 3:
                        T_turned(j + 1)
                    heads_out(j, h, 0)
                    if h % 2 == 1 and h != H - 3:
                        for hp, b in FOLDS_AT[h - 1]:
                            fold(j, hp, b)
                    heads_out(j, h, 1)
                    if after and h == H - 3:
                        T_lo(j + 1)
                    if h + 2 < H:
                        elu(j, h + 2)
                    if h % 2 == 1 or h == H - 4:
                        for hp, b in FOLDS_AT[h]:
                            fold(j, hp, b)
                    if before and h == 1:
                        ln2_moments(j - 1)
                    if before and h == 3:
                        ln2_rows(j - 1)
                    if after and h == 8:
                        ln1_moments(j + 1)
                    if after and h == 11:
                        ln1_rows(j + 1)
                    if after and h == H - 2:
                        KV_bias(j + 1, 0)
                        KV_elu(j + 1, 0)
                if after:
                    prepare(j + 1)
                else:
                    ln2_moments(j)
                    ln2_rows(j)

            def prepare(j):
                KV_lo(j, 0)
                for c in (1, 2):
                    KV_bias(j, c)
                    KV_elu(j, c)
                    KV_lo(j, c)
                elu(j, 0)
                state(j, 0)
                KV_bias(j, 3)
                KV_elu(j, 3)
                fold(j, 0, 0)
                KV_lo(j, 3)
                elu(j, 1)
                fold(j, 1, 0)
                state(j, 1)
                fold(j, 0, 1)
                fold(j, 1, 1)

            dve.memset(ones_f[:], 1.0).then_inc(s["ones_made"], 1)
            silu_c()
            ln1_moments(0)
            ln1_rows(0)
            columns()
            T_turned(0)
            for n in range(4):
                dve.wait_ge(s["wkv_hi"], n + 1)
                split(wkv_lo[:, n % 2, n // 2, :], wkv_raw[n], wkv_hi[:, n % 2, n // 2, :]).then_inc(s["wkv_lo"], 1)
            T_lo(0)
            gates_read()
            dve.wait_ge(s["bias_in"], 32)
            dve.tensor_scalar(bq1_sb[:], bq_sb[:], 1.0, None, ALU.add).then_inc(s["bq1"], 1)
            KV_bias(0, 0)
            KV_elu(0, 0)
            gates_made()
            dve.wait_ge(s["bq1"], 1)
            prepare(0)
            over_pairs(dve, pair)
            steps_done = [0]

            def then(ins):
                ins.then_inc(s["route_step"], 1)
                steps_done[0] += 1
                dve.wait_ge(s["route_step"], steps_done[0])

            iota_row, tile_row = cst[:, C_IOTA:C_IOTA + E], cst[0:1, C_TILE:C_TILE + TILES]
            flat = lambda t: t.rearrange("p c k -> p (c k)")
            dve.wait_ge(s["cst_in"], 16)
            dve.wait_ge(s["router_in"], 32)
            dve.wait_ge(s["h2_step"], 2 * CH)
            dve.wait_ge(s["x1_out"], 16 * PAIRS)
            dve.tensor_copy(tri[:], cst[:, C_TRI:C_TRI + 2 * P])
            dve.memset(cum[:, 0, :], 0.0)
            for c in range(CH):
                dve.wait_ge(s["logits"], c + 1)
                dve.tensor_tensor(lg[:, c, :], ps_q[:, c % 2, 0:E], ebias_sb[:], ALU.add).then_inc(s["lg_made"], 1)
            dve.wait_ge(s["lg_made"], CH)
            for c in range(CH):
                last = dve.max(top8[:, c, :], lg[:, c, :])
            then(last)
            for c in range(CH):
                last = dve.max_index(arg8[:, c, :], top8[:, c, :], lg[:, c, :])
            dve.tensor_tensor(gap[:], top8[:, :, 0:TOPK], top8[:, :, 0:1].broadcast_to([P, CH, TOPK]), ALU.subtract).then_inc(s["gap_made"], 1)
            then(last)
            then(dve.tensor_copy(arg_f[:], arg8[:, :, 0:TOPK]))
            hot_n = hot[:].rearrange("p c k e -> p (c k) e")
            then(dve.tensor_tensor(hot_n, flat(arg_f[:]).unsqueeze(2).broadcast_to([P, CH * TOPK, E]),
                                   iota_row.unsqueeze(1).broadcast_to([P, CH * TOPK, E]), ALU.is_equal))
            then(dve.tensor_reduce(pos[:], hot[:].rearrange("p c k e -> p c e k"), AX_X, ALU.add))
            dve.tensor_copy(mask[:], pos[:]).then_inc(s["mask_made"], 1)
            dve.wait_ge(s["exp_done"], 1)
            then(dve.tensor_reduce(wsum[:], weight[:], AX_X, ALU.add))
            then(dve.reciprocal(wrec[:], wsum[:]))
            then(dve.tensor_tensor(wgt[:], weight[:], wrec[:].unsqueeze(2).broadcast_to([P, CH, TOPK]), ALU.mult))
            dve.wait_ge(s["counted"], 1)
            for c in range(CH):
                then(dve.tensor_tensor(cum[:, c + 1, :], cum[:, c, :], ps_d[:, 1, c * E:(c + 1) * E], ALU.add))
            then(dve.tensor_scalar(steps[:], iota_row, float(P), None, ALU.mult))
            then(dve.tensor_tensor(cmp[:], cum[:, CH, :].unsqueeze(2).broadcast_to([P, E, E]), steps[:].unsqueeze(1).broadcast_to([P, E, E]), ALU.is_gt))
            then(dve.tensor_reduce(ntile[:], cmp[:], AX_X, ALU.add))
            low = cst[:, C_LOW:C_LOW + E * E].rearrange("p (a b) -> p a b", b=E)
            then(dve.tensor_tensor(cmp[:], low, ntile[:].unsqueeze(1).broadcast_to([P, E, E]), ALU.mult))
            then(dve.tensor_reduce(start[:], cmp[:], AX_X, ALU.add))
            then(dve.tensor_scalar(start_slot[:], start[:], float(P), None, ALU.mult))
            then(dve.tensor_tensor(pos[:], ps_d[:, 0, 0:CH * E].rearrange("p (c e) -> p c e", e=E), cum[:, 0:CH, :], ALU.add))
            then(dve.tensor_tensor(pos[:], pos[:], start_slot[:].unsqueeze(1).broadcast_to([P, CH, E]), ALU.add))
            then(dve.tensor_tensor(hot[:], hot[:], pos[:].unsqueeze(2).broadcast_to([P, CH, TOPK, E]), ALU.mult))
            then(dve.tensor_reduce(flat(arg_f[:]), hot_n, AX_X, ALU.add))
            dve.tensor_copy(slot_i[:], arg_f[:]).then_inc(s["slots_made"], 1)
            then(dve.tensor_tensor(tcmp[:], start[0:1, :].unsqueeze(1).broadcast_to([1, TILES, E]), tile_row.unsqueeze(2).broadcast_to([1, TILES, E]), ALU.is_le))
            then(dve.tensor_reduce(tsum[:], tcmp[:], AX_X, ALU.add))
            dve.tensor_scalar(tile_e[:], tsum[:], -1.0, None, ALU.add).then_inc(s["tiles_made"], 1)
            dve.wait_ge(s["tiles_made"], 1)

            for i, (lo, raw, hi) in enumerate(((gu_lo, gu_raw, gu_hi), (dn_lo, dn_raw, dn_hi))):
                with dve.Fori(0, E) as m:
                    e = bass.ds(m, 1)
                    dve.wait_ge(s["gw_hi"], m + (E * i + 1))
                    split(lo[:, e, :, :], raw[:, e, :, :], hi[:, e, :, :]).then_inc(s["gw_lo"], 1)

            def x_lo(n, q):
                dve.wait_ge(s["xT_hi"], n + 1)
                split(xT_lo[:, q, :, :].rearrange("p k n -> p (k n)"), ps_d[:, q, 0:HID],
                      xT_hi[:, q, :, :].rearrange("p k n -> p (k n)")).then_inc(s["xT_lo"], 1)

            def step(t, par, what):
                par %= 2
                if "X" in what:
                    x_lo(t + 1, 1 - par)
                if "G" in what:
                    dve.wait_ge(s["silu_done"], t + 1)
                    if not (isinstance(t, int) and t < 2):
                        dve.wait_ge(s["m_turned"], t - 1)
                    dve.tensor_tensor(mid[:, par, :], silu[:, par, :], ps_q[:, par, FF:2 * FF], ALU.mult).then_inc(s["mid_done"], 1)
                if "A" in what:
                    n, q = t - 1, 1 - par
                    dve.wait_ge(s["mT_hi"], n + 1)
                    split(mT_lo[:, q, :, :].rearrange("p i n -> p (i n)"), ps_d[0:FH, 2 + q, 0:2 * P],
                          mT_hi[:, q, :, :].rearrange("p i n -> p (i n)")).then_inc(s["mT_lo"], 1)

            x_lo(0, 0)
            over_tiles(dve, step)

            dve.wait_ge(s["gb_in"], 16)
            for c in range(CH):
                r, o = c % RING, o_sb[:, c % RING, :]
                dve.wait_ge(s[f"gathered{r}"], 16 * TOPK * (c // RING + 1))
                if c >= RING:
                    dve.wait_ge(s[f"o_out{r}"], 16 * (c // RING))
                then(dve.tensor_scalar(o, yg[:, r, 0, :], wgt[:, c, 0:1], None, ALU.mult))
                for k in range(1, TOPK):
                    then(dve.scalar_tensor_tensor(o, yg[:, r, k, :], wgt[:, c, k:k + 1], o, ALU.mult, ALU.add))
                then(dve.tensor_tensor(o, o, gb_sb[:, c * P // S, :], ALU.mult))
                dve.wait_ge(s[f"x1_back{r}"], 16 * (c // RING + 1))
                dve.tensor_tensor(o, o, x1_sb[:, r, :], ALU.add).then_inc(s["o_made"], 1)

        @block.gpsimd
        def _(pool):
            def inverse_root(n, counter):
                pool.tensor_tensor(rstd[:, 0:n], ve[:, 0:n], half[:, 0:n], ALU.pow).then_inc(counter, 1)

            pool.memset(half[:], -0.5).then_inc(s["half_made"], 1)
            pool.memset(zero[:], 0.0).then_inc(s["zero_made"], 1)
            pool.wait_ge(s["half_made"], 1)
            pool.wait_ge(s["ln1_step"], 2 * PC + 1)
            inverse_root(PC, s["ln1_rstd"])
            def piece_lo(n):
                pool.wait_ge(s["wst_hi"], n + 1)
                pool.tensor_tensor(piece_of(n, wq_lo, wo_lo), wst[:, n % 2, :], piece_of(n, wq_hi, wo_hi).bitcast(F32), ALU.subtract
                                   ).then_inc(s["wst_lo"], 1)

            def key_sum(j, b):
                pool.wait_ge(s["sk_f"], j * PC + 2 * (b + 1))
                pool.tensor_tensor(key_sums[:, b, :], kt[:, 0, :], kt[:, 1, :], ALU.add).then_inc(s["ksum_in"], 1)

            def lo(j, h):
                pool.wait_ge(s["sq_hi"], j * H + (h + 1))
                pool.tensor_tensor(sq_lo[:, h % 2, :], qe[:, h % 2, :], sq_hi[:, h % 2, :].bitcast(F32), ALU.subtract).then_inc(s["sq_lo"], 1)

            def add3(j, h):
                pool.wait_ge(s["d3_scaled"], j * H + (h + 1))
                if h >= 2:
                    pool.wait_ge(s["acc3_done"], j * (H - 1) + (h - 1))
                pool.tensor_tensor(acc[:, 3, :], acc[:, 3, :], d3[:, h % 2, :], ALU.add).then_inc(s["acc3_done"], 1)

            def v_lo_of(j, c):
                pool.wait_ge(s["v_hi"], j * PC + (c + 1))
                pool.tensor_tensor(v_lo[:, c, :], vf[:, c % 2, :], v_hi[:, c, :].bitcast(F32), ALU.subtract).then_inc(s["v_lo"], 1)

            def x1(j, c):
                if c == 0:
                    pool.wait_ge(s["ga_in"], j * 16 + 16)
                    pool.wait_ge(s["acc_done"], j * (3 * H) + 3 * H)
                if c == 3:
                    pool.wait_ge(s["acc3_done"], j * (H - 1) + (H - 1))
                x = x_sb[:, bass.ds(j * PC + c, 1), :]
                pool.tensor_tensor(acc[:, c, :], acc[:, c, :], ga_rows[:, c // 2, :], ALU.mult).then_inc(s["x1_step"], 1)
                wait_apart(pool, s["x1_step"], j * PC + (c + 1))
                pool.tensor_tensor(x, acc[:, c:c + 1, :], x, ALU.add).then_inc(s["x1_made"], 1)

            def h2(j, c):
                x = x_sb[:, bass.ds(j * PC + c, 1), :]
                if c == 0:
                    pool.wait_ge(s["rows_in"], j * 16 + 16)
                wait_apart(pool, s["h2_n"], j * PC + (c + 1))
                pool.tensor_tensor(x, x, rows[:, c // 2, 1:2, :], ALU.mult).then_inc(s["h2_step"], 1)
                wait_apart(pool, s["h2_step"], j * (2 * PC) + (2 * c + 1))
                pool.tensor_tensor(x, x, rows[:, c // 2, 0:1, :], ALU.add).then_inc(s["h2_step"], 1)

            def ln2_rstd(j):
                pool.wait_ge(s["ln2_step"], j * (2 * PC + 1) + (2 * PC + 1))
                inverse_root(PC, s["ln2_rstd"])

            def pair(j, before, after):
                for h in range(H):
                    if h + 1 < H:
                        lo(j, h + 1)
                    if h >= 2:
                        add3(j, h - 1)
                    if not before and h < 8:
                        piece_lo(8 + h)
                    if before and h == 1:
                        ln2_rstd(j - 1)
                    if before and 4 <= h < 4 + PC:
                        h2(j - 1, h - 4)
                    if after and h == 9:
                        pool.wait_ge(s["ln1_step"], j * (2 * PC + 1) + 2 * (2 * PC + 1))
                        inverse_root(PC, s["ln1_rstd"])
                    if after and h == H - 1:
                        v_lo_of(j + 1, 0)
                add3(j, H - 1)
                if after:
                    key_sum(j + 1, 0)
                    v_lo_of(j + 1, 1)
                    x1(j, 0)
                    v_lo_of(j + 1, 2)
                    x1(j, 1)
                    v_lo_of(j + 1, 3)
                    key_sum(j + 1, 1)
                    lo(j + 1, 0)
                    for c in (2, 3):
                        x1(j, c)
                else:
                    for c in range(PC):
                        x1(j, c)
                    ln2_rstd(j)
                    for c in range(PC):
                        h2(j, c)

            for n in range(8):
                piece_lo(n)
                if n == 3:
                    key_sum(0, 0)
                if n == 5:
                    key_sum(0, 1)
                    lo(0, 0)
            over_pairs(pool, pair)
            pool.wait_ge(s["zeroed"], 16)
            pool.wait_ge(s["slots_made"], 1)
            for c in range(CH):
                for k in range(TOPK):
                    pool.indirect_dma_start(xs_dram, bass.IndirectOffsetOnAxis(slot_i[:, c, k:k + 1], 0), x_sb[:, c, :], None
                                            ).then_inc(s["scattered"], 16)
            for par in range(2):
                pool.wait_ge(s[f"y_out{par}"], 8 * TILES)
            for c in range(CH):
                if c >= RING:
                    pool.wait_ge(s["o_made"], c - RING + 1)
                for k in range(TOPK):
                    pool.indirect_dma_start(yg[:, c % RING, k, :], None, ys_dram, bass.IndirectOffsetOnAxis(slot_i[:, c, k:k + 1], 0)
                                            ).then_inc(s[f"gathered{c % RING}"], 16)


def kernel(**inputs):
    import numpy as np
    import concourse.bacc as bacc
    from concourse.bass_utils import run_bass_kernel_spmd

    a = {n.removeprefix("L0_").removeprefix("attn_").removeprefix("ffn_"): np.asarray(v) for n, v in inputs.items()}
    laid = {
        "x_in": a["hidden_states"].reshape(TOK, HID),
        "wqT": a["Wq"].T,
        "wkvT": np.concatenate([a["Wk"].T, a["Wv"].T], axis=1),
        "woT": a["Wo"].T.reshape(H, D, HID).transpose(1, 0, 2).reshape(D, H * HID),
        "bqT": a["bq"].reshape(H, D).T,
        "bkv": np.concatenate([a["bk"], a["bv"]]),
        "routerT": a["router_w"].T,
        "ebias": a["expert_bias"],
        "w_gu": np.concatenate([a["gate_proj"], a["up_proj"]], axis=2),
        "w_down": a["down_proj"],
        "cT": a["c"].T,
        "wmod": a["wmod"],
        "consts": constants(),
    }
    nc = bacc.Bacc("TRN2", target_bir_lowering=False, num_devices=1)
    arrays, args = {}, []
    for name, v in laid.items():
        arrays[name] = np.ascontiguousarray(v)
        args.append(nc.dram_tensor(name, v.shape, mybir.dt.from_np(v.dtype), kind="ExternalInput").ap())
    args.append(nc.dram_tensor("out", (TOK, HID), F32, kind="ExternalOutput").ap())
    adaln_block(nc, *args)
    r = run_bass_kernel_spmd(nc, [arrays], core_ids=[0])
    return r.results[0]["out"].reshape(B, S, HID)
```

```python
from contextlib import ExitStack

import concourse.bass as bass
from concourse import mybir

P = 128
F32 = mybir.dt.float32
F32R = mybir.dt.float32r
BF16 = mybir.dt.bfloat16
I32 = mybir.dt.int32
U32 = mybir.dt.uint32
ALU = mybir.AluOpType
ACT = mybir.ActivationFunctionType
AX_X = mybir.AxisListType.X

B, S, HID = 8, 256, 256
H, KVH, D = 16, 4, 128
GROUPS = H // KVH
KT = HID // P
TOK = B * S
CH = TOK // P
PAIRS = B // 2
PC = CH // PAIRS
PT = PC * P
E, TOPK, FF = 16, 4, 224
FH = FF // 2
LN_EPS, NORM_EPS = 1e-5, 1e-6
TILES = (TOK * TOPK + E * (P - 1)) // P
UNROLL = 8
TILES += -TILES % UNROLL
LO_BETWEEN, LO_POOL = 6, 11
EXPERT_ROWS = TOK + P
SLOTS = E * EXPERT_ROWS
W2 = HID + 2
XR = 4
RING = 4
ROUTING_AT = 153 * 1024
STAGE = 512


def constants():
    import numpy as np
    eye = np.eye(P)
    iota = np.tile(np.arange(E), (P, 1))
    first_row = np.tile(np.arange(E) * EXPERT_ROWS, (P, 1))
    low = np.tile((np.arange(E)[None, :] < np.arange(E)[:, None]).reshape(1, E * E), (P, 1))
    before = np.arange(P)[:, None] < np.arange(P)[None, :]
    tiles = np.tile(np.arange(TILES), (P, 1))
    return np.concatenate([eye, iota, first_row, low, before, np.ones((P, P)), tiles], axis=1).astype(np.float32)


C_EYE, C_IOTA, C_FIRST, C_LOW = 0, P, P + E, P + 2 * E
C_TRI = C_LOW + E * E
C_TILE = C_TRI + 2 * P
C_END = C_TILE + TILES


def adaln_block(nc, x_in, wqT, wkvT, woT, bqT, bkv, routerT, ebias, w_gu, w_down, cT, wmod, consts, out):
    mod_rows = nc.dram_tensor("mod_rows", (B, 4 * HID), F32).ap()
    x1_dram = nc.dram_tensor("x1_dram", (TOK, HID), F32).ap()
    xs_dram = nc.dram_tensor("xs_dram", (SLOTS, HID), F32).ap()
    ys_dram = nc.dram_tensor("ys_dram", (TILES * P, HID), F32).ap()

    with ExitStack() as ctx:
        keep = lambda name, shape, dt=F32: ctx.enter_context(nc.sbuf_tensor(name, shape, dt))
        ps_q = ctx.enter_context(nc.psum_tensor("ps_q", [P, 2, 512], F32))
        ps_d = ctx.enter_context(nc.psum_tensor("ps_d", [P, PC, 512], F32))
        ps_m = ctx.enter_context(nc.psum_tensor("ps_m", [P, 2, 512], F32))

        ident = keep("ident", [P, P])
        wgt = keep("wgt", [P, CH, TOPK])
        in_row = keep("in_row", [P, CH, TOPK])
        slot_i = keep("slot_i", [P, CH, TOPK], I32)
        pair_slots = keep("pair_slots", [P, PC, TOPK], I32)
        tile_e = keep("tile_e", [1, TILES], I32)
        tile_row = keep("tile_row", [1, TILES], I32)
        end_row = keep("end_row", [1, E], I32)
        ebias_sb = keep("ebias_sb", [P, E])
        router_sb = keep("router_sb", [P, KT, E])
        iota_first = keep("iota_first", [P, 2, E])
        lg = keep("lg", [P, PC, E])
        pos = keep("pos", [P, PC, E])
        cum = keep("cum", [P, E])
        top8 = keep("top8", [P, PC, 8])
        arg8 = keep("arg8", [P, PC, 8], U32)
        arg_f, gap, weight = (keep(n, [P, PC, TOPK]) for n in ("arg_f", "gap", "weight"))
        wsum, wrec = (keep(n, [P, PC]) for n in ("wsum", "wrec"))
        mask = keep("mask", [P, PC, E], BF16)
        tri = keep("tri", [P, 2 * P], BF16)
        carry_v, carry_g = keep("carry_v", [P, 8]), keep("carry_g", [P, 8])
        half = keep("half", [P, PC])
        stats = keep("stats", [P, PC, 6])
        mv = keep("mv", [P, PC, 2])
        ve = keep("ve", [P, PC])
        rstd = keep("rstd", [P, PC])
        rr = keep("rr", [P, 2, 2])
        rn = keep("rn", [P, 2, 2])

        with ExitStack() as attn:
            sb = lambda name, shape, dt=F32: attn.enter_context(nc.sbuf_tensor(name, shape, dt))
            wkv_hi, wkv_lo = (sb(n, [P, KT, 2, KVH * D], F32R) for n in ("wkv_hi", "wkv_lo"))
            sk_hi, sk_lo = (sb(n, [P, PC, KVH * D], F32R) for n in ("sk_hi", "sk_lo"))
            v_hi, v_lo = (sb(n, [P, PC, KVH * D], F32R) for n in ("v_hi", "v_lo"))
            kt = sb("kt", [P, 2, 512])
            bkv_sb = sb("bkv_sb", [P, 2, 512])
            wq_hi, wq_lo = (sb(n, [P, KT, H * D], F32R) for n in ("wq_hi", "wq_lo"))
            wo_hi, wo_lo = (sb(n, [P, H, HID], F32R) for n in ("wo_hi", "wo_lo"))
            hT_hi, hT_lo = (sb(n, [P, KT, PT], F32R) for n in ("hT_hi", "hT_lo"))
            kvT_hi, kvT_lo = (sb(n, [P, 2, KVH * D], F32R) for n in ("kvT_hi", "kvT_lo"))
            kvwo_hi, kvwo_lo = (sb(n, [P, 2, 2, 2, W2], F32R) for n in ("kvwo_hi", "kvwo_lo"))
            ks_hi, ks_lo = (sb(n, [P, 2, KVH, 2], F32R) for n in ("ks_hi", "ks_lo"))
            sq_hi, sq_lo = (sb(n, [P, 2, PT], F32R) for n in ("sq_hi", "sq_lo"))
            vf = sb("vf", [P, 2, 512])
            ke = sb("ke", [P, 512])
            acc = sb("acc", [P, PC, HID])
            wst = sb("wst", [P, 2, STAGE])
            rows = sb("rows", [P, 2, 2, HID])
            ones_f = sb("ones_f", [P, 2])
            bq_sb, nbq_sb, bq1_sb = (sb(n, [P, H]) for n in ("bq_sb", "nbq_sb", "bq1_sb"))
            cs = sb("cs", [P, KT, 4, B])
            sa_col, ca_col = (sb(n, [P, KT, B]) for n in ("sa_col", "ca_col"))
            key_sums = sb("key_sums", [P, 2, KVH * D])
            qe = sb("qe", [P, 2, PT])
            x_sb = sb("x_sb", [P, 4, PC, HID])
        x_ln1, x_res, h2 = (x_sb[:, n, :, :] for n in range(3))
        ga_rows = wst[:, 0, :].rearrange("p (b n) -> p b n", b=2)
        hot = ke[:, 0:PC * TOPK * E].rearrange("p (c k e) -> p c k e", k=TOPK, e=E)
        h2T = vf[:].rearrange("p b (c k n) -> p (b c) k n", c=2, k=KT)
        xn = kt[:].rearrange("p a (c n) -> p (a c) n", n=HID)
        wmod_sb = x_sb[:, 1:, :, :].rearrange("p a c n -> p (a c) n").rearrange("p (k m) n -> p k m n", k=KT)
        gate_rows = rows[0:B].rearrange("p a m n -> p (a m n)")
        d3 = key_sums[:].rearrange("p b (n m) -> p b n m", n=2)[:, :, 0, :]
        wkv_raw = [acc[:, 0:2, :].rearrange("p c n -> p (c n)"), acc[:, 2:4, :].rearrange("p c n -> p (c n)"),
                   wst[:, 0, :], wst[:, 1, :]]

        with ExitStack() as ffn:
            sb = lambda name, shape, dt=F32: ffn.enter_context(nc.sbuf_tensor(name, shape, dt))
            gu_lo, gu_hi = (sb(n, [P, E, KT, 2 * FF], F32R) for n in ("gu_lo", "gu_hi"))
            dn_lo, dn_hi = (sb(n, [FH, E, 2, HID], F32R) for n in ("dn_lo", "dn_hi"))
            xt = sb("xt", [P, XR, HID])
            xT_hi, xT_lo = (sb(n, [P, 2, KT, P], F32R) for n in ("xT_hi", "xT_lo"))
            silu = sb("silu", [P, 2, FF])
            mid = sb("mid", [P, 2, FF])
            mT_hi, mT_lo = (sb(n, [FH, 2, 2, P], F32R) for n in ("mT_hi", "mT_lo"))
            y_sb = sb("y_sb", [P, 2, HID])
        with ExitStack() as arrive:
            sb = lambda name, shape, dt=F32: arrive.enter_context(nc.sbuf_tensor(name, shape, dt))
            gu_raw = sb("gu_raw", [P, E, KT, 2 * FF])
            sb("over_gu_hi", [P, E, KT, 2 * FF])
            dn_raw = sb("dn_raw", [FH, E, 2, HID])
        with ExitStack() as route:
            sb = lambda name, shape, dt=F32: route.enter_context(nc.sbuf_tensor(name, shape, dt))
            sb("below_routing", [P, ROUTING_AT // 4])
            cst = sb("cst", [P, C_END])
            cmp = sb("cmp", [P, E, E])
            steps = sb("steps", [P, E])
            ntile, start = (sb(n, [P, E]) for n in ("ntile", "start"))
            count = sb("count", [P, E])
            total = sb("total", [P, 1])
            zero = sb("zero", [P, HID])
            reached = sb("reached", [P, CH * TOPK, E])
            n_reached, out_first, out_row = (sb(n, [P, CH * TOPK]) for n in ("n_reached", "out_first", "out_row"))
            tcmp = sb("tcmp", [1, TILES, E])
            tile, tsum, tstart, trow = (sb(n, [1, TILES]) for n in ("tile", "tsum", "tstart", "trow"))
        with ExitStack() as combine:
            sb = lambda name, shape, dt=F32: combine.enter_context(nc.sbuf_tensor(name, shape, dt))
            yg = sb("yg", [P, RING, TOPK, HID])
            x1_sb = sb("x1_sb", [P, RING, HID])
            gb_sb = sb("gb_sb", [P, B, HID])
            o_sb = sb("o_sb", [P, RING, HID])

        s = {n: ctx.enter_context(nc.semaphore(n)) for n in (
            "x_ln1_in", "x_res_in", "ident_in", "bias_in", "router_in", "c_in", "mod_in0", "mod_in1", "wkv_in", "wst_in0", "wst_in1", "ga_in", "rows_in", "ksum_in", "zero_made", "zeroed", "final_step", "x1_out",
            "silu_exp", "silu_step", "gates", "gate_step", "modrow_out", "ones_made", "half_made",
            "wkv_hi", "wkv_lo", "wst_hi", "wst_lo", "misc_ready", "misc_done", "misc_hi",
            "ln1_step", "ln1_rstd", "ln2_step", "ln2_rstd", "xn_ready", "hT_hi", "hT_lo",
            "k_neg", "k_act", "q_neg", "q_exp", "nbq", "bq1", "sk_f", "sk_hi", "sk_lo", "v_hi", "v_lo",
            "q_ready", "sq_f", "sq_hi", "sq_lo", "d_ready", "rn_step", "acc_done", "d3_scaled", "acc3_done",
            "x1_step", "x1_made", "h2_n", "h2_step",
            "cst_in", "iota_in", "tri_in", "tri_made", "h2T_made", "cum_made", "route_step", "exp_done", "mask_made",
            "slots_made", "ends_made", "outs_made", "tiles_made", "scattered",
            "gu_in", "dn_in", "gw_hi", "gw_lo", *(f"xt_in{r}" for r in range(XR)), "x_turned", "xT_hi", "xT_lo", "gu_done", "silu_done", "mid_done",
            "m_turned", "mT_hi", "mT_lo", "down_done", "y_made", "y_out0", "y_out1",
            "gap_made", *(f"{n}{r}" for n in ("gathered", "x1_back", "o_out") for r in range(RING)), "gb_in", "o_made")}

        FOLDS_AT = [[(h // 2 + 1, h % 2)] if 2 <= h < H - 4 else [] for h in range(H)]
        FOLDS_AT[H - 4] = [(H // 2 - 1, 0), (H // 2 - 1, 1)]
        ROUTES_AT = {h: [] for h in range(H)}
        ROUTES_AT[5], ROUTES_AT[7], ROUTES_AT[9], ROUTES_AT[11] = [("turn", 0)], [("turn", 1)], [("logits", 0)], [("ranks", 0)]
        ROUTES = sum(ROUTES_AT.values(), [])

        PREPARED = 20
        place, n_jobs = {}, 4 + PREPARED - 2
        for h in range(H):
            for job in FOLDS_AT[h] + ROUTES_AT[h]:
                place[job] = n_jobs
                n_jobs += 1
        JOBS = n_jobs - 4
        assert JOBS % 2 == 0
        job_T = lambda j, k: j * JOBS + ((2 if isinstance(j, int) and j == 0 else 4) + k)
        job_KV = lambda j, c, v: j * JOBS + (6 + 2 * c + 2 * (c // 3) + v)
        job_kvT = lambda j, b: j * JOBS + (12 + 6 * b)
        job_ks = lambda j, b: j * JOBS + (13 + 6 * b)
        fold_place = lambda hp, b: (4 + 2 * hp + b) if hp >= 2 else (2 + hp + 4 * b)
        job_fold = lambda j, hp, b: j * JOBS + (place[hp, b] if hp >= 2 else 14 + fold_place(hp, b))
        is_last = lambda j: isinstance(j, int) and j == PAIRS - 1
        h2_of = lambda j: x_ln1 if is_last(j) else h2
        job_route = lambda j, r: PAIRS * JOBS + 4 + ROUTES.index(r) if is_last(j) else j * JOBS + (JOBS + place[r])
        def jobs_passed(j, hp, b):
            skipped = [len(ROUTES_AT[h]) for h in range(H) if FOLDS_AT[h] and FOLDS_AT[h][-1] == (hp, b)]
            return 1 + (sum(skipped) if isinstance(j, int) and j == 0 else 0)
        bank = lambda n: ps_m[:, n % 2, :]
        def piece_of(n, wq, wo):
            quad, m = n // 4, n % 4
            if m < 2:
                return wq[:, m, quad * STAGE:(quad + 1) * STAGE]
            return wo[:, 4 * quad + 2 * m - 4:4 * quad + 2 * m - 2, :].rearrange("p h n -> p (h n)")

        HIS = 20
        hi_kvT = lambda j, b: j * HIS + 4 * b
        hi_ks = lambda j, b: j * HIS + (4 * b + 1)
        hi_fold = lambda j, hp, b: j * HIS + fold_place(hp, b)
        bank_route = lambda j, r: bank(job_route(j if is_last(j) else 0, r))
        bank_fold = lambda hp, b: bank(job_fold(0, hp, b))

        carried = [0]

        def wait_from(eng, semaphore, value):
            if not (isinstance(value, int) and value == 0):
                eng.wait_ge(semaphore, value)

        def wait_apart(eng, semaphore, value):
            eng.wait_ge(semaphore, value)
            col = slice(carried[0] % 8, carried[0] % 8 + 1)
            carried[0] += 1
            if eng.engine == nc.vector.engine:
                eng.memset(carry_v[:, col], 0.0)
            else:
                eng.tensor_tensor(carry_g[:, col], half[:, 0:1], half[:, 0:1], ALU.add)

        def over_pairs(eng, body):
            body(0, False, True)
            with eng.Fori(1, PAIRS - 1) as j:
                body(j, True, True)
            body(PAIRS - 1, True, False)

        def over_tiles(eng, step):
            for t in range(UNROLL):
                step(t, t, "LGX" + "A" * (t >= 1) + "D" * (t >= 2))
            with eng.Fori(1, TILES // UNROLL - 1) as m:
                for n in range(UNROLL):
                    step(m * UNROLL + n, n, "LGXAD")
            for n in range(UNROLL + 2):
                t = TILES - UNROLL + n
                step(t, n, "L" * (t + XR - 1 < TILES) + "X" * (t + 1 < TILES) + "G" * (t < TILES) + "A" * (t <= TILES) + "D")

        block = ctx.enter_context(nc.Block())

        @block.sync
        def _(sp):
            def load_x(dst, j, arrived):
                sp.dma_start(dst, x_in[bass.ds(j * PT, PT), :].rearrange("(c p) n -> p c n", p=P)).then_inc(arrived, 16)

            for k in range(KT):
                sp.dma_start(cs[:, k, 0, :], cT[k * P:(k + 1) * P, :]).then_inc(s["c_in"], 16)
            load_x(x_ln1, 0, s["x_ln1_in"])
            load_wmod = lambda part, k, m: sp.dma_start(wmod_sb[:, k, m[0]:m[1], :], wmod[k * P:(k + 1) * P, HID * m[0]:HID * m[1]].rearrange(
                "p (m n) -> p m n", n=HID)).then_inc(s[f"mod_in{part}"], 16)
            for k in range(KT):
                load_wmod(0, k, (0, 2))
            sp.dma_start(ident[:], consts[:, C_EYE:C_EYE + P]).then_inc(s["ident_in"], 16)
            for n in range(4):
                sp.dma_start(wkv_raw[n], wkvT[(n % 2) * P:(n % 2 + 1) * P, (n // 2) * 512:(n // 2 + 1) * 512]).then_inc(s["wkv_in"], 16)
            for k in range(KT):
                load_wmod(1, k, (2, 6))
            sp.dma_start(bkv_sb[:].rearrange("p a n -> p (a n)"), bkv.partition_broadcast(P)).then_inc(s["bias_in"], 16)
            sp.dma_start(bq_sb[:], bqT).then_inc(s["bias_in"], 16)
            sp.dma_start(iota_first[:].rearrange("p a e -> p (a e)"), consts[:, C_IOTA:C_IOTA + 2 * E]).then_inc(s["iota_in"], 16)
            sp.dma_start(ebias_sb[:], ebias.partition_broadcast(P)).then_inc(s["router_in"], 16)
            sp.dma_start(router_sb[:], routerT.rearrange("(k p) e -> p k e", p=P)).then_inc(s["router_in"], 16)
            sp.wait_ge(s["misc_ready"], 6)
            load_x(x_res, 0, s["x_res_in"])
            sp.wait_ge(s["xn_ready"], PC)
            load_x(x_ln1, 1, s["x_ln1_in"])
            sp.wait_ge(s["wkv_lo"], 4)
            sp.dma_start(acc[:, 0, :], consts[:, C_TRI:C_TRI + 2 * P]).then_inc(s["tri_in"], 16)
            for n in range(16):
                if n >= 2:
                    sp.wait_ge(s["wst_lo"], n - 1)
                quad, m = n // 4, n % 4
                if m < 2:
                    src = wqT[m * P:(m + 1) * P, quad * STAGE:(quad + 1) * STAGE]
                else:
                    src = woT[:, (2 * quad + m - 2) * STAGE:(2 * quad + m - 1) * STAGE]
                sp.dma_start(wst[:, n % 2, :], src).then_inc(s[f"wst_in{n % 2}"], 16)
            sp.wait_ge(s["gates"], 1)
            sp.dma_start(mod_rows, gate_rows).then_inc(s["modrow_out"], 16)
            sp.wait_ge(s["modrow_out"], 16)

            def pair_traffic(j, after):
                if after and not (isinstance(j, int) and j == 0):
                    sp.wait_ge(s["xn_ready"], j * PC + PC)
                    load_x(x_ln1, j + 1, s["x_ln1_in"])
                of_pair = lambda lo, hi: mod_rows[bass.ds(j * 2, 2), lo:hi].partition_broadcast(P)
                first = isinstance(j, int) and j == 0
                if first:
                    sp.wait_ge(s["wst_lo"], 16)
                else:
                    sp.wait_ge(s["x1_made"], j * PC)
                sp.dma_start(ga_rows, of_pair(0, HID)).then_inc(s["ga_in"], 16)
                if not first:
                    sp.wait_ge(s["h2_step"], j * (2 * PC))
                    load_x(x_res, j, s["x_res_in"])
                sp.dma_start(rows[:].rearrange("p b m n -> p b (m n)"), of_pair(HID, 3 * HID)).then_inc(s["rows_in"], 16)
                if not after:
                    sp.wait_ge(s["misc_ready"], job_ks(j, 1) + 1)
                    with sp.Fori(0, E) as e:
                        sp.dma_start(gu_raw[:, bass.ds(e, 1), :, :], w_gu[bass.ds(e, 1), :, :].rearrange("a (k p) n -> p a k n", p=P)
                                     ).then_inc(s["gu_in"], 16)
                sp.wait_ge(s["x1_made"], j * PC + PC)
                sp.dma_start(x1_dram[bass.ds(j * PT, PT), :].rearrange("(c p) n -> p c n", p=P), x_res).then_inc(s["x1_out"], 16)

            pair_traffic(0, True)
            with sp.Fori(1, PAIRS - 1) as j:
                pair_traffic(j, True)
            pair_traffic(PAIRS - 1, False)
            sp.wait_ge(s["h2_step"], 2 * CH)
            sp.wait_ge(s["x1_out"], 16 * PAIRS)
            sp.dma_start(cst[:], consts).then_inc(s["cst_in"], 16)

            with sp.Fori(0, E) as e:
                sp.dma_start(dn_raw[:, bass.ds(e, 1), :, :], w_down[bass.ds(e, 1), :, :].rearrange("a (k p) n -> p a k n", p=FH)
                             ).then_inc(s["dn_in"], 16)
            sp.wait_ge(s["zero_made"], 1)
            sp.wait_ge(s["ends_made"], 1)
            for e in range(E):
                row = sp.value_load(end_row[0:1, e:e + 1], min_val=0, max_val=SLOTS - P)
                sp.dma_start(xs_dram[bass.ds(row, P), :], zero[:]).then_inc(s["zeroed"], 16)
            sp.wait_ge(s["tiles_made"], 2)
            sp.wait_ge(s["scattered"], 16 * CH * TOPK)
            sp.wait_ge(s["zeroed"], 16 * E)

            row_of = lambda n: sp.value_load(tile_row[0:1, bass.ds(n, 1)], min_val=0, max_val=SLOTS - P)

            def load_tile(row, place):
                sp.dma_start(xt[:, place, :], xs_dram[bass.ds(row, P), :]).then_inc(s[f"xt_in{place}"], 16)

            def step(t, n, what):
                if "L" in what:
                    row = row_of(t + XR - 1)
                    wait_from(sp, s["x_turned"], t)
                    load_tile(row, (n + XR - 1) % XR)
                if "D" in what:
                    sp.wait_ge(s["y_made"], t - 1)
                    sp.dma_start(ys_dram[bass.ds((t - 2) * P, P), :], y_sb[:, n % 2, :]).then_inc(s[f"y_out{n % 2}"], 16)

            for n in range(XR - 1):
                load_tile(row_of(n), n)
            over_tiles(sp, step)
            for par in range(2):
                sp.wait_ge(s[f"y_out{par}"], 8 * TILES)
            sp.dma_start(gb_sb[:], mod_rows[:, 3 * HID:4 * HID].partition_broadcast(P)).then_inc(s["gb_in"], 16)

            def store_chunk(c):
                sp.wait_ge(s["o_made"], c + 1)
                sp.dma_start(out[c * P:(c + 1) * P, :], o_sb[:, c % RING, :]).then_inc(s[f"o_out{c % RING}"], 16)

            for c in range(CH):
                if c >= RING:
                    sp.wait_ge(s["o_made"], c - RING + 1)
                sp.dma_start(x1_sb[:, c % RING, :], x1_dram[c * P:(c + 1) * P, :]).then_inc(s[f"x1_back{c % RING}"], 16)
                if c >= RING - 1:
                    store_chunk(c - RING + 1)
            for c in range(CH - RING + 1, CH):
                store_chunk(c)
            for r in range(RING):
                sp.wait_ge(s[f"o_out{r}"], 16 * CH // RING)

        @block.tensor
        def _(pe):
            def product(dst, l_hi, l_lo, r_hi, r_lo, first, last):
                pe.matmul(dst, l_hi, r_hi, start=first, stop=False)
                pe.matmul(dst, l_hi, r_lo, start=False, stop=False)
                return pe.matmul(dst, l_lo, r_hi, start=False, stop=last)

            def columns():
                pe.wait_ge(s["silu_step"], 3)
                pe.wait_ge(s["mod_in0"], 32)
                for m in range(2):
                    for kk in range(KT):
                        for k in range(KT):
                            last = pe.matmul(bank(m)[:, kk * B:(kk + 1) * B], wmod_sb[:, k, m, kk * P:(kk + 1) * P], cs[:, k, 0, :],
                                             start=(k == 0), stop=(k == KT - 1))
                    last.then_inc(s["misc_ready"], 1)

            def gates():
                pe.wait_ge(s["mod_in1"], 32)
                for n in range(2):
                    pe.wait_ge(s["misc_done"], n + 3)
                    for k in range(KT):
                        last = pe.matmul(bank(n)[0:B, :], cs[:, k, 0, :], wmod_sb[:, k, 2 + 2 * n:4 + 2 * n, :].rearrange("p m n -> p (m n)"),
                                         start=(k == 0), stop=(k == KT - 1))
                    last.then_inc(s["misc_ready"], 1)

            def T(j):
                pe.wait_ge(s["xn_ready"], j * PC + PC)
                for k in range(KT):
                    pe.wait_ge(s["misc_done"], job_T(j, k) - 1)
                    for c in range(PC):
                        last = pe.transpose(bank(k)[:, c * P:(c + 1) * P], xn[:, c, k * P:(k + 1) * P], ident[:])
                    last.then_inc(s["misc_ready"], 1)

            def KV(j, c):
                pe.wait_ge(s["hT_lo"], j * KT + KT)
                for v in range(2):
                    pe.wait_ge(s["misc_done"], job_KV(j, c, v) - 1)
                    tok = slice(c * P, (c + 1) * P)
                    for k in range(KT):
                        last = product(bank(v), hT_hi[:, k, tok], hT_lo[:, k, tok], wkv_hi[:, k, v, :], wkv_lo[:, k, v, :],
                                       k == 0, k == KT - 1)
                    last.then_inc(s["misc_ready"], 1)

            def state(j, b):
                pe.wait_ge(s["sk_lo"], j * PC + 2 * (b + 1))
                pe.wait_ge(s["v_lo"], j * PC + 2 * (b + 1))
                pe.wait_ge(s["misc_done"], job_kvT(j, b) - 1)
                for g in range(KVH):
                    gd = slice(g * D, (g + 1) * D)
                    for n in range(2):
                        c = 2 * b + n
                        last = product(bank(0)[:, gd], v_hi[:, c, gd], v_lo[:, c, gd], sk_hi[:, c, gd], sk_lo[:, c, gd],
                                       n == 0, n == 1)
                last.then_inc(s["misc_ready"], 1)
                pe.wait_ge(s["ksum_in"], j * 2 + (b + 1))
                pe.wait_ge(s["misc_done"], job_ks(j, b) - 1)
                for g in range(KVH):
                    last = pe.matmul(bank(1)[:, 2 * g:2 * g + 2], key_sums[:, b, g * D:(g + 1) * D], ones_f[:], start=True, stop=True)
                last.then_inc(s["misc_ready"], 1)

            def fold(j, hp, b):
                pe.wait_ge(s["misc_done"], job_fold(j, hp, b) - 1)
                gd = slice((hp // 2) * D, (hp // 2 + 1) * D)
                w_hi, w_lo = (w[:, 2 * hp:2 * hp + 2, :].rearrange("p h n -> p (h n)") for w in (wo_hi, wo_lo))
                product(bank_fold(hp, b), kvT_hi[:, b, gd], kvT_lo[:, b, gd], w_hi, w_lo, True, True).then_inc(s["misc_ready"], jobs_passed(j, hp, b))

            def Q(j, h):
                wait_from(pe, s["sq_f"], j * H + (h - 1 if h >= 2 else 0))
                hd = slice(h * D, (h + 1) * D)
                for k in range(KT):
                    last = product(ps_q[:, h % 2, :], wq_hi[:, k, hd], wq_lo[:, k, hd], hT_hi[:, k, :], hT_lo[:, k, :],
                                   k == 0, k == KT - 1)
                last.then_inc(s["q_ready"], 1)

            def heads_out(j, h, b):
                pe.wait_ge(s["sq_lo"], j * H + (h + 1))
                pe.wait_ge(s["misc_done"], job_fold(j, h // 2, b) + 1)
                wait_from(pe, s["acc_done"], j * (3 * H) + (3 * (h - 1) + 2 + b if h else 0))
                if b == 1:
                    wait_from(pe, s["d3_scaled"], j * H + h)
                r_hi, r_lo = (r[:, (h // 2) % 2, b, h % 2, :] for r in (kvwo_hi, kvwo_lo))
                for c in (2 * b, 2 * b + 1):
                    tok = slice(c * P, (c + 1) * P)
                    last = product(ps_d[:, c, 0:W2], sq_hi[:, h % 2, tok], sq_lo[:, h % 2, tok], r_hi, r_lo, True, True)
                last.then_inc(s["d_ready"], 1)

            def pair(j, before, after):
                for h in range(H):
                    if after and h == H - 3:
                        T(j + 1)
                    heads_out(j, h, 0)
                    if h + 2 < H:
                        pe.wait_ge(s["wst_lo"], 4 * ((h + 2) // 4) + 4)
                        Q(j, h + 2)
                    heads_out(j, h, 1)
                    for hp, b in FOLDS_AT[h]:
                        fold(j, hp, b)
                    if before:
                        for r in ROUTES_AT[h]:
                            route(j - 1, *r)
                    if after and h == H - 2:
                        KV(j + 1, 0)
                if after:
                    prepare(j + 1)
                else:
                    for r in ROUTES:
                        route(j, *r)

            def route(j, what, c):
                pe.wait_ge(s["misc_done"], job_route(j, (what, c)) - 1)
                dst = bank_route(j, (what, c))
                if what == "turn":
                    pe.wait_ge(s["h2_step"], j * (2 * PC) + (4 * c + 4))
                    for i in range(2):
                        for k in range(KT):
                            col = (KT * i + k) * P
                            last = pe.transpose(dst[:, col:col + P], h2_of(j)[:, 2 * c + i, k * P:(k + 1) * P], ident[:])
                elif what == "logits":
                    pe.wait_ge(s["router_in"], 32)
                    pe.wait_ge(s["h2T_made"], j * 2 + 2)
                    for i in range(PC):
                        for k in range(KT):
                            last = pe.matmul(dst[:, i * E:(i + 1) * E], h2T[:, i, k, :], router_sb[:, k, :], start=(k == 0), stop=(k == KT - 1))
                else:
                    pe.wait_ge(s["mask_made"], j + 1)
                    flat_mask = mask[:].rearrange("p c e -> p (c e)")
                    before, all_of = tri[:, 0:P], tri[:, P:2 * P]
                    pe.matmul(dst[:, 0:PC * E], before, flat_mask, start=True, stop=False)
                    for i in range(1, PC):
                        for n in range(i):
                            pe.matmul(dst[:, i * E:(i + 1) * E], all_of, mask[:, n, :], start=False, stop=(i == PC - 1 and n == i - 1))
                    for n in range(PC):
                        last = pe.matmul(dst[:, PC * E:(PC + 1) * E], all_of, mask[:, n, :], start=(n == 0), stop=(n == PC - 1))
                last.then_inc(s["misc_ready"], 1)

            def prepare(j):
                KV(j, 1)
                KV(j, 2)
                pe.wait_ge(s["wst_lo"], 2)
                Q(j, 0)
                state(j, 0)
                KV(j, 3)
                pe.wait_ge(s["wst_lo"], 4)
                fold(j, 0, 0)
                Q(j, 1)
                fold(j, 1, 0)
                state(j, 1)
                fold(j, 0, 1)
                fold(j, 1, 1)

            pe.wait_ge(s["ident_in"], 16)
            columns()
            T(0)
            gates()
            pe.wait_ge(s["wkv_lo"], 4)
            pe.wait_ge(s["ones_made"], 1)
            KV(0, 0)
            prepare(0)
            over_pairs(pe, pair)
            pe.wait_ge(s["h2_step"], 2 * CH)
            pe.wait_ge(s["x1_out"], 16 * PAIRS)
            pe.wait_ge(s["tiles_made"], 2)

            expert_of = {}

            def step(t, place, what):
                par, other = place % 2, 1 - place % 2
                if "G" in what:
                    expert_of[place] = pe.value_load(tile_e[0:1, bass.ds(t, 1)], min_val=0, max_val=E - 1)
                if "X" in what:
                    n, r = t + 1, (place + 1) % XR
                    pe.wait_ge(s[f"xt_in{r}"], n * (16 // XR) + (16 - 16 // XR * r))
                    for k in range(KT):
                        last = pe.transpose(ps_d[:, other, k * P:(k + 1) * P], xt[:, r, k * P:(k + 1) * P], ident[:])
                    last.then_inc(s["x_turned"], 1)
                if "G" in what:
                    e = expert_of[place]
                    pe.wait_ge(s["xT_lo"], t + 1)
                    for k in range(KT):
                        r_hi, r_lo = (w[:, bass.ds(e, 1), k, :] for w in (gu_hi, gu_lo))
                        last = product(ps_q[:, par, 0:2 * FF], xT_hi[:, par, k, :], xT_lo[:, par, k, :], r_hi, r_lo, k == 0, k == KT - 1)
                    last.then_inc(s["gu_done"], 1)
                if "A" in what:
                    pe.wait_ge(s["mid_done"], t)
                    for i in range(2):
                        last = pe.transpose(ps_d[0:FH, 2 + other, i * P:(i + 1) * P], mid[:, other, i * FH:(i + 1) * FH], ident[:])
                    last.then_inc(s["m_turned"], 1)
                if "D" in what:
                    e = expert_of[place - 2] if place >= 2 else pe.value_load(tile_e[0:1, bass.ds(t - 2, 1)], min_val=0, max_val=E - 1)
                    pe.wait_ge(s["mT_lo"], t - 1)
                    for i in range(2):
                        r_hi, r_lo = (w[:, bass.ds(e, 1), i, :] for w in (dn_hi, dn_lo))
                        last = product(ps_m[:, par, 0:HID], mT_hi[:, par, i, :], mT_lo[:, par, i, :], r_hi, r_lo, i == 0, i == 1)
                    last.then_inc(s["down_done"], 1)

            pe.wait_ge(s["xt_in0"], 16)
            for k in range(KT):
                last = pe.transpose(ps_d[:, 0, k * P:(k + 1) * P], xt[:, 0, k * P:(k + 1) * P], ident[:])
            last.then_inc(s["x_turned"], 1)
            pe.wait_ge(s["gw_lo"], 2 * E)
            over_tiles(pe, step)

        @block.scalar
        def _(act):
            def copy_hi(dst, src):
                return act.activation(dst, src, ACT.Copy)

            def T(j, first=False):
                for k in range(KT):
                    act.wait_ge(s["misc_done"], job_T(j, k) + 1)
                    if not first:
                        act.wait_ge(s["q_ready"], j * H)
                    copy_hi(hT_hi[:, k, :], vf[:, k, :]).then_inc(s["hT_hi"], 1)

            def KV(j, c, first=False):
                act.wait_ge(s["misc_done"], job_KV(j, c, 0) + 1)
                wait_from(act, s["sk_f"], j * PC + c)
                act.activation(ke[:], kt[:, c % 2, :], ACT.Relu, scale=-1.0).then_inc(s["k_neg"], 1)
                act.wait_ge(s["k_neg"], j * PC + (c + 1))
                act.activation(ke[:], ke[:], ACT.Exp, scale=-1.0).then_inc(s["k_act"], 1)
                act.wait_ge(s["misc_done"], job_KV(j, c, 1) + 1)
                if not first:
                    act.wait_ge(s["misc_ready"], j * JOBS + (18 - JOBS))
                copy_hi(v_hi[:, c, :], vf[:, c % 2, :]).then_inc(s["v_hi"], 1)
                act.wait_ge(s["sk_f"], j * PC + (c + 1))
                copy_hi(sk_hi[:, c, :], kt[:, c % 2, :]).then_inc(s["sk_hi"], 1)

            def state(j, b):
                act.wait_ge(s["misc_ready"], job_kvT(j, b) + 1)
                copy_hi(kvT_hi[:, b, :], bank(0)).then_inc(s["misc_hi"], 1)
                act.wait_ge(s["misc_ready"], job_ks(j, b) + 1)
                copy_hi(ks_hi[:, b, :, :].rearrange("p g n -> p (g n)"), bank(1)[:, 0:2 * KVH]).then_inc(s["misc_hi"], 1)

            def fold(j, hp, b):
                act.wait_ge(s["misc_ready"], job_fold(j, hp, b) + 1)
                wait_from(act, s["d_ready"], j * (2 * H) + (4 * hp - 4 if hp >= 2 else 0))
                copy_hi(kvwo_hi[:, hp % 2, b, :, 0:HID], bank_fold(hp, b).rearrange("p (h n) -> p h n", h=2)).then_inc(s["misc_hi"], 1)

            def elu(j, h):
                act.wait_ge(s["q_ready"], j * H + (h + 1))
                wait_from(act, s["sq_lo"], j * H + (h - 1 if h >= 2 else 0))
                act.activation(qe[:, h % 2, :], ps_q[:, h % 2, :], ACT.Relu, bias=nbq_sb[:, h:h + 1], scale=-1.0).then_inc(s["q_neg"], 1)
                act.wait_ge(s["q_neg"], j * H + (h + 1))
                act.activation(qe[:, h % 2, :], qe[:, h % 2, :], ACT.Exp, scale=-1.0).then_inc(s["q_exp"], 1)

            def hi(j, h):
                act.wait_ge(s["sq_f"], j * H + (h + 1))
                wait_from(act, s["d_ready"], j * (2 * H) + (2 * h - 2 if h >= 2 else 0))
                copy_hi(sq_hi[:, h % 2, :], qe[:, h % 2, :]).then_inc(s["sq_hi"], 1)

            def pair(j, before, after):
                for h in range(H):
                    if h == H - 2:
                        scale3(j, h - 1)
                    if h + 1 < H:
                        hi(j, h + 1)
                    if 1 <= h < H - 2:
                        scale3(j, h - 1)
                    if after and h == H - 3:
                        T(j + 1)
                    if h + 2 < H:
                        elu(j, h + 2)
                    for hp, b in FOLDS_AT[h]:
                        fold(j, hp, b)
                    if before and h == 10:
                        weights(j - 1)
                    if not before and h < 8:
                        piece_hi(8 + h)
                    if h == H - 2:
                        scale3(j, h)
                    if after and h == H - 2:
                        KV(j + 1, 0)
                scale3(j, H - 1)
                if after:
                    prepare(j + 1)
                else:
                    act.wait_ge(s["gu_in"], 16 * E)
                    high_parts(gu_hi, gu_raw)
                    weights(j)

            def high_parts(hi, raw):
                with act.Fori(0, E) as m:
                    e = bass.ds(m, 1)
                    copy_hi(hi[:, e, :, :], raw[:, e, :, :]).then_inc(s["gw_hi"], 1)

            def weights(j):
                act.wait_ge(s["gap_made"], j + 1)
                act.activation(weight[:], gap[:], ACT.Exp).then_inc(s["exp_done"], 1)

            def scale3(j, h):
                act.wait_ge(s["rn_step"], j * (4 * H) + (4 * h + 4))
                if h == 0:
                    wait_from(act, s["x1_made"], j * PC)
                elif h >= 3:
                    act.wait_ge(s["acc3_done"], j * (H - 1) + (h - 2))
                act.activation(acc[:, 3, :] if h == 0 else d3[:, h % 2, :], ps_d[:, 3, 0:HID], ACT.Copy,
                               scale=rn[:, 1, 1:2]).then_inc(s["d3_scaled"], 1)

            def piece_hi(n):
                act.wait_ge(s[f"wst_in{n % 2}"], 16 * (n // 2 + 1))
                copy_hi(piece_of(n, wq_hi, wo_hi), wst[:, n % 2, :]).then_inc(s["wst_hi"], 1)

            def prepare(j, first=False):
                for c in range(1, PC):
                    if first:
                        piece_hi(2 * c - 2)
                        piece_hi(2 * c - 1)
                    KV(j, c, first)
                    if c == 2:
                        state(j, 0)
                        elu(j, 0)
                        hi(j, 0)
                fold(j, 0, 0)
                elu(j, 1)
                fold(j, 1, 0)
                if first:
                    piece_hi(6)
                    piece_hi(7)
                state(j, 1)
                fold(j, 0, 1)
                fold(j, 1, 1)

            act.wait_ge(s["c_in"], 32)
            act.activation(cs[:, :, 1, :], cs[:, :, 0, :], ACT.Exp, scale=-1.0).then_inc(s["silu_exp"], 1)
            for n in range(4):
                act.wait_ge(s["wkv_in"], 64)
                copy_hi(wkv_hi[:, n % 2, n // 2, :], wkv_raw[n]).then_inc(s["wkv_hi"], 1)
            T(0, first=True)
            act.wait_ge(s["bias_in"], 32)
            act.activation(nbq_sb[:], bq_sb[:], ACT.Copy, scale=-1.0).then_inc(s["nbq"], 1)
            act.wait_ge(s["nbq"], 1)
            KV(0, 0, first=True)
            prepare(0, first=True)
            over_pairs(act, pair)
            act.wait_ge(s["dn_in"], 16 * E)
            act.wait_ge(s["tiles_made"], 2)
            act.wait_ge(s["zeroed"], 16 * E)
            high_parts(dn_hi, dn_raw)

            def x_hi(n, q):
                act.wait_ge(s["x_turned"], n + 1)
                if not (isinstance(n, int) and n < 2):
                    act.wait_ge(s["gu_done"], n - 1)
                copy_hi(xT_hi[:, q, :, :].rearrange("p k n -> p (k n)"), ps_d[:, q, 0:HID]).then_inc(s["xT_hi"], 1)

            def step(t, par, what):
                par %= 2
                if "X" in what:
                    x_hi(t + 1, 1 - par)
                if "G" in what:
                    act.wait_ge(s["gu_done"], t + 1)
                    act.activation(silu[:, par, :], ps_q[:, par, 0:FF], ACT.Silu).then_inc(s["silu_done"], 1)
                if "A" in what:
                    n, q = t - 1, 1 - par
                    act.wait_ge(s["m_turned"], n + 1)
                    if not (isinstance(n, int) and n < 2):
                        act.wait_ge(s["down_done"], n - 1)
                    copy_hi(mT_hi[:, q, :, :].rearrange("p i n -> p (i n)"), ps_d[0:FH, 2 + q, 0:2 * P]).then_inc(s["mT_hi"], 1)
                if "D" in what:
                    n = t - 2
                    act.wait_ge(s["down_done"], n + 1)
                    if not (isinstance(n, int) and n < 2):
                        act.wait_ge(s[f"y_out{par}"], n * 8 - 8 * par)
                    act.activation(y_sb[:, par, :], ps_m[:, par, 0:HID], ACT.Copy).then_inc(s["y_made"], 1)

            x_hi(0, 0)
            over_tiles(act, step)

        @block.vector
        def _(dve):
            def split(dst, src, hi):
                return dve.tensor_tensor(dst, src, hi.bitcast(F32), ALU.subtract)

            def silu_c():
                dve.wait_ge(s["silu_exp"], 1)
                dve.tensor_scalar(cs[:, :, 2, :], cs[:, :, 1, :], 1.0, None, ALU.add).then_inc(s["silu_step"], 1)
                dve.wait_ge(s["silu_step"], 1)
                dve.reciprocal(cs[:, :, 3, :], cs[:, :, 2, :]).then_inc(s["silu_step"], 1)
                dve.wait_ge(s["silu_step"], 2)
                dve.tensor_tensor(cs[:, :, 0, :], cs[:, :, 0, :], cs[:, :, 3, :], ALU.mult).then_inc(s["silu_step"], 1)

            def columns():
                for m, dst in enumerate((sa_col, ca_col)):
                    dve.wait_ge(s["misc_ready"], m + 1)
                    dve.tensor_scalar(dst[:].rearrange("p k b -> p (k b)"), bank(m)[:, 0:KT * B], float(m), None,
                                      ALU.add).then_inc(s["misc_done"], 1)
                dve.wait_ge(s["misc_done"], 2)

            def gates_read():
                for n in range(2):
                    dve.wait_ge(s["misc_ready"], n + 5)
                    dve.tensor_copy(gate_rows[:, 2 * n * HID:(2 * n + 2) * HID], bank(n)[0:B, :]).then_inc(s["misc_done"], 1)

            def gates_made():
                dve.wait_ge(s["misc_done"], 6)
                step = 0
                tmp = qe[0:B].rearrange("p a n -> p (a n)")
                for m in (0, 3):
                    g, sign, size = gate_rows[:, m * HID:(m + 1) * HID], tmp[:, 0:HID], tmp[:, HID:2 * HID]
                    dve.tensor_scalar(sign, g, 0.0, 2.0, ALU.is_ge, ALU.mult).then_inc(s["gate_step"], 1)
                    dve.scalar_tensor_tensor(size, g, -1.0, g, ALU.mult, ALU.max).then_inc(s["gate_step"], 1)
                    dve.wait_ge(s["gate_step"], step + 2)
                    dve.tensor_scalar(sign, sign, -1.0, None, ALU.add).then_inc(s["gate_step"], 1)
                    dve.wait_ge(s["gate_step"], step + 3)
                    dve.scalar_tensor_tensor(g, size, 0.25, sign, ALU.max, ALU.mult).then_inc(s["gate_step"], 1)
                    step += 4
                    dve.wait_ge(s["gate_step"], step)
                cb = gate_rows[:, 2 * HID:3 * HID]
                dve.tensor_scalar(cb, cb, 1.0, None, ALU.add).then_inc(s["gates"], 1)

            def moments(src, n, step, base):
                for c in range(n):
                    dve.bn_stats(stats[:, c, :], src(c)).then_inc(step, 1)
                wait_apart(dve, step, base + n)
                for c in range(n):
                    dve.bn_aggr(mv[:, c, :], stats[:, c, :]).then_inc(step, 1)
                dve.wait_ge(step, base + 2 * n)
                dve.tensor_scalar(ve[:, 0:n], mv[:, 0:n, 1], LN_EPS, None, ALU.add).then_inc(step, 1)

            def ln1_moments(j):
                dve.wait_ge(s["x_ln1_in"], j * 16 + 16)
                moments(lambda c: x_ln1[:, c, :], PC, s["ln1_step"], j * (2 * PC + 1))

            def ln1_rows(j):
                dve.wait_ge(s["ln1_rstd"], j + 1)
                for c in range(PC):
                    dve.tensor_scalar(xn[:, c, :], x_ln1[:, c, :], mv[:, c, 0:1], rstd[:, c:c + 1],
                                      ALU.subtract, ALU.mult).then_inc(s["xn_ready"], 1)

            def T_turned(j):
                for k in range(KT):
                    dve.wait_ge(s["misc_ready"], job_T(j, k) + 1)
                    for b in range(2):
                        col = bass.ds(j * 2 + b, 1)
                        tok = slice(b * S, (b + 1) * S)
                        last = dve.tensor_scalar(vf[:, k, tok], bank(k)[:, tok], ca_col[:, k, col], sa_col[:, k, col], ALU.mult, ALU.add)
                    last.then_inc(s["misc_done"], 1)

            def T_lo(j):
                for k in range(KT):
                    dve.wait_ge(s["hT_hi"], j * KT + (k + 1))
                    split(hT_lo[:, k, :], vf[:, k, :], hT_hi[:, k, :]).then_inc(s["hT_lo"], 1)

            def KV_bias(j, c):
                for v, dst in enumerate((kt, vf)):
                    if c == 2 and v == 0:
                        dve.wait_ge(s["ksum_in"], j * 2 + 1)
                    dve.wait_ge(s["misc_ready"], job_KV(j, c, v) + 1)
                    if v == 1 and c == 2 and not (isinstance(j, int) and j == 0):
                        dve.wait_ge(s["v_lo"], j * PC + 2)
                    dve.tensor_tensor(dst[:, c % 2, :], bank(v), bkv_sb[:, v, :], ALU.add).then_inc(s["misc_done"], 1)

            def KV_elu(j, c):
                dve.wait_ge(s["k_act"], j * PC + (c + 1))
                dve.scalar_tensor_tensor(kt[:, c % 2, :], kt[:, c % 2, :], 1.0, ke[:], ALU.add, ALU.max).then_inc(s["sk_f"], 1)

            def KV_lo(j, c):
                if c % 2 == 1 or (isinstance(j, int) and j == 0):
                    dve.wait_ge(s["v_hi"], j * PC + (c + 1))
                    split(v_lo[:, c, :], vf[:, c % 2, :], v_hi[:, c, :]).then_inc(s["v_lo"], 1)
                dve.wait_ge(s["sk_hi"], j * PC + (c + 1))
                split(sk_lo[:, c, :], kt[:, c % 2, :], sk_hi[:, c, :]).then_inc(s["sk_lo"], 1)

            def state(j, b):
                dve.wait_ge(s["misc_hi"], hi_kvT(j, b) + 1)
                split(kvT_lo[:, b, :], bank(0), kvT_hi[:, b, :]).then_inc(s["misc_done"], 1)
                dve.wait_ge(s["misc_hi"], hi_ks(j, b) + 1)
                split(ks_lo[:, b, :, :].rearrange("p g n -> p (g n)"), bank(1)[:, 0:2 * KVH],
                      ks_hi[:, b, :, :].rearrange("p g n -> p (g n)")).then_inc(s["misc_done"], 1)
                dve.wait_ge(s["misc_done"], job_ks(j, b) + 1)

            def fold(j, hp, b):
                dve.wait_ge(s["misc_hi"], hi_fold(j, hp, b) + 1)
                for src, dst in ((ks_hi, kvwo_hi), (ks_lo, kvwo_lo)):
                    dve.tensor_copy(dst[:, hp % 2, b, :, HID:W2], src[:, b, hp // 2:hp // 2 + 1, :].broadcast_to([P, 2, 2]))
                split(kvwo_lo[:, hp % 2, b, :, 0:HID], bank_fold(hp, b).rearrange("p (h n) -> p h n", h=2),
                      kvwo_hi[:, hp % 2, b, :, 0:HID]).then_inc(s["misc_done"], jobs_passed(j, hp, b))

            def following(j, h, before):
                for hp, b in FOLDS_AT[h]:
                    fold(j, hp, b)
                if before:
                    for r in ROUTES_AT[h]:
                        route(j - 1, *r)

            def later(h):
                return h % 2 == 0 and h != H - 4 and len(ROUTES_AT[h]) < 2

            ROUTE_STEPS = 8
            route_steps = [0]

            def then(j, ins):
                ins.then_inc(s["route_step"], 1)
                route_steps[0] = route_steps[0] % ROUTE_STEPS + 1
                wait_apart(dve, s["route_step"], j * ROUTE_STEPS + route_steps[0])

            flat = lambda t: t.rearrange("p c k -> p (c k)")
            hot_n = hot.rearrange("p c k e -> p (c k) e")

            def choices(j):
                for c in range(PC):
                    last = dve.max(top8[:, c, :], lg[:, c, :])
                then(j, last)
                for c in range(PC):
                    last = dve.max_index(arg8[:, c, :], top8[:, c, :], lg[:, c, :])
                then(j, last)
                dve.tensor_tensor(gap[:], top8[:, :, 0:TOPK], top8[:, :, 0:1].broadcast_to([P, PC, TOPK]), ALU.subtract).then_inc(s["gap_made"], 1)
                then(j, dve.tensor_copy(arg_f[:], arg8[:, :, 0:TOPK]))
                then(j, dve.tensor_tensor(hot_n, flat(arg_f[:]).unsqueeze(2).broadcast_to([P, PC * TOPK, E]),
                                          iota_first[:, 0:1, :].broadcast_to([P, PC * TOPK, E]), ALU.is_equal))
                then(j, dve.tensor_reduce(pos[:], hot.rearrange("p c k e -> p c e k"), AX_X, ALU.add))
                dve.tensor_copy(mask[:], pos[:]).then_inc(s["mask_made"], 1)

            def route(j, what, c):
                job = job_route(j, (what, c))
                src = bank_route(j, (what, c))
                dve.wait_ge(s["misc_ready"], job + 1)
                if what == "turn":
                    dve.tensor_copy(h2T[:, 2 * c:2 * c + 2, :, :].rearrange("p c k n -> p (c k n)"), src).then_inc(s["misc_done"], 1)
                    dve.wait_ge(s["misc_done"], job + 1)
                    dve.memset(carry_v[:, 7:8], 0.0).then_inc(s["h2T_made"], 1)
                elif what == "logits":
                    dve.tensor_tensor(lg[:], src[:, 0:PC * E].rearrange("p (c e) -> p c e", e=E),
                                      ebias_sb[:].unsqueeze(1).broadcast_to([P, PC, E]), ALU.add).then_inc(s["misc_done"], 1)
                    wait_apart(dve, s["misc_done"], job + 1)
                    choices(j)
                else:
                    dve.tensor_tensor(pos[:], src[:, 0:PC * E].rearrange("p (c e) -> p c e", e=E),
                                      cum[:].unsqueeze(1).broadcast_to([P, PC, E]), ALU.add)
                    dve.wait_ge(s["exp_done"], j + 1)
                    then(j, dve.tensor_reduce(wsum[:], weight[:], AX_X, ALU.add))
                    dve.tensor_tensor(cum[:], cum[:], src[:, PC * E:(PC + 1) * E], ALU.add).then_inc(s["misc_done"], 1)
                    dve.reciprocal(wrec[:], wsum[:])
                    then(j, dve.tensor_tensor(hot[:], hot[:], pos[:].unsqueeze(2).broadcast_to([P, PC, TOPK, E]), ALU.mult))
                    dve.tensor_tensor(wgt[:, bass.ds(j * PC, PC), :], weight[:], wrec[:].unsqueeze(2).broadcast_to([P, PC, TOPK]), ALU.mult)
                    then(j, dve.tensor_reduce(flat(arg_f[:]), hot_n, AX_X, ALU.add))
                    wait_from(dve, s["scattered"], j * (16 * PC * TOPK))
                    dve.tensor_copy(pair_slots[:], arg_f[:]).then_inc(s["slots_made"], 1)
                    dve.tensor_copy(in_row[:, bass.ds(j * PC, PC), :], arg_f[:]).then_inc(s["cum_made"], 1)

            def elu(j, h):
                dve.wait_ge(s["q_exp"], j * H + (h + 1))
                dve.scalar_tensor_tensor(qe[:, h % 2, :], ps_q[:, h % 2, :], bq1_sb[:, h:h + 1], qe[:, h % 2, :], ALU.add, ALU.max
                                         ).then_inc(s["sq_f"], 1)

            def heads_out(j, h, b):
                dve.wait_ge(s["d_ready"], j * (2 * H) + (2 * h + b + 1))
                n = 4 * h + 2 * b
                dve.tensor_scalar(rr[:, b, :], ps_d[:, 2 * b:2 * b + 2, HID], NORM_EPS, None, ALU.add).then_inc(s["rn_step"], 1)
                dve.wait_ge(s["rn_step"], j * (4 * H) + (n + 1))
                dve.reciprocal(rn[:, b, :], rr[:, b, :]).then_inc(s["rn_step"], 1)
                dve.wait_ge(s["rn_step"], j * (4 * H) + (n + 2))
                for i in range(2 - b):
                    c = 2 * b + i
                    if h == 0:
                        wait_from(dve, s["x1_made"], j * PC)
                        dve.tensor_scalar(acc[:, c, :], ps_d[:, c, 0:HID], rn[:, b, i:i + 1], None, ALU.mult).then_inc(s["acc_done"], 1)
                    else:
                        dve.wait_ge(s["acc_done"], j * (3 * H) + (3 * (h - 1) + c + 1))
                        dve.scalar_tensor_tensor(acc[:, c, :], ps_d[:, c, 0:HID], rn[:, b, i:i + 1], acc[:, c, :],
                                                 ALU.mult, ALU.add).then_inc(s["acc_done"], 1)

            def ln2_moments(j):
                dve.wait_ge(s["x1_made"], j * PC + PC)
                moments(lambda c: x_res[:, c, :], PC, s["ln2_step"], j * (2 * PC + 1))

            def ln2_rows(j):
                dve.wait_ge(s["ln2_rstd"], j + 1)
                dve.wait_ge(s["x1_out"], j * 16 + 16)
                for c in range(PC):
                    x = x_res[:, c, :]
                    dve.tensor_scalar(x, x, mv[:, c, 0:1], rstd[:, c:c + 1], ALU.subtract, ALU.mult).then_inc(s["h2_n"], 1)

            def pair(j, before, after):
                for h in range(H):
                    if after and h == H - 3:
                        T_turned(j + 1)
                    heads_out(j, h, 0)
                    if h >= 1 and later(h - 1):
                        following(j, h - 1, before)
                    if after and h == H - 1:
                        KV_bias(j + 1, 1)
                    heads_out(j, h, 1)
                    if after and h == H - 3:
                        T_lo(j + 1)
                    if h + 2 < H:
                        elu(j, h + 2)
                    if not later(h):
                        following(j, h, before)
                    if before and h == 1:
                        ln2_moments(j - 1)
                    if before and h == 2:
                        ln2_rows(j - 1)
                    if after and h == 6:
                        ln1_moments(j + 1)
                    if after and h == 9:
                        ln1_rows(j + 1)
                    if after and h == H - 2:
                        KV_bias(j + 1, 0)
                        KV_elu(j + 1, 0)
                if after:
                    prepare(j + 1)
                else:
                    last_x1(j)
                    ln2_moments(j)
                    gate_up_lo(0, 2)
                    ln2_rows(j)
                    last_h2(j)
                    shares = (2, 3, 4, LO_BETWEEN, LO_BETWEEN)
                    for n, r in enumerate(ROUTES):
                        route(j, *r)
                        gate_up_lo(shares[n], shares[n + 1])

            def last_x1(j):
                dve.wait_ge(s["ga_in"], j * 16 + 16)
                dve.wait_ge(s["acc_done"], (j + 1) * (3 * H))
                dve.wait_ge(s["acc3_done"], (j + 1) * (H - 1))
                for c in range(PC):
                    dve.tensor_tensor(acc[:, c, :], acc[:, c, :], ga_rows[:, c // 2, :], ALU.mult).then_inc(s["x1_step"], 1)
                dve.wait_ge(s["x_res_in"], j * 16 + 16)
                for c in range(PC):
                    dve.wait_ge(s["x1_step"], j * PC + (c + 1))
                    dve.tensor_tensor(x_res[:, c, :], acc[:, c, :], x_res[:, c, :], ALU.add).then_inc(s["x1_made"], 1)

            def last_h2(j):
                dve.wait_ge(s["rows_in"], j * 16 + 16)
                for c in range(PC):
                    x = x_res[:, c, :]
                    dve.wait_ge(s["h2_n"], j * PC + (c + 1))
                    dve.tensor_tensor(x, x, rows[:, c // 2, 1, :], ALU.mult).then_inc(s["h2_step"], 1)
                    dve.wait_ge(s["h2_step"], j * (2 * PC) + (2 * c + 1))
                    dve.tensor_tensor(h2_of(j)[:, c, :], x, rows[:, c // 2, 0, :], ALU.add).then_inc(s["h2_step"], 1)

            def gate_up_lo(first, end):
                for m in range(first, end):
                    e = slice(m, m + 1)
                    dve.wait_ge(s["gw_hi"], m + 1)
                    split(gu_lo[:, e, :, :], gu_raw[:, e, :, :], gu_hi[:, e, :, :]).then_inc(s["gw_lo"], 1)

            def prepare(j):
                KV_lo(j, 0)
                KV_elu(j, 1)
                KV_lo(j, 1)
                KV_bias(j, 2)
                KV_elu(j, 2)
                KV_lo(j, 2)
                state(j, 0)
                elu(j, 0)
                KV_bias(j, 3)
                KV_elu(j, 3)
                KV_lo(j, 3)
                fold(j, 0, 0)
                elu(j, 1)
                fold(j, 1, 0)
                state(j, 1)
                fold(j, 0, 1)
                fold(j, 1, 1)

            dve.memset(ones_f[:], 1.0).then_inc(s["ones_made"], 1)
            silu_c()
            ln1_moments(0)
            ln1_rows(0)
            columns()
            T_turned(0)
            for n in range(4):
                dve.wait_ge(s["wkv_hi"], n + 1)
                split(wkv_lo[:, n % 2, n // 2, :], wkv_raw[n], wkv_hi[:, n % 2, n // 2, :]).then_inc(s["wkv_lo"], 1)
            T_lo(0)
            gates_read()
            dve.wait_ge(s["bias_in"], 32)
            dve.tensor_scalar(bq1_sb[:], bq_sb[:], 1.0, None, ALU.add).then_inc(s["bq1"], 1)
            KV_bias(0, 0)
            KV_elu(0, 0)
            gates_made()
            KV_bias(0, 1)
            dve.wait_ge(s["bq1"], 1)
            prepare(0)
            dve.wait_ge(s["iota_in"], 16)
            dve.wait_ge(s["router_in"], 32)
            dve.tensor_copy(cum[:], iota_first[:, 1, :]).then_inc(s["cum_made"], 1)
            dve.wait_ge(s["tri_in"], 16)
            dve.tensor_copy(tri[:], acc[:, 0, :]).then_inc(s["tri_made"], 1)
            over_pairs(dve, pair)
            steps_done = [0]

            def then(ins):
                ins.then_inc(s["final_step"], 1)
                steps_done[0] += 1
                dve.wait_ge(s["final_step"], steps_done[0])

            iota_row, first_row = iota_first[:, 0, :], iota_first[:, 1, :]
            dve.wait_ge(s["cum_made"], PAIRS + 1)
            dve.tensor_copy(end_row[:], cum[0:1, :]).then_inc(s["ends_made"], 1)
            dve.wait_ge(s["cst_in"], 16)
            dve.wait_ge(s["h2_step"], 2 * CH)
            dve.wait_ge(s["x1_out"], 16 * PAIRS)
            dve.memset(zero[:], 0.0).then_inc(s["zero_made"], 1)
            dve.tensor_scalar(steps[:], iota_row, float(P), None, ALU.mult)
            then(dve.tensor_tensor(count[:], cum[:], first_row, ALU.subtract))
            then(dve.tensor_tensor(cmp[:], count[:].unsqueeze(2).broadcast_to([P, E, E]), steps[:].unsqueeze(1).broadcast_to([P, E, E]), ALU.is_gt))
            then(dve.tensor_reduce(ntile[:], cmp[:], AX_X, ALU.add))
            low = cst[:, C_LOW:C_LOW + E * E].rearrange("p (a b) -> p a b", b=E)
            dve.tensor_reduce(total[:], ntile[:], AX_X, ALU.add)
            then(dve.tensor_tensor(cmp[:], low, ntile[:].unsqueeze(1).broadcast_to([P, E, E]), ALU.mult))
            then(dve.tensor_reduce(start[:], cmp[:], AX_X, ALU.add))
            rows_in = in_row[:].rearrange("p c k -> p (c k)")
            each_choice = lambda t: t.unsqueeze(1).broadcast_to([P, CH * TOPK, E])
            then(dve.tensor_tensor(reached[:], rows_in.unsqueeze(2).broadcast_to([P, CH * TOPK, E]), each_choice(first_row), ALU.is_ge))
            then(dve.tensor_reduce(n_reached[:], reached[:], AX_X, ALU.add))
            then(dve.tensor_tensor(reached[:], reached[:], each_choice(start[:]), ALU.mult))
            then(dve.tensor_reduce(out_first[:], reached[:], AX_X, ALU.max))
            then(dve.scalar_tensor_tensor(out_row[:], out_first[:], float(P), rows_in, ALU.mult, ALU.add))
            then(dve.tensor_scalar(n_reached[:], n_reached[:], -1.0, float(-EXPERT_ROWS), ALU.add, ALU.mult))
            dve.tensor_tensor(slot_i[:].rearrange("p c k -> p (c k)"), out_row[:], n_reached[:], ALU.add).then_inc(s["outs_made"], 1)
            then(dve.tensor_scalar(tsum[:], cst[0:1, C_TILE:C_TILE + TILES], 1.0, None, ALU.add))
            then(dve.tensor_scalar(tile[:], tsum[:], total[0:1, 0:1], -1.0, ALU.min, ALU.add))
            at = lambda t: t.unsqueeze(2).broadcast_to([1, TILES, E])
            each = start[0:1, :].unsqueeze(1).broadcast_to([1, TILES, E])
            then(dve.tensor_tensor(tcmp[:], each, at(tile[:]), ALU.is_le))
            then(dve.tensor_reduce(tsum[:], tcmp[:], AX_X, ALU.add))
            then(dve.tensor_scalar(tsum[:], tsum[:], -1.0, None, ALU.add))
            then(dve.tensor_tensor(tcmp[:], tcmp[:], each, ALU.mult))
            then(dve.tensor_reduce(tstart[:], tcmp[:], AX_X, ALU.max))
            then(dve.tensor_tensor(trow[:], tile[:], tstart[:], ALU.subtract))
            then(dve.tensor_scalar(trow[:], trow[:], float(P), None, ALU.mult))
            then(dve.scalar_tensor_tensor(trow[:], tsum[:], float(EXPERT_ROWS), trow[:], ALU.mult, ALU.add))
            dve.tensor_copy(tile_row[:], trow[:]).then_inc(s["tiles_made"], 1)
            dve.tensor_copy(tile_e[:], tsum[:]).then_inc(s["tiles_made"], 1)
            dve.wait_ge(s["tiles_made"], 2)

            for i, (lo, raw, hi) in enumerate(((gu_lo, gu_raw, gu_hi), (dn_lo, dn_raw, dn_hi))):
                with dve.Fori(0 if i else LO_BETWEEN, E if i else LO_POOL) as m:
                    e = bass.ds(m, 1)
                    dve.wait_ge(s["gw_hi"], m + (E * i + 1))
                    split(lo[:, e, :, :], raw[:, e, :, :], hi[:, e, :, :]).then_inc(s["gw_lo"], 1)

            def x_lo(n, q):
                dve.wait_ge(s["xT_hi"], n + 1)
                split(xT_lo[:, q, :, :].rearrange("p k n -> p (k n)"), ps_d[:, q, 0:HID],
                      xT_hi[:, q, :, :].rearrange("p k n -> p (k n)")).then_inc(s["xT_lo"], 1)

            def step(t, par, what):
                par %= 2
                if "X" in what:
                    x_lo(t + 1, 1 - par)
                if "G" in what:
                    dve.wait_ge(s["silu_done"], t + 1)
                    if not (isinstance(t, int) and t < 2):
                        dve.wait_ge(s["m_turned"], t - 1)
                    dve.tensor_tensor(mid[:, par, :], silu[:, par, :], ps_q[:, par, FF:2 * FF], ALU.mult).then_inc(s["mid_done"], 1)
                if "A" in what:
                    n, q = t - 1, 1 - par
                    dve.wait_ge(s["mT_hi"], n + 1)
                    split(mT_lo[:, q, :, :].rearrange("p i n -> p (i n)"), ps_d[0:FH, 2 + q, 0:2 * P],
                          mT_hi[:, q, :, :].rearrange("p i n -> p (i n)")).then_inc(s["mT_lo"], 1)

            x_lo(0, 0)
            over_tiles(dve, step)

            dve.wait_ge(s["gb_in"], 16)
            for c in range(CH):
                r, o = c % RING, o_sb[:, c % RING, :]
                dve.wait_ge(s[f"gathered{r}"], 16 * TOPK * (c // RING + 1))
                if c >= RING:
                    dve.wait_ge(s[f"o_out{r}"], 16 * (c // RING))
                then(dve.tensor_scalar(o, yg[:, r, 0, :], wgt[:, c, 0:1], None, ALU.mult))
                for k in range(1, TOPK):
                    then(dve.scalar_tensor_tensor(o, yg[:, r, k, :], wgt[:, c, k:k + 1], o, ALU.mult, ALU.add))
                then(dve.tensor_tensor(o, o, gb_sb[:, c * P // S, :], ALU.mult))
                dve.wait_ge(s[f"x1_back{r}"], 16 * (c // RING + 1))
                dve.tensor_tensor(o, o, x1_sb[:, r, :], ALU.add).then_inc(s["o_made"], 1)

        @block.gpsimd
        def _(pool):
            def inverse_root(n, counter):
                pool.tensor_tensor(rstd[:, 0:n], ve[:, 0:n], half[:, 0:n], ALU.pow).then_inc(counter, 1)

            pool.memset(half[:], -0.5).then_inc(s["half_made"], 1)
            pool.wait_ge(s["half_made"], 1)
            pool.wait_ge(s["ln1_step"], 2 * PC + 1)
            inverse_root(PC, s["ln1_rstd"])

            def piece_lo(n):
                pool.wait_ge(s["wst_hi"], n + 1)
                pool.tensor_tensor(piece_of(n, wq_lo, wo_lo), wst[:, n % 2, :], piece_of(n, wq_hi, wo_hi).bitcast(F32), ALU.subtract
                                   ).then_inc(s["wst_lo"], 1)

            def key_sum(j, b):
                pool.wait_ge(s["sk_f"], j * PC + 2 * (b + 1))
                pool.tensor_tensor(key_sums[:, b, :], kt[:, 0, :], kt[:, 1, :], ALU.add).then_inc(s["ksum_in"], 1)

            def lo(j, h):
                pool.wait_ge(s["sq_hi"], j * H + (h + 1))
                pool.tensor_tensor(sq_lo[:, h % 2, :], qe[:, h % 2, :], sq_hi[:, h % 2, :].bitcast(F32), ALU.subtract).then_inc(s["sq_lo"], 1)

            def add3(j, h):
                pool.wait_ge(s["d3_scaled"], j * H + (h + 1))
                if h >= 2:
                    pool.wait_ge(s["acc3_done"], j * (H - 1) + (h - 1))
                pool.tensor_tensor(acc[:, 3, :], acc[:, 3, :], d3[:, h % 2, :], ALU.add).then_inc(s["acc3_done"], 1)

            def v_lo_of(j, c):
                pool.wait_ge(s["v_hi"], j * PC + (c + 1))
                pool.tensor_tensor(v_lo[:, c, :], vf[:, c % 2, :], v_hi[:, c, :].bitcast(F32), ALU.subtract).then_inc(s["v_lo"], 1)

            def x1(j, c):
                if c == 0:
                    pool.wait_ge(s["ga_in"], j * 16 + 16)
                    pool.wait_ge(s["acc_done"], j * (3 * H) + 3 * H)
                if c == 3:
                    pool.wait_ge(s["acc3_done"], j * (H - 1) + (H - 1))
                x = x_res[:, c, :]
                pool.tensor_tensor(acc[:, c, :], acc[:, c, :], ga_rows[:, c // 2, :], ALU.mult).then_inc(s["x1_step"], 1)
                if c == 0:
                    pool.wait_ge(s["x_res_in"], j * 16 + 16)
                pool.wait_ge(s["x1_step"], j * PC + (c + 1))
                pool.tensor_tensor(x, acc[:, c, :], x, ALU.add).then_inc(s["x1_made"], 1)

            def h2_made(j, c):
                if c == 0:
                    pool.wait_ge(s["rows_in"], j * 16 + 16)
                    if not is_last(j):
                        wait_from(pool, s["scattered"], j * (16 * PC * TOPK))
                x = x_res[:, c, :]
                pool.wait_ge(s["h2_n"], j * PC + (c + 1))
                pool.tensor_tensor(x, x, rows[:, c // 2, 1, :], ALU.mult).then_inc(s["h2_step"], 1)
                pool.wait_ge(s["h2_step"], j * (2 * PC) + (2 * c + 1))
                pool.tensor_tensor(h2_of(j)[:, c, :], x, rows[:, c // 2, 0, :], ALU.add).then_inc(s["h2_step"], 1)

            def ln2_rstd(j):
                pool.wait_ge(s["ln2_step"], j * (2 * PC + 1) + (2 * PC + 1))
                inverse_root(PC, s["ln2_rstd"])

            def pair(j, before, after):
                for h in range(H):
                    if h + 1 < H:
                        lo(j, h + 1)
                    if h >= 2:
                        add3(j, h - 1)
                    if not before and h < 8:
                        piece_lo(8 + h)
                    if before and h == 1:
                        ln2_rstd(j - 1)
                    if before and 3 <= h < 3 + PC:
                        h2_made(j - 1, h - 3)
                    if before and h in SENT_AT:
                        scatter(j - 1, *SENT_AT[h])
                    if after and h == 7:
                        pool.wait_ge(s["ln1_step"], j * (2 * PC + 1) + 2 * (2 * PC + 1))
                        inverse_root(PC, s["ln1_rstd"])
                    if after and h == H - 1:
                        v_lo_of(j + 1, 0)
                add3(j, H - 1)
                if after:
                    key_sum(j + 1, 0)
                    if before:
                        scatter(j - 1, 8, 2)
                    x1(j, 0)
                    v_lo_of(j + 1, 2)
                    if before:
                        scatter(j - 1, 10, 3)
                    x1(j, 1)
                    key_sum(j + 1, 1)
                    lo(j + 1, 0)
                    for c in (2, 3):
                        x1(j, c)
                    if before:
                        scatter(j - 1, 13, 3)
                else:
                    scatter(j - 1, 8, 2)
                    ln2_rstd(j)
                    scatter(j - 1, 10, 6)
                    scatter(j, 0, 16)
                    for e in range(LO_POOL, E):
                        pool.wait_ge(s["gw_hi"], e + 1)
                        pool.tensor_tensor(gu_lo[:, e, :, :], gu_raw[:, e, :, :], gu_hi[:, e, :, :].bitcast(F32), ALU.subtract
                                           ).then_inc(s["gw_lo"], 1)

            SENT_AT = {12: (0, 2), 13: (2, 2), 14: (4, 2), 15: (6, 2)}

            def scatter(j, first, n):
                wait_apart(pool, s["slots_made"], j + 1)
                for i in range(first, first + n):
                    c, k = i // TOPK, i % TOPK
                    pool.indirect_dma_start(xs_dram, bass.IndirectOffsetOnAxis(pair_slots[:, c, k:k + 1], 0), h2_of(j)[:, c, :], None
                                            ).then_inc(s["scattered"], 16)

            for n in range(8):
                piece_lo(n)
                if n == 1:
                    key_sum(0, 0)
                if n == 5:
                    key_sum(0, 1)
                    lo(0, 0)
            over_pairs(pool, pair)
            pool.wait_ge(s["outs_made"], 1)
            for par in range(2):
                pool.wait_ge(s[f"y_out{par}"], 8 * TILES)
            for c in range(CH):
                if c >= RING:
                    pool.wait_ge(s["o_made"], c - RING + 1)
                for k in range(TOPK):
                    pool.indirect_dma_start(yg[:, c % RING, k, :], None, ys_dram, bass.IndirectOffsetOnAxis(slot_i[:, c, k:k + 1], 0)
                                            ).then_inc(s[f"gathered{c % RING}"], 16)


def kernel(**inputs):
    import numpy as np
    import concourse.bacc as bacc
    from concourse.bass_utils import run_bass_kernel_spmd

    a = {n.removeprefix("L0_").removeprefix("attn_").removeprefix("ffn_"): np.asarray(v) for n, v in inputs.items()}
    laid = {
        "x_in": a["hidden_states"].reshape(TOK, HID),
        "wqT": a["Wq"].T,
        "wkvT": np.concatenate([a["Wk"].T, a["Wv"].T], axis=1),
        "woT": a["Wo"].T.reshape(H, D, HID).transpose(1, 0, 2).reshape(D, H * HID),
        "bqT": a["bq"].reshape(H, D).T,
        "bkv": np.concatenate([a["bk"], a["bv"]]),
        "routerT": a["router_w"].T,
        "ebias": a["expert_bias"],
        "w_gu": np.concatenate([a["gate_proj"], a["up_proj"]], axis=2),
        "w_down": a["down_proj"],
        "cT": a["c"].T,
        "wmod": a["wmod"],
        "consts": constants(),
    }
    nc = bacc.Bacc("TRN2", target_bir_lowering=False, num_devices=1)
    arrays, args = {}, []
    for name, v in laid.items():
        arrays[name] = np.ascontiguousarray(v)
        args.append(nc.dram_tensor(name, v.shape, mybir.dt.from_np(v.dtype), kind="ExternalInput").ap())
    args.append(nc.dram_tensor("out", (TOK, HID), F32, kind="ExternalOutput").ap())
    adaln_block(nc, *args)
    r = run_bass_kernel_spmd(nc, [arrays], core_ids=[0])
    return r.results[0]["out"].reshape(B, S, HID)
```
